# Optimizing a Trainium2 kernel written in Bass

```python
import numpy as np
import jax
import jax.numpy as jnp

def _softmax(x, axis=-1):
    return jax.nn.softmax(x, axis=axis)

def _gelu(x):
    return jax.nn.gelu(x, approximate=True)

def _silu(x):
    return jax.nn.silu(x)

def _sigmoid(x):
    return jax.nn.sigmoid(x)

def _layernorm(x, axis=-1, eps=1e-05):
    m = jnp.mean(x, axis=axis, keepdims=True)
    v = jnp.var(x, axis=axis, keepdims=True)
    return (x - m) / jnp.sqrt(v + eps)

def _scatter_add(tgt, idx, src, axis=0):
    return tgt.at[idx].add(src)

def _segment_sum(src, seg, n):
    return jax.ops.segment_sum(src, seg, n)
kernel_name = 'mk_recurrent_d2_jaxref_r8_16e1c4'

def setup_inputs(seed: int=0):
    np.random.seed(seed)
    _w = jnp.asarray

    def _L0_attn_setup():
        import jax, jax.numpy as jnp
        import numpy as np
        B, N, D, H = (2, 256, 128, 16)
        HD = D // H
        SCALING = (D / H) ** 0.5
        EPS = 1e-05
        key = jax.random.key(seed)
        k1, k2, k3 = jax.random.split(key, 3)
        return {'z': jax.random.normal(k1, (B, N, D), dtype=jnp.float32), 'ln_scale': jnp.ones((D,), dtype=jnp.float32), 'ln_bias': jnp.zeros((D,), dtype=jnp.float32), 'w_qkv': jax.random.normal(k2, (D, 3 * D), dtype=jnp.float32) * D ** (-0.5), 'w_proj': jax.random.normal(k3, (D, D), dtype=jnp.float32) * D ** (-0.5), 'b_proj': jnp.zeros((D,), dtype=jnp.float32)}
    _L0_attn_in = _L0_attn_setup()

    def _L0_ffn_setup():
        import jax, jax.numpy as jnp
        import numpy as np
        DIM = 128
        DEPTH = 2
        HEADS = 8
        DIM_HEAD = 64
        WINDOW = 64
        INNER = HEADS * DIM_HEAD
        HID = int(DIM * 4 * 2 / 3)
        B, N = (2, 1024)
        QK_SCALE = 8.0

        def shift_token(t):
            t1, t2 = jnp.split(t, 2, axis=-1)
            t2 = jnp.pad(t2, ((0, 0), (1, 0), (0, 0)))[:, :-1]
            return jnp.concatenate([t1, t2], axis=-1)

        def l2norm(t):
            return t / jnp.clip(jnp.linalg.norm(t, axis=-1, keepdims=True), 1e-12)

        def rotate_half(x):
            x1, x2 = jnp.split(x, 2, axis=-1)
            return jnp.concatenate([-x2, x1], axis=-1)

        def rotary_xpos(q, k):
            n = q.shape[-2]
            half_idx = jnp.arange(0, DIM_HEAD, 2, dtype=jnp.float32)
            inv_freq = 1.0 / 10000.0 ** (half_idx / DIM_HEAD)
            t = jnp.arange(n, dtype=jnp.float32)
            freqs = t[:, None] * inv_freq[None, :]
            freqs = jnp.concatenate([freqs, freqs], axis=-1)
            base = (half_idx + 0.4 * DIM_HEAD) / (1.4 * DIM_HEAD)
            power = (t - n // 2) / float(WINDOW // 2)
            scale = base[None, :] ** power[:, None]
            scale = jnp.concatenate([scale, scale], axis=-1)
            cos, sin = (jnp.cos(freqs), jnp.sin(freqs))
            q = q * cos * scale + rotate_half(q) * sin * scale
            k = k * cos / scale + rotate_half(k) * sin / scale
            return (q, k)

        def local_attention(q, k, v):
            b, h, n, d = q.shape
            w = n // WINDOW
            bq = q.reshape(b, h, w, WINDOW, d) * QK_SCALE
            bk = k.reshape(b, h, w, WINDOW, d)
            bv = v.reshape(b, h, w, WINDOW, d)

            def look_around(t):
                p = jnp.pad(t, ((0, 0), (0, 0), (1, 0), (0, 0), (0, 0)))
                return jnp.concatenate([p[:, :, :w], p[:, :, 1:]], axis=3)
            bk, bv = (look_around(bk), look_around(bv))
            bt = jnp.arange(n).reshape(w, WINDOW)
            btp = jnp.pad(bt, ((1, 0), (0, 0)), constant_values=-1)
            btk = jnp.concatenate([btp[:w], btp[1:]], axis=1)
            sim = jnp.einsum('bhwid,bhwjd->bhwij', bq, bk)
            i = bt[:, :, None]
            j = btk[:, None, :]
            mask = (i < j) | (i > j + WINDOW) | (j == -1)
            sim = jnp.where(mask, -jnp.finfo(sim.dtype).max, sim)
            attn = jax.nn.softmax(sim, axis=-1)
            out = jnp.einsum('bhwij,bhwjd->bhwid', attn, bv)
            return out.reshape(b, h, n, d)

        def _layer(x, wqkv, qs, ksc, wo, lg, lb, w1, b1, w2, b2):
            b, n, _ = x.shape
            h = shift_token(x)
            qkv = h @ wqkv
            q, k, v = jnp.split(qkv, 3, axis=-1)
            to_heads = lambda t: t.reshape(b, n, HEADS, DIM_HEAD).transpose(0, 2, 1, 3)
            q, k, v = (to_heads(q), to_heads(k), to_heads(v))
            q = l2norm(q) * qs
            k = l2norm(k) * ksc
            q, k = rotary_xpos(q, k)
            o = local_attention(q, k, v)
            o = o.transpose(0, 2, 1, 3).reshape(b, n, INNER)
            x = x + o @ wo
            h = shift_token(x)
            mu = h.mean(-1, keepdims=True)
            var = h.var(-1, keepdims=True)
            h = (h - mu) / jnp.sqrt(var + 1e-05) * lg + lb
            h = h @ w1 + b1
            a, g = jnp.split(h, 2, axis=-1)
            h = a * jax.nn.gelu(g, approximate=False)
            x = x + h @ w2 + b2
            return x
        key = jax.random.key(seed)
        ks = jax.random.split(key, 6)
        return {'x': jax.random.normal(ks[0], (B, N, DIM), jnp.float32), 'wqkv': jax.random.normal(ks[1], (DEPTH, DIM, 3 * INNER), jnp.float32) * 0.02, 'q_scale': jnp.ones((DEPTH, DIM_HEAD), jnp.float32), 'k_scale': jnp.ones((DEPTH, DIM_HEAD), jnp.float32), 'wo': jax.random.normal(ks[2], (DEPTH, INNER, DIM), jnp.float32) * 0.02, 'ln_g': jnp.ones((DEPTH, DIM), jnp.float32), 'ln_b': jnp.zeros((DEPTH, DIM), jnp.float32), 'w1': jax.random.normal(ks[3], (DEPTH, DIM, 2 * HID), jnp.float32) * 0.02, 'b1': jnp.zeros((DEPTH, 2 * HID), jnp.float32), 'w2': jax.random.normal(ks[4], (DEPTH, HID, DIM), jnp.float32) * 0.02, 'b2': jnp.zeros((DEPTH, DIM), jnp.float32)}
    _L0_ffn_in = _L0_ffn_setup()

    def _L1_attn_setup():
        import jax, jax.numpy as jnp
        import numpy as np
        B, T, D_IN, D_OUT, NH = (4, 256, 128, 128, 16)
        HD = D_OUT // NH
        SCALE = 1.0 / float(np.sqrt(HD))
        key = jax.random.key(seed)
        k1, k2, k3 = jax.random.split(key, 3)
        x = jax.random.normal(k1, (B, T, D_IN), dtype=jnp.float32)
        w_qkv = jax.random.normal(k2, (3 * D_OUT, D_IN), dtype=jnp.float32) / np.sqrt(D_IN)
        w_out = jax.random.normal(k3, (D_OUT, D_OUT), dtype=jnp.float32) / np.sqrt(D_OUT)
        return {'x': x, 'w_qkv': w_qkv, 'w_out': w_out}
    _L1_attn_in = _L1_attn_setup()

    def _L1_ffn_setup():
        import jax, jax.numpy as jnp
        import numpy as np
        E = 8
        K = 2
        key = jax.random.key(seed)
        ks = jax.random.split(key, 8)
        B, T, d = (4, 256, 128)
        h = 4 * d // E
        s = 0.02
        X = jax.random.normal(ks[0], (B, T, d), jnp.float32)
        routing_W = jax.random.normal(ks[1], (E, d), jnp.float32) * s
        expert_bias = jnp.zeros((E,), jnp.float32)
        sW1 = jax.random.normal(ks[2], (d, h), jnp.float32) * s
        sb1 = jnp.zeros((h,), jnp.float32)
        sW2 = jax.random.normal(ks[3], (h, d), jnp.float32) * s
        sb2 = jnp.zeros((d,), jnp.float32)
        rW1 = jax.random.normal(ks[4], (E, d, h), jnp.float32) * s
        rb1 = jnp.zeros((E, h), jnp.float32)
        rW2 = jax.random.normal(ks[5], (E, h, d), jnp.float32) * s
        rb2 = jnp.zeros((E, d), jnp.float32)
        return dict(X=X, routing_W=routing_W, expert_bias=expert_bias, sW1=sW1, sb1=sb1, sW2=sW2, sb2=sb2, rW1=rW1, rb1=rb1, rW2=rW2, rb2=rb2)
    _L1_ffn_in = _L1_ffn_setup()
    _d = {'L0_attn_z': _L0_attn_in['z'], 'L0_attn_ln_scale': _L0_attn_in['ln_scale'], 'L0_attn_ln_bias': _L0_attn_in['ln_bias'], 'L0_attn_w_qkv': _L0_attn_in['w_qkv'], 'L0_attn_w_proj': _L0_attn_in['w_proj'], 'L0_attn_b_proj': _L0_attn_in['b_proj'], 'L0_ffn_wqkv': _L0_ffn_in['wqkv'], 'L0_ffn_q_scale': _L0_ffn_in['q_scale'], 'L0_ffn_k_scale': _L0_ffn_in['k_scale'], 'L0_ffn_wo': _L0_ffn_in['wo'], 'L0_ffn_ln_g': _L0_ffn_in['ln_g'], 'L0_ffn_ln_b': _L0_ffn_in['ln_b'], 'L0_ffn_w1': _L0_ffn_in['w1'], 'L0_ffn_b1': _L0_ffn_in['b1'], 'L0_ffn_w2': _L0_ffn_in['w2'], 'L0_ffn_b2': _L0_ffn_in['b2'], 'L1_attn_w_qkv': _L1_attn_in['w_qkv'], 'L1_attn_w_out': _L1_attn_in['w_out'], 'L1_ffn_routing_W': _L1_ffn_in['routing_W'], 'L1_ffn_expert_bias': _L1_ffn_in['expert_bias'], 'L1_ffn_sW1': _L1_ffn_in['sW1'], 'L1_ffn_sb1': _L1_ffn_in['sb1'], 'L1_ffn_sW2': _L1_ffn_in['sW2'], 'L1_ffn_sb2': _L1_ffn_in['sb2'], 'L1_ffn_rW1': _L1_ffn_in['rW1'], 'L1_ffn_rb1': _L1_ffn_in['rb1'], 'L1_ffn_rW2': _L1_ffn_in['rW2'], 'L1_ffn_rb2': _L1_ffn_in['rb2']}
    _x0 = _d['L0_attn_z']
    _d['L0_attn_z'] = jax.random.normal(jax.random.fold_in(jax.random.key(seed), 1), (1, 2048, 128), dtype=_x0.dtype)
    del _x0
    return _d

def reference(L0_attn_z, L0_attn_ln_scale, L0_attn_ln_bias, L0_attn_w_qkv, L0_attn_w_proj, L0_attn_b_proj, L0_ffn_wqkv, L0_ffn_q_scale, L0_ffn_k_scale, L0_ffn_wo, L0_ffn_ln_g, L0_ffn_ln_b, L0_ffn_w1, L0_ffn_b1, L0_ffn_w2, L0_ffn_b2, L1_attn_w_qkv, L1_attn_w_out, L1_ffn_routing_W, L1_ffn_expert_bias, L1_ffn_sW1, L1_ffn_sb1, L1_ffn_sW2, L1_ffn_sb2, L1_ffn_rW1, L1_ffn_rb1, L1_ffn_rW2, L1_ffn_rb2):

    def _L0_attn_ref(z, ln_scale, ln_bias, w_qkv, w_proj, b_proj):
        import jax, jax.numpy as jnp
        import numpy as np
        B, N, D, H = (2, 256, 128, 16)
        HD = D // H
        SCALING = (D / H) ** 0.5
        EPS = 1e-05
        b, n, d = z.shape
        mu = jnp.mean(z, axis=-1, keepdims=True)
        var = jnp.mean(jnp.square(z - mu), axis=-1, keepdims=True)
        zn = (z - mu) / jnp.sqrt(var + EPS) * ln_scale + ln_bias
        qkv = zn @ w_qkv
        qkv5 = qkv.reshape(b, n, H, HD, 3)
        q = jnp.transpose(qkv5[..., 0], (0, 2, 1, 3))
        k = jnp.transpose(qkv5[..., 1], (0, 2, 1, 3))
        v = jnp.transpose(qkv5[..., 2], (0, 2, 1, 3))
        scores = jnp.einsum('bhqd,bhkd->bhqk', q, k) / SCALING
        att = jax.nn.softmax(scores, axis=-1)
        out = jnp.einsum('bhal,bhlv->bhav', att, v)
        out = jnp.transpose(out, (0, 2, 1, 3)).reshape(b, n, d)
        out = out @ w_proj + b_proj
        return z + out

    def _L0_ffn_ref(x, wqkv, q_scale, k_scale, wo, ln_g, ln_b, w1, b1, w2, b2):
        import jax, jax.numpy as jnp
        import numpy as np
        DIM = 128
        DEPTH = 2
        HEADS = 8
        DIM_HEAD = 64
        WINDOW = 64
        INNER = HEADS * DIM_HEAD
        HID = int(DIM * 4 * 2 / 3)
        B, N = (2, 1024)
        QK_SCALE = 8.0

        def shift_token(t):
            t1, t2 = jnp.split(t, 2, axis=-1)
            t2 = jnp.pad(t2, ((0, 0), (1, 0), (0, 0)))[:, :-1]
            return jnp.concatenate([t1, t2], axis=-1)

        def l2norm(t):
            return t / jnp.clip(jnp.linalg.norm(t, axis=-1, keepdims=True), 1e-12)

        def rotate_half(x):
            x1, x2 = jnp.split(x, 2, axis=-1)
            return jnp.concatenate([-x2, x1], axis=-1)

        def rotary_xpos(q, k):
            n = q.shape[-2]
            half_idx = jnp.arange(0, DIM_HEAD, 2, dtype=jnp.float32)
            inv_freq = 1.0 / 10000.0 ** (half_idx / DIM_HEAD)
            t = jnp.arange(n, dtype=jnp.float32)
            freqs = t[:, None] * inv_freq[None, :]
            freqs = jnp.concatenate([freqs, freqs], axis=-1)
            base = (half_idx + 0.4 * DIM_HEAD) / (1.4 * DIM_HEAD)
            power = (t - n // 2) / float(WINDOW // 2)
            scale = base[None, :] ** power[:, None]
            scale = jnp.concatenate([scale, scale], axis=-1)
            cos, sin = (jnp.cos(freqs), jnp.sin(freqs))
            q = q * cos * scale + rotate_half(q) * sin * scale
            k = k * cos / scale + rotate_half(k) * sin / scale
            return (q, k)

        def local_attention(q, k, v):
            b, h, n, d = q.shape
            w = n // WINDOW
            bq = q.reshape(b, h, w, WINDOW, d) * QK_SCALE
            bk = k.reshape(b, h, w, WINDOW, d)
            bv = v.reshape(b, h, w, WINDOW, d)

            def look_around(t):
                p = jnp.pad(t, ((0, 0), (0, 0), (1, 0), (0, 0), (0, 0)))
                return jnp.concatenate([p[:, :, :w], p[:, :, 1:]], axis=3)
            bk, bv = (look_around(bk), look_around(bv))
            bt = jnp.arange(n).reshape(w, WINDOW)
            btp = jnp.pad(bt, ((1, 0), (0, 0)), constant_values=-1)
            btk = jnp.concatenate([btp[:w], btp[1:]], axis=1)
            sim = jnp.einsum('bhwid,bhwjd->bhwij', bq, bk)
            i = bt[:, :, None]
            j = btk[:, None, :]
            mask = (i < j) | (i > j + WINDOW) | (j == -1)
            sim = jnp.where(mask, -jnp.finfo(sim.dtype).max, sim)
            attn = jax.nn.softmax(sim, axis=-1)
            out = jnp.einsum('bhwij,bhwjd->bhwid', attn, bv)
            return out.reshape(b, h, n, d)

        def _layer(x, wqkv, qs, ksc, wo, lg, lb, w1, b1, w2, b2):
            b, n, _ = x.shape
            h = shift_token(x)
            qkv = h @ wqkv
            q, k, v = jnp.split(qkv, 3, axis=-1)
            to_heads = lambda t: t.reshape(b, n, HEADS, DIM_HEAD).transpose(0, 2, 1, 3)
            q, k, v = (to_heads(q), to_heads(k), to_heads(v))
            q = l2norm(q) * qs
            k = l2norm(k) * ksc
            q, k = rotary_xpos(q, k)
            o = local_attention(q, k, v)
            o = o.transpose(0, 2, 1, 3).reshape(b, n, INNER)
            x = x + o @ wo
            h = shift_token(x)
            mu = h.mean(-1, keepdims=True)
            var = h.var(-1, keepdims=True)
            h = (h - mu) / jnp.sqrt(var + 1e-05) * lg + lb
            h = h @ w1 + b1
            a, g = jnp.split(h, 2, axis=-1)
            h = a * jax.nn.gelu(g, approximate=False)
            x = x + h @ w2 + b2
            return x
        for l in range(DEPTH):
            x = _layer(x, wqkv[l], q_scale[l], k_scale[l], wo[l], ln_g[l], ln_b[l], w1[l], b1[l], w2[l], b2[l])
        return x

    def _L1_attn_ref(x, w_qkv, w_out):
        import jax, jax.numpy as jnp
        import numpy as np
        B, T, D_IN, D_OUT, NH = (4, 256, 128, 128, 16)
        HD = D_OUT // NH
        SCALE = 1.0 / float(np.sqrt(HD))
        b, t, _ = x.shape
        qkv = jnp.einsum('btd,ed->bte', x, w_qkv)
        qkv = qkv.reshape(b, t, 3, NH, HD)
        q, k, v = jnp.moveaxis(qkv, 2, 0)
        scores = jnp.einsum('bqhd,bkhd->bhqk', q, k) * SCALE
        causal_bias = (1.0 - jnp.tril(jnp.ones((t, t), dtype=x.dtype))) * -10000.0
        scores = scores + causal_bias
        attn = jax.nn.softmax(scores, axis=-1)
        out = jnp.einsum('bhqk,bkhd->bqhd', attn, v)
        out = out.reshape(b, t, D_OUT)
        return jnp.einsum('btd,ed->bte', out, w_out)

    def _L1_ffn_ref(X, routing_W, expert_bias, sW1, sb1, sW2, sb2, rW1, rb1, rW2, rb2):
        import jax, jax.numpy as jnp
        import numpy as np
        E = 8
        K = 2
        B, T, d = X.shape
        shared = jax.nn.silu(X @ sW1 + sb1) @ sW2 + sb2
        logits = jnp.einsum('btd,ed->bte', X, routing_W) + expert_bias
        activation = jnp.sqrt(jax.nn.softplus(logits))
        top_vals, top_idx = jax.lax.top_k(activation, K)
        combine = jnp.sum(jax.nn.one_hot(top_idx, E, dtype=X.dtype) * top_vals[..., None], axis=-2)
        Xf = X.reshape(-1, d)
        cf = combine.reshape(-1, E)
        hdn = jax.nn.silu(jnp.einsum('nd,edh->enh', Xf, rW1) + rb1[:, None, :])
        y = jnp.einsum('enh,ehd->end', hdn, rW2) + rb2[:, None, :]
        routed = jnp.einsum('ne,end->nd', cf, y).reshape(B, T, d)
        return shared + routed
    x = L0_attn_z
    xn = _layernorm(x, axis=-1)
    s = _L0_attn_ref(xn, L0_attn_ln_scale, L0_attn_ln_bias, L0_attn_w_qkv, L0_attn_w_proj, L0_attn_b_proj)
    g = _silu(_L0_ffn_ref(xn, L0_ffn_wqkv, L0_ffn_q_scale, L0_ffn_k_scale, L0_ffn_wo, L0_ffn_ln_g, L0_ffn_ln_b, L0_ffn_w1, L0_ffn_b1, L0_ffn_w2, L0_ffn_b2))
    x = x + s * g
    xn = _layernorm(x, axis=-1)
    s = _L1_attn_ref(xn, L1_attn_w_qkv, L1_attn_w_out)
    g = _silu(_L1_ffn_ref(xn, L1_ffn_routing_W, L1_ffn_expert_bias, L1_ffn_sW1, L1_ffn_sb1, L1_ffn_sW2, L1_ffn_sb2, L1_ffn_rW1, L1_ffn_rb1, L1_ffn_rW2, L1_ffn_rb2))
    x = x + s * g
    return x

_drawn_inputs = setup_inputs


def setup_inputs(seed=0):
    import zlib

    import numpy as np

    out = dict(_drawn_inputs(seed))
    spreads = {'L0_attn_ln_scale': (1.0, 0.6),
     'L0_attn_ln_bias': (0.0, 0.1),
     'L0_attn_b_proj': (0.0, 0.1),
     'L0_ffn_q_scale': (1.0, 0.6),
     'L0_ffn_k_scale': (1.0, 0.6),
     'L0_ffn_ln_g': (1.0, 0.6),
     'L0_ffn_ln_b': (0.0, 0.8),
     'L0_ffn_b1': (0.0, 0.8),
     'L0_ffn_b2': (0.0, 0.1),
     'L1_ffn_expert_bias': (0.0, 0.8),
     'L1_ffn_sb1': (0.0, 0.8),
     'L1_ffn_sb2': (0.0, 0.8),
     'L1_ffn_rb1': (0.0, 0.8),
     'L1_ffn_rb2': (0.0, 0.623)}
    factors = {'L0_ffn_wqkv': 5.112,
     'L0_ffn_wo': 5.065,
     'L0_ffn_w1': 7.651,
     'L0_ffn_w2': 7.471,
     'L1_attn_w_qkv': 4.542,
     'L1_attn_w_out': 3.503,
     'L1_ffn_routing_W': 5.235,
     'L1_ffn_sW1': 8.0,
     'L1_ffn_sW2': 8.0,
     'L1_ffn_rW1': 8.0,
     'L1_ffn_rW2': 8.0}
    for name, (base, spread) in spreads.items():
        noise = np.random.default_rng([zlib.crc32(name.encode()), seed]).standard_normal(out[name].shape)
        drawn = base * np.exp(spread * noise) if base else spread * noise
        out[name] = jnp.asarray(drawn.astype(out[name].dtype))
    for name, factor in factors.items():
        out[name] = (out[name] * factor).astype(out[name].dtype)
    return out
```

```python
from contextlib import ExitStack, contextmanager

import concourse.bass as bass
import numpy as np
from concourse import mybir

F32 = mybir.dt.float32
BF16 = mybir.dt.bfloat16
ALU = mybir.AluOpType
ACT = mybir.ActivationFunctionType
AX = mybir.AxisListType

P = 128
T = 2048
D = 128
NT = T // P
CH = 512
NC = T // CH
TPC = CH // P
EPS = 1e-5
NEG = -30000.0

H = 16
HD = D // H
PARTS = 3
ROWS = PARTS * PARTS * HD
MROW = 96
KROWS = MROW + PARTS
VW = 32
SCALE = 1.0 / float(np.sqrt(HD))


class Memory:
    pass


def tiles_of(ap):
    return ap.rearrange("(i p) d -> p i d", p=P)


@contextmanager
def stage(nc, name):
    with ExitStack() as ctx:
        used = []

        def sem(n):
            used.append(nc.alloc_semaphore(f"{name}_{n}"))
            return used[-1]

        def give_back():
            nc.clear_and_free_semaphores(used)
            nc.all_engine_barrier()

        ctx.callback(give_back)
        yield ctx, sem


def attention_units(causal):
    units = []
    for kb in range(NT):
        for c in range(kb // TPC if causal else 0, NC):
            first = max(0, kb * P - c * CH) if causal else 0
            units.append((kb, c, first))
    return units


def max_tiles(causal):
    tiles = []
    for i in range(NT):
        keys = (i + 1) * P if causal else T
        for half in range(2):
            n = min(2 * CH, keys - half * 2 * CH)
            if n > 0:
                tiles.append((i, half, half * 2 * CH, n))
    return tiles


def attention(nc, mem, name, causal):
    units = attention_units(causal)
    mtiles = max_tiles(causal)
    NU, NM = len(units), len(mtiles)
    assert NM % 2 == 0
    group_of = [[u for u, x in enumerate(units) if x[0] == kb] for kb in range(NT)]
    LEAD = 0.84

    with stage(nc, name) as (ctx, sem):
        def sb(n, shape, dt):
            return ctx.enter_context(nc.sbuf_tensor(f"{name}_{n}", shape, dt))


        QS, KS = mem.QS, mem.KS
        v_head = sb("v_head", [P, NT, VW], F32)
        probs = sb("probs", [P, 2, NC, CH], F32)
        part_max = sb("part_max", [P, NT, 2], F32)
        neg_max = sb("neg_max", [P, NT], F32)
        m_rest = sb("m_rest", [NT, P], F32)
        m_parts = sb("m_parts", [NT, PARTS, P], BF16)

        ps_max = [ctx.enter_context(nc.psum_tensor(f"{name}_ps_max{s}", [P, 2 * CH], F32)) for s in range(2)]
        ps_exp = [ctx.enter_context(nc.psum_tensor(f"{name}_ps_exp{s}", [P, CH], F32)) for s in range(3)]
        ps_out = ctx.enter_context(nc.psum_tensor(f"{name}_ps_out", [P, CH], F32))

        filled_first = sem("filled_first")
        filled_rest = sem("filled_rest")
        loads = [sem(f"loads{s}") for s in range(2)]
        heads_loaded = sem("heads_loaded")
        v_cleared = sem("v_cleared")
        v_staged = sem("v_staged")
        max_cleared = sem("max_cleared")
        max_scores = sem("max_scores")
        max_taken = sem("max_taken")
        max_folded = sem("max_folded")
        split = sem("split")
        m_ready = sem("m_ready")
        m_loaded = sem("m_loaded")
        exp_scores = sem("exp_scores")
        probs_ready = sem("probs_ready")
        pv_done = sem("pv_done")
        out_taken = sem("out_taken")

        block = ctx.enter_context(nc.Block())

        @block.sync
        def _(sp):
            def load_rows(h, s):
                for g in range(PARTS):
                    for j in range(PARTS):
                        r = (g * PARTS + j) * HD
                        for stack, parts, n in ((QS, mem.q_parts_dram, g), (KS, mem.k_parts_dram, j)):
                            sp.dma_start(stack[r:r + HD, bass.ds(h * T, T)],
                                         parts[n, bass.ds(h * HD, HD), :]).then_inc(loads[s], 16)

            n_dma = 2 * PARTS * PARTS * 16
            def fill_rows(h, heads, filled):
                for stack, r0, r1, n in ((QS, ROWS, MROW, 0), (KS, ROWS, MROW, 0), (KS, MROW, KROWS, 1)):
                    sp.dma_start(stack[r0:r1, h * T:(h + heads) * T].rearrange("p (h t) -> p h t", t=T),
                                 mem.fill[n, 0:r1 - r0, :].unsqueeze(1).broadcast_to([r1 - r0, heads, T])
                                 ).then_inc(filled, 16)

            load_rows(0, 0)
            fill_rows(0, 1, filled_first)
            load_rows(1, 1)
            fill_rows(1, H - 1, filled_rest)
            with sp.Fori(0, H // 2 - 1) as i:
                for s in range(2):
                    sp.wait_ge(loads[s], i * n_dma + n_dma)
                    sp.sem_inc(heads_loaded, 1)
                    load_rows(i * 2 + (s + 2), s)
            for s in range(2):
                sp.wait_ge(loads[s], n_dma * (H // 2))
                sp.sem_inc(heads_loaded, 1)

        @block.gpsimd
        def _(pool):
            nc.gpsimd.memset(v_head[:], 0.0).then_inc(v_cleared, 1)
            pool.wait_ge(v_cleared, 1)
            nc.gpsimd.memset(v_head[:, :, HD:HD + 1], 1.0).then_inc(v_cleared, 1)
            pool.wait_ge(v_cleared, 2)

            def stage(h):
                nc.gpsimd.tensor_copy(v_head[:, :, 0:HD],
                                      mem.v_tok[:, :, bass.ds(h * HD, HD)]).then_inc(v_staged, 1)
            stage(0)

            def load_max(h):
                pool.wait_ge(m_ready, h + 1)
                for g in range(PARTS):
                    pool.dma_start(
                        QS[MROW + g:MROW + g + 1, bass.ds(h * T, T)].rearrange("o (i p) -> o i p", p=P),
                        m_parts[:, g, :]).then_inc(m_loaded, 16)
            load_max(0)
            with pool.Fori(1, H) as h:
                load_max(h)
                pool.wait_ge(pv_done, h * NT)
                stage(h)

        @block.tensor
        def _(pe):
            def max_tile(h, k):
                i, half, key0, n = mtiles[k]
                if k == 0:
                    if not (isinstance(h, int) and h == 0):
                        pe.wait_ge(m_ready, h)
                    pe.wait_ge(heads_loaded, h + 1)
                    if isinstance(h, int) and h < 2:
                        pe.wait_ge(filled_rest if h else filled_first, 48)
                elif k >= 2:
                    pe.wait_ge(max_taken, h * NM + (k - 1))
                out = ps_max[k % 2]
                last = causal and key0 + n == (i + 1) * P
                for a in range(0, n, CH):
                    m = min(CH, n - a)
                    masked = last and a + m == n
                    mm = nc.tensor.matmul(out[:, a:a + m],
                                          QS[0:MROW, bass.ds(h * T + i * P, P)],
                                          KS[0:MROW, bass.ds(h * T + (key0 + a), m)],
                                          start=True, stop=not masked)
                    if masked:
                        mm = nc.tensor.matmul(out[:, n - P:n], mem.ident_bf[:, :], mem.hide_later_keys[:, :],
                                              start=False, stop=True)
                mm.then_inc(max_scores, 1)

            def transpose_max(h):
                pe.wait_ge(max_folded, h + 1)
                nc.tensor.transpose(ps_max[0][0:NT, 0:P], neg_max[:, :], mem.ident[:, :]).then_inc(max_scores, 1)

            def exp_unit(h, u):
                kb, c, first = units[u]
                if u >= 3:
                    pe.wait_ge(probs_ready, h * NU + (u - 2))
                out = ps_exp[u % 3]
                masked = causal and c == kb // TPC
                mm = nc.tensor.matmul(out[:, 0:CH - first],
                                      KS[0:KROWS, bass.ds(h * T + kb * P, P)],
                                      QS[0:KROWS, bass.ds(h * T + (c * CH + first), CH - first)],
                                      start=True, stop=not masked)
                if masked:
                    mm = nc.tensor.matmul(out[:, 0:P], mem.ident_bf[:, :], mem.hide_earlier_queries[:, :],
                                          start=False, stop=True)
                mm.then_inc(exp_scores, 1)

            def pv(h, kb):
                pe.wait_ge(probs_ready, h * NU + (group_of[kb][-1] + 1))
                if kb == 0:
                    pe.wait_ge(v_staged, h + 1)
                    if not (isinstance(h, int) and h == 0):
                        pe.wait_ge(out_taken, h)
                for u in group_of[kb]:
                    _, c, first = units[u]
                    last = (kb == (c + 1) * TPC - 1) if causal else kb == NT - 1
                    mm = nc.tensor.matmul(ps_out[32 * c:32 * c + VW, first:CH], v_head[:, kb, :],
                                          probs[:, kb % 2, c, first:CH], start=(kb == 0), stop=last,
                                          skip_group_check=True)
                mm.then_inc(pv_done, 1)

            def head(h, next_max):
                pe.wait_ge(m_loaded, h * (16 * PARTS) + 16 * PARTS)
                tiles_done = 0
                for u in range(NU):
                    exp_unit(h, u)
                    kb = units[u][0]
                    if next_max:
                        want = min(NM, int(round(NM * (u + 1) / (LEAD * NU))))
                        while tiles_done < want:
                            max_tile(h + 1, tiles_done)
                            tiles_done += 1
                    if kb >= 1 and u == group_of[kb][min(1, len(group_of[kb]) - 1)]:
                        pv(h, kb - 1)
                if next_max:
                    transpose_max(h + 1)
                pv(h, NT - 1)

            for k in range(NM):
                max_tile(0, k)
            transpose_max(0)
            head(0, True)
            with pe.Fori(1, H - 1) as h:
                head(h, True)
            head(H - 1, False)

        @block.scalar
        def _(act):
            def head(h):
                for u, (kb, c, first) in enumerate(units):
                    if u == group_of[kb][0]:
                        if kb >= 2:
                            act.wait_ge(pv_done, h * NT + (kb - 1))
                        elif kb == 0 and not (isinstance(h, int) and h == 0):
                            act.wait_ge(pv_done, h * NT)
                    act.wait_ge(exp_scores, h * NU + (u + 1))
                    nc.scalar.activation(probs[:, kb % 2, c, first:CH], ps_exp[u % 3][:, 0:CH - first],
                                         ACT.Exp, scale=SCALE).then_inc(probs_ready, 1)
            head(0)
            with act.Fori(1, H) as h:
                head(h)

        @block.vector
        def _(dve):
            def maxima(h):
                for k, (i, half, _, n) in enumerate(mtiles):
                    dve.wait_ge(max_scores, h * (NM + 1) + (k + 1))
                    nc.vector.tensor_reduce(part_max[:, i, half:half + 1], ps_max[k % 2][:, 0:n], AX.X,
                                            ALU.max).then_inc(max_taken, 1)
                dve.wait_ge(max_taken, (h + 1) * NM)
                nc.vector.tensor_reduce(neg_max[:, :], part_max[:, :, :], AX.X, ALU.max,
                                        negate=True).then_inc(max_folded, 1)
                dve.wait_ge(max_scores, (h + 1) * (NM + 1))
                turned = ps_max[0][0:NT, 0:P]
                if not (isinstance(h, int) and h == 0):
                    dve.wait_ge(m_loaded, h * (16 * PARTS))
                nc.vector.tensor_copy(m_parts[:, 0, :], turned).then_inc(split, 1)
                dve.wait_ge(split, h * 3 + 1)
                nc.vector.tensor_tensor(m_rest[:, :], turned, m_parts[:, 0, :], ALU.subtract).then_inc(split, 1)
                dve.wait_ge(split, h * 3 + 2)
                nc.vector.tensor_copy(m_parts[:, 1, :], m_rest[:, :]).then_inc(split, 1)
                dve.wait_ge(split, h * 3 + 3)
                nc.vector.tensor_tensor(m_parts[:, 2, :], m_rest[:, :], m_parts[:, 1, :],
                                        ALU.subtract).then_inc(m_ready, 1)

            def save(h):
                dve.wait_ge(pv_done, (h + 1) * NT)
                nc.vector.tensor_copy(mem.heads_out[:, bass.ds(h * CH, CH)], ps_out[:, :]).then_inc(out_taken, 1)

            nc.vector.memset(part_max[:], -3.0e38).then_inc(max_cleared, 1)
            dve.wait_ge(max_cleared, 1)
            maxima(0)
            with dve.Fori(0, H - 1) as h:
                maxima(h + 1)
                save(h)
            save(H - 1)


def normalise(nc, mem, name, steps):
    with stage(nc, name) as (ctx, sem):

        summed = sem("summed")
        moments_ready = sem("moments_ready")
        widened = sem("widened")
        rstd_ready = sem("rstd_ready")
        scaled = sem("scaled")
        half_set = sem("half_set")
        block = ctx.enter_context(nc.Block())

        @block.vector
        def _(dve):
            for n, (src, dst) in enumerate(steps):
                if n:
                    dve.wait_ge(scaled, n * NT)
                for i in range(NT):
                    nc.vector.bn_stats(mem.sums[:, i, :], src[:, i, :]).then_inc(summed, 1)
                dve.wait_ge(summed, (n + 1) * NT)
                for i in range(NT):
                    nc.vector.bn_aggr(mem.moments[:, i, :], mem.sums[:, i, :]).then_inc(moments_ready, 1)
                dve.wait_ge(rstd_ready, n + 1)
                for i in range(NT):
                    nc.vector.tensor_scalar(dst[:, i, :], src[:, i, :], mem.moments[:, i, 0:1],
                                            mem.rstd[:, i:i + 1], ALU.subtract, ALU.mult).then_inc(scaled, 1)

        @block.gpsimd
        def _(pool):
            nc.gpsimd.memset(mem.minus_half[:], -0.5).then_inc(half_set, 1)
            pool.wait_ge(half_set, 1)
            for n in range(len(steps)):
                pool.wait_ge(moments_ready, (n + 1) * NT)
                if n:
                    pool.wait_ge(scaled, n * NT)
                nc.gpsimd.tensor_scalar(mem.rstd[:, :], mem.moments[:, :, 1], 1.0, EPS, ALU.mult,
                                        ALU.add).then_inc(widened, 1)
                pool.wait_ge(widened, n + 1)
                nc.gpsimd.tensor_tensor(mem.rstd[:, :], mem.rstd[:, :], mem.minus_half[:, :],
                                        ALU.pow).then_inc(rstd_ready, 1)


def project(nc, mem, name, src, wide, wq, wk, wv, affine=None):
    with stage(nc, name) as (ctx, sem):

        parts = [ctx.enter_context(nc.sbuf_tensor(f"{name}_parts{n}", [P, PARTS, T], BF16)) for n in range(2)]
        rest = ctx.enter_context(nc.sbuf_tensor(f"{name}_rest", [P, T], F32))
        ps = [ctx.enter_context(nc.psum_tensor(f"{name}_ps{b}", [P, CH], F32)) for b in range(8)]
        turned = sem("turned")
        wide_ready = sem("wide_ready")
        product = sem("product")
        first_part = sem("first_part")
        rest_ready = sem("rest_ready")
        second_part = sem("second_part")
        third_part = sem("third_part")
        v_ready = sem("v_ready")
        parts_stored = sem("parts_stored")
        block = ctx.enter_context(nc.Block())

        @block.sync
        def _(sp):
            for n, dram in enumerate((mem.q_parts_dram, mem.k_parts_dram)):
                sp.wait_ge(third_part, NC * (n + 1))
                sp.dma_start(dram.rearrange("g p t -> p g t"), parts[n][:, :, :]).then_inc(parts_stored, 16)
            sp.wait_ge(parts_stored, 32)

        @block.tensor
        def _(pe):
            for c in range(NC):
                for i in range(TPC):
                    mm = nc.tensor.transpose(ps[c][:, i * P:(i + 1) * P], src[:, c * TPC + i, :], mem.ident[:, :])
                mm.then_inc(turned, 1)
            for n, w in enumerate((wq, wk)):
                for c in range(NC):
                    if n == 0:
                        pe.wait_ge(wide_ready, c + 1)
                    if n == 1 and c == 0:
                        pe.wait_ge(wide_ready, NC)
                    nc.tensor.matmul(ps[4 * (1 - n) + c][:, :], w[:, :], wide[:, c * CH:(c + 1) * CH],
                                     start=True, stop=True).then_inc(product, 1)
            for c in range(NC):
                pe.wait_ge(rest_ready, c + 1)
                for i in range(TPC):
                    t = c * TPC + i
                    mm = nc.tensor.matmul(ps[4 + c][:, i * P:(i + 1) * P], wide[:, t * P:(t + 1) * P], wv[:, :],
                                          start=(i == 0), stop=(i == TPC - 1), skip_group_check=True)
                mm.then_inc(product, 1)

        @block.scalar
        def _(act):
            for c in range(NC):
                act.wait_ge(turned, c + 1)
                out = wide[:, c * CH:(c + 1) * CH]
                if affine is None:
                    nc.scalar.activation(out, ps[c][:, :], ACT.Copy).then_inc(wide_ready, 1)
                else:
                    nc.scalar.activation(out, ps[c][:, :], ACT.Identity, bias=affine[1],
                                         scale=affine[0]).then_inc(wide_ready, 1)
            for n in range(2):
                for c in range(NC):
                    act.wait_ge(product, n * NC + c + 1)
                    nc.scalar.activation(parts[n][:, 0, c * CH:(c + 1) * CH], ps[4 * (1 - n) + c][:, :],
                                         ACT.Copy).then_inc(first_part, 1)
                for c in range(NC):
                    act.wait_ge(rest_ready, n * NC + c + 1)
                    nc.scalar.activation(parts[n][:, 1, c * CH:(c + 1) * CH], rest[:, c * CH:(c + 1) * CH],
                                         ACT.Copy).then_inc(second_part, 1)

        @block.vector
        def _(dve):
            for n in range(2):
                for c in range(NC):
                    col = slice(c * CH, (c + 1) * CH)
                    dve.wait_ge(first_part, n * NC + c + 1)
                    if n == 1:
                        dve.wait_ge(third_part, c + 1)
                    nc.vector.tensor_tensor(rest[:, col], ps[4 * (1 - n) + c][:, :], parts[n][:, 0, col],
                                            ALU.subtract).then_inc(rest_ready, 1)
                for c in range(NC):
                    col = slice(c * CH, (c + 1) * CH)
                    dve.wait_ge(second_part, n * NC + c + 1)
                    nc.vector.tensor_tensor(parts[n][:, 2, col], rest[:, col], parts[n][:, 1, col],
                                            ALU.subtract).then_inc(third_part, 1)
            for c in range(NC):
                dve.wait_ge(product, 2 * NC + c + 1)
                nc.vector.tensor_copy(mem.v_tok[:, c * TPC:(c + 1) * TPC, :],
                                      ps[4 + c][:, :].rearrange("p (i d) -> p i d", d=D)).then_inc(v_ready, 1)


def gather_heads(nc, mem, name, out_tok):
    with stage(nc, name) as (ctx, sem):

        inv = ctx.enter_context(nc.sbuf_tensor(f"{name}_inv", [P, 4, NT], F32))
        ps = [ctx.enter_context(nc.psum_tensor(f"{name}_ps{b}", [P, TPC, NC, VW], F32)) for b in range(4)]
        turned = sem("turned")
        inverted = sem("inverted")
        divided = sem("divided")
        block = ctx.enter_context(nc.Block())

        @block.tensor
        def _(pe):
            for h in range(H):
                if h >= 4:
                    pe.wait_ge(divided, h - 3)
                for s in range(TPC):
                    mm = nc.tensor.transpose(ps[h % 4][:, s, :, :].rearrange("p c r -> p (c r)"),
                                             mem.heads_out[:, h * CH + s * P:h * CH + (s + 1) * P], mem.ident[:, :])
                mm.then_inc(turned, 1)

        @block.vector
        def _(dve):
            def divide(h):
                dve.wait_ge(inverted, h + 1)
                nc.vector.tensor_tensor(
                    out_tok[:, :, h * HD:(h + 1) * HD].rearrange("p (c s) d -> p c s d", c=NC),
                    ps[h % 4][:, :, :, 0:HD].rearrange("p s c d -> p c s d"),
                    inv[:, h % 4, :].rearrange("p (c s) -> p c s", c=NC).unsqueeze(3).broadcast_to([P, NC, TPC, HD]),
                    ALU.mult).then_inc(divided, 1)

            for h in range(H):
                dve.wait_ge(turned, h + 1)
                if h >= 4:
                    dve.wait_ge(divided, h - 3)
                nc.vector.reciprocal(inv[:, h % 4, :].rearrange("p (c s) -> p c s", c=NC),
                                     ps[h % 4][:, :, :, HD].rearrange("p s c -> p c s")).then_inc(inverted, 1)
                if h >= 1:
                    divide(h - 1)
            divide(H - 1)


DEPTH = 2
FH = 8
FD = 64
WIN = 64
KEYS = WIN + P
INNER = FH * FD
HID = int(D * 4 * 2 / 3)
HCH = [(m, min(P, HID - m)) for m in range(0, HID, P)]
QK_SCALE = 8.0
HIDE = -1.0e30
TINY = 1e-24


def rotary_tables():
    half = np.arange(0, FD, 2, dtype=np.float32)
    inv_freq = (1.0 / np.float32(10000.0) ** (half / np.float32(FD))).astype(np.float32)
    t = np.arange(T, dtype=np.float32)
    freqs = (t[:, None] * inv_freq[None, :]).astype(np.float32)
    base = ((half + np.float32(0.4 * FD)) / np.float32(1.4 * FD)).astype(np.float32)
    power = ((t - T // 2) / np.float32(WIN // 2)).astype(np.float32)
    scale = (base[None, :] ** power[:, None]).astype(np.float32)
    cos, sin = np.cos(freqs), np.sin(freqs)
    out = np.empty((2, T, 2, FD), np.float32)
    for n, s in enumerate((scale, 1 / scale)):
        out[0, :, n, :] = np.concatenate([cos * s, cos * s], -1)
        out[1, :, n, :] = np.concatenate([-sin * s, sin * s], -1)
    return out


def window_masks():
    i = np.arange(P)[:, None]
    j = np.arange(KEYS)[None, :] - WIN
    hidden = (i < j) | (i > j + WIN)
    both = np.stack([np.where(hidden | (j < 0), HIDE, 0.0), np.where(hidden, HIDE, 0.0)]).astype(np.float32)
    return (both.view(np.uint32) >> 16).astype(np.uint16)


def shift_tokens(nc, mem, name, src):
    half = D // 2
    with stage(nc, name) as (ctx, sem):
        cleared = sem("cleared")
        shifted = sem("shifted")
        block = ctx.enter_context(nc.Block())

        @block.sync
        def _(sp):
            sp.dma_start(mem.h[1:P, :, half:D], src[0:P - 1, :, half:D]).then_inc(shifted, 16)
            sp.dma_start(mem.h[0:1, 1:NT, half:D], src[P - 1:P, 0:NT - 1, half:D]).then_inc(shifted, 16)
            sp.wait_ge(shifted, 32)

        @block.vector
        def _(dve):
            nc.vector.tensor_copy(mem.h[:, :, 0:half], src[:, :, 0:half]).then_inc(cleared, 1)
            nc.vector.memset(mem.h[0:1, 0, half:D], 0.0).then_inc(cleared, 1)


def load_layer(nc, mem, a, name, layer):
    with stage(nc, name) as (ctx, sem):
        loaded = sem("loaded")
        gained = sem("gained")
        gains = ctx.enter_context(nc.sbuf_tensor(f"{name}_gains", [P, 2, FD], F32))
        block = ctx.enter_context(nc.Block())

        @block.sync
        def _(sp):
            n = 0
            for dst, src in (
                (gains[:, 0, :], a["q_scale"][layer].partition_broadcast(P)),
                (gains[:, 1, :], a["k_scale"][layer].partition_broadcast(P)),
                (mem.rot_cos[:, :, :, :], a["rotary"][0].rearrange("(i p) n d -> p i n d", p=P)),
                (mem.rot_sin[:, :, :, :], a["rotary"][1].rearrange("(i p) n d -> p i n d", p=P)),
            ):
                sp.dma_start(dst, src).then_inc(loaded, 16)
            rest = [
                (mem.wqkv[:, :], a["wqkv"][layer]),
                (mem.wo[:, :, :], a["wo"][layer].rearrange("(j p) n -> p j n", p=P)),
                (mem.w1[:, :], a["w1"][layer]),
                (mem.b2[:, :], a["b2"][layer].partition_broadcast(P)),
                (mem.ln[:, 0:1], a["ln_g"][layer].unsqueeze(1)),
                (mem.ln[:, 1:2], a["ln_b"][layer].unsqueeze(1)),
            ]
            for m, (h0, n) in enumerate(HCH):
                rest.append((mem.w2[0:n, m, :], a["w2"][layer][h0:h0 + n, :]))
                for half in range(2):
                    rest.append((mem.b1[0:n, half, m:m + 1],
                                 a["b1"][layer][half * HID + h0:half * HID + h0 + n].unsqueeze(1)))
            for dst, src in rest:
                sp.dma_start(dst, src).then_inc(loaded, 16)
            sp.wait_ge(loaded, 16 * (4 + len(rest)))

        @block.vector
        def _(dve):
            dve.wait_ge(loaded, 16 * (4 + 6 + 3 * len(HCH)))
            nc.vector.tensor_scalar(gains[:, 0, :], gains[:, 0, :], QK_SCALE, None, ALU.mult).then_inc(gained, 1)
            dve.wait_ge(gained, 1)
            hf = FD // 2
            whole = gains[:, :, :].unsqueeze(1).broadcast_to([P, NT, 2, FD])
            nc.vector.tensor_tensor(mem.rot_cos[:, :, :, :], mem.rot_cos[:, :, :, :], whole,
                                    ALU.mult).then_inc(gained, 1)
            for half in range(2):
                d = slice(half * hf, (half + 1) * hf)
                o = slice((1 - half) * hf, (2 - half) * hf)
                nc.vector.tensor_tensor(mem.rot_sin[:, :, :, d], mem.rot_sin[:, :, :, d],
                                        gains[:, :, o].unsqueeze(1).broadcast_to([P, NT, 2, hf]),
                                        ALU.mult).then_inc(gained, 1)


def local_attention(nc, mem, name, src, dst):
    NQ = 2 * FH
    with stage(nc, name) as (ctx, sem):
        def sb(n, shape, dt=F32):
            return ctx.enter_context(nc.sbuf_tensor(f"{name}_{n}", shape, dt))

        def psum(n, shape):
            return ctx.enter_context(nc.psum_tensor(f"{name}_{n}", shape, F32))


        h_tile = sb("h_tile", [P, D])
        hT = sb("hT", [P, P])
        squares = sb("squares", [P, NQ, FD])
        norms = sb("norms", [P, NQ])
        inv_norm = sb("inv_norm", [P, NQ])
        minus_half = sb("minus_half", [P, NQ])
        straight = sb("straight", [P, NQ, FD])
        turned = sb("turned", [P, NQ, FD])
        qk = sb("qk", [P, NQ, FD])
        qkT = sb("qkT", [P, FH // 2, P])
        kT = sb("kT", [P, FH // 2, KEYS])
        v = sb("v", [P, INNER])
        v_before = sb("v_before", [WIN, INNER])
        neg_max = sb("neg_max", [P, FH])
        sums = sb("sums", [P, FH])
        inv_sum = sb("inv_sum", [P, FH])
        probs = sb("probs", [P, FH, KEYS])
        pT = sb("pT", [P, FH, P])
        pT_before = sb("pT_before", [WIN, FH, P])
        oT = sb("oT", [P, FH // 2, P])

        ps_qk = psum("ps_qk", [P, NQ, FD])
        ps_v = psum("ps_v", [P, INNER])
        ps_o = psum("ps_o", [P, FH // 2, P])
        ps_s = psum("ps_s", [P, FH // 2, CH])

        h_copied = sem("h_copied")
        h_turned = sem("h_turned")
        hT_ready = sem("hT_ready")
        qkv_made = sem("qkv_made")
        squared = sem("squared")
        norms_summed = sem("norms_summed")
        norms_ready = sem("norms_ready")
        inv_norm_ready = sem("inv_norm_ready")
        rotated = sem("rotated")
        added = sem("added")
        qk_ready = sem("qk_ready")
        qk_turned = sem("qk_turned")
        k_kept = sem("k_kept")
        qT_ready = sem("qT_ready")
        v_kept = sem("v_kept")
        v_ready = sem("v_ready")
        scored = sem("scored")
        negated = sem("negated")
        exped = sem("exped")
        inverted = sem("inverted")
        divided = sem("divided")
        p_turned = sem("p_turned")
        pT_ready = sem("pT_ready")
        weighed = sem("weighed")
        oT_ready = sem("oT_ready")
        projected = sem("projected")
        result = sem("result")
        first_set = sem("first_set")
        block = ctx.enter_context(nc.Block())

        def scores_of(hd):
            bank, at = 2 * (hd // 4) + hd % 2, hd % 4 // 2 * KEYS
            return ps_s[:, bank, at:at + KEYS]

        def tiles(eng, body):
            body(0, True, False)
            with eng.Fori(1, NT - 1) as i:
                body(i, False, False)
            body(NT - 1, False, True)

        @block.gpsimd
        def _(pool):
            nc.gpsimd.memset(minus_half[:], -0.5).then_inc(first_set, 1)
            nc.gpsimd.memset(kT[:, :, 0:WIN], 0.0).then_inc(k_kept, 1)
            nc.gpsimd.memset(v_before[:], 0.0).then_inc(v_kept, 1)
            pool.wait_ge(first_set, 1)

            def make(i):
                if not isinstance(i, int) or i > 0:
                    pool.wait_ge(h_turned, i)
                nc.gpsimd.tensor_copy(h_tile[:, :], mem.h[:, bass.ds(i, 1), :].squeeze(1)).then_inc(h_copied, 1)
                pool.wait_ge(norms_ready, i + 1)
                nc.gpsimd.tensor_tensor(inv_norm[:, :], norms[:, :], minus_half[:, :],
                                        ALU.pow).then_inc(inv_norm_ready, 1)
                pool.wait_ge(rotated, 6 * (i + 1))
                nc.gpsimd.tensor_tensor(straight[:, :, :], straight[:, :, :], turned[:, :, :],
                                        ALU.add).then_inc(added, 1)

            def tile(i, first, last):
                if not last:
                    make(i + 1)
            make(0)
            tiles(pool, tile)

        @block.tensor
        def _(pe):
            def make(i):
                pe.wait_ge(h_copied, i + 1)
                if not isinstance(i, int) or i > 0:
                    pe.wait_ge(v_ready, i)
                nc.tensor.transpose(ps_v[:, 0:P], h_tile[:, :], mem.ident[:, :]).then_inc(h_turned, 1)
                pe.wait_ge(hT_ready, i + 1)
                for n in range(2):
                    mm = nc.tensor.matmul(ps_qk[:, n * FH:(n + 1) * FH, :].rearrange("p h d -> p (h d)"), hT[:, :],
                                          mem.wqkv[:, n * INNER:(n + 1) * INNER], start=True, stop=True)
                mm.then_inc(qkv_made, 1)
                nc.tensor.matmul(ps_v[:, :], hT[:, :], mem.wqkv[:, 2 * INNER:3 * INNER], start=True,
                                 stop=True).then_inc(qkv_made, 1)

            def tile(i, first, last):
                pe.wait_ge(qk_ready, i + 1)
                if not first:
                    pe.wait_ge(pT_ready, i * 4)
                for n in range(2):
                    for j in range(FH // 2):
                        mm = nc.tensor.transpose(
                            ps_s[:, n, j * P:(j + 1) * P],
                            qk[:, n * FH + 2 * j:n * FH + 2 * j + 2, :].rearrange("p h d -> p (h d)"),
                            mem.ident[:, :])
                    mm.then_inc(qk_turned, 1)
                pe.wait_ge(qT_ready, 2 * (i + 1))
                pe.wait_ge(k_kept, i + 1)
                mask = mem.window_masks[:, 0 if first else 1, :].unsqueeze(1).broadcast_to([P, 2, KEYS])
                for g in range(2):
                    for bank in (2 * g, 2 * g + 1):
                        nc.tensor.matmul(ps_s[:, bank, 0:2 * KEYS].rearrange("p (h k) -> p h k", k=KEYS),
                                         mem.ident_bf[:, :], mask, start=True, stop=False, skip_group_check=True)
                    for hd in range(4 * g, 4 * g + 4):
                        r = slice(hd % 2 * FD, (hd % 2 + 1) * FD)
                        mm = nc.tensor.matmul(scores_of(hd), qkT[r, hd // 2, :], kT[r, hd // 2, :],
                                              start=False, stop=(hd % 4 >= 2), skip_group_check=True)
                    mm.then_inc(scored, 1)
                if not last:
                    make(i + 1)
                for j in range(FH):
                    pe.wait_ge(divided, i * FH + (j + 1))
                    nc.tensor.transpose(ps_s[:, j // 4, (j % 4) * P:(j % 4 + 1) * P], probs[:, j, WIN:KEYS],
                                        mem.ident[:, :])
                    mm = nc.tensor.transpose(ps_s[0:WIN, 2 + j // 4, (j % 4) * P:(j % 4 + 1) * P],
                                             probs[:, j, 0:WIN], mem.ident[:, :])
                    if j % 4 == 3:
                        mm.then_inc(p_turned, 1)
                pe.wait_ge(v_ready, i + 1)
                pe.wait_ge(v_kept, i + 1)
                if not first:
                    pe.wait_ge(result, i)
                for j in range(FH // 2):
                    if j % 2 == 0:
                        pe.wait_ge(pT_ready, i * 4 + (j + 2))
                    for n in range(2):
                        hd = 2 * j + n
                        out = ps_o[n * FD:(n + 1) * FD, j, :]
                        nc.tensor.matmul(out, v[:, hd * FD:(hd + 1) * FD], pT[:, hd, :],
                                         start=(j == 0), stop=False, skip_group_check=True)
                        mm = nc.tensor.matmul(out, v_before[:, hd * FD:(hd + 1) * FD], pT_before[:, hd, :],
                                              start=False, stop=True, skip_group_check=True)
                mm.then_inc(weighed, 1)
                pe.wait_ge(oT_ready, i + 1)
                for j in range(FH // 2):
                    mm = nc.tensor.matmul(ps_o[:, 0, :], oT[:, j, :], mem.wo[:, j, :], start=(j == 0),
                                          stop=(j == FH // 2 - 1))
                mm.then_inc(projected, 1)

            make(0)
            tiles(pe, tile)

        @block.scalar
        def _(act):
            def make(i):
                act.wait_ge(h_turned, i + 1)
                nc.scalar.activation(hT[:, :], ps_v[:, 0:P], ACT.Copy).then_inc(hT_ready, 1)
                act.wait_ge(qkv_made, 2 * i + 1)
                nc.scalar.activation(squares[:, :, :], ps_qk[:, :, :], ACT.Square).then_inc(squared, 1)

            def keep_v(i):
                act.wait_ge(qkv_made, 2 * i + 2)
                act.wait_ge(v_kept, i + 1)
                nc.scalar.activation(v[:, :], ps_v[:, :], ACT.Copy).then_inc(v_ready, 1)

            def tile(i, first, last):
                for n, dst_T in enumerate((qkT[:, :, :], kT[:, :, WIN:KEYS])):
                    act.wait_ge(qk_turned, 2 * i + (n + 1))
                    if n == 1:
                        act.wait_ge(k_kept, i + 1)
                    nc.scalar.activation(dst_T, ps_s[:, n, :].rearrange("p (j t) -> p j t", t=P),
                                         ACT.Copy).then_inc(qT_ready, 1)
                if not last:
                    act.wait_ge(h_turned, i + 2)
                    nc.scalar.activation(hT[:, :], ps_v[:, 0:P], ACT.Copy).then_inc(hT_ready, 1)
                for j in range(FH):
                    if j % 4 == 0:
                        act.wait_ge(negated, 2 * i + (j // 4 + 1))
                    nc.scalar.activation(probs[:, j, :], scores_of(j), ACT.Exp, bias=neg_max[:, j:j + 1],
                                         accum_out=sums[:, j:j + 1]).then_inc(exped, 1)
                if not last:
                    act.wait_ge(qkv_made, 2 * i + 3)
                    nc.scalar.activation(squares[:, :, :], ps_qk[:, :, :], ACT.Square).then_inc(squared, 1)
                for j in range(2):
                    act.wait_ge(p_turned, 2 * i + (j + 1))
                    nc.scalar.activation(pT[:, 4 * j:4 * j + 4, :],
                                         ps_s[:, j, :].rearrange("p (h t) -> p h t", t=P),
                                         ACT.Copy).then_inc(pT_ready, 1)
                    nc.scalar.activation(pT_before[:, 4 * j:4 * j + 4, :],
                                         ps_s[0:WIN, 2 + j, :].rearrange("p (h t) -> p h t", t=P),
                                         ACT.Copy).then_inc(pT_ready, 1)
                act.wait_ge(weighed, i + 1)
                nc.scalar.activation(oT[:, :, :], ps_o[:, :, :], ACT.Copy).then_inc(oT_ready, 1)
                if not last:
                    keep_v(i + 1)

            make(0)
            keep_v(0)
            tiles(act, tile)

        @block.vector
        def _(dve):
            hf = FD // 2

            def make(i):
                dve.wait_ge(squared, i + 1)
                nc.vector.tensor_reduce(norms[:, :], squares[:, :, :], AX.X, ALU.add).then_inc(norms_summed, 1)
                dve.wait_ge(norms_summed, i + 1)
                nc.vector.tensor_scalar(norms[:, :], norms[:, :], TINY, None, ALU.max).then_inc(norms_ready, 1)
                if not isinstance(i, int) or i > 0:
                    dve.wait_ge(qk_ready, i)
                for n in range(2):
                    c = slice(n * FH, (n + 1) * FH)
                    cos = mem.rot_cos[:, bass.ds(i, 1), n, :].broadcast_to([P, FH, FD])
                    nc.vector.tensor_tensor(straight[:, c, :], ps_qk[:, c, :], cos, ALU.mult).then_inc(rotated, 1)
                for n in range(2):
                    c = slice(n * FH, (n + 1) * FH)
                    for half in range(2):
                        d = slice(half * hf, (half + 1) * hf)
                        o = slice((1 - half) * hf, (2 - half) * hf)
                        sin = mem.rot_sin[:, bass.ds(i, 1), n, d].broadcast_to([P, FH, hf])
                        nc.vector.tensor_tensor(turned[:, c, d], ps_qk[:, c, o], sin, ALU.mult).then_inc(rotated, 1)

            def normed(i):
                dve.wait_ge(inv_norm_ready, i + 1)
                dve.wait_ge(added, i + 1)
                if not isinstance(i, int) or i > 0:
                    dve.wait_ge(qk_turned, 2 * i)
                nc.vector.tensor_tensor(qk[:, :, :], straight[:, :, :],
                                        inv_norm[:, :].unsqueeze(2).broadcast_to([P, NQ, FD]),
                                        ALU.mult).then_inc(qk_ready, 1)

            def tile(i, first, last):
                for g in range(2):
                    dve.wait_ge(scored, 2 * i + (g + 1))
                    if g == 0 and not first:
                        dve.wait_ge(exped, i * FH)
                    nc.vector.tensor_reduce(
                        neg_max[:, 4 * g:4 * g + 4].rearrange("p (h b) -> p b h", b=2),
                        ps_s[:, 2 * g:2 * g + 2, 0:2 * KEYS].rearrange("p b (h k) -> p b h k", k=KEYS),
                        AX.X, ALU.max, negate=True).then_inc(negated, 1)
                if not last:
                    nc.vector.tensor_copy(kT[:, :, 0:WIN], kT[:, :, P:KEYS]).then_inc(k_kept, 1)
                dve.wait_ge(exped, (i + 1) * FH)
                nc.vector.reciprocal(inv_sum[:, :], sums[:, :]).then_inc(inverted, 1)
                dve.wait_ge(inverted, i + 1)
                for j in range(FH):
                    nc.vector.tensor_scalar(probs[:, j, :], probs[:, j, :], inv_sum[:, j:j + 1], None,
                                            ALU.mult).then_inc(divided, 1)
                if not last:
                    make(i + 1)
                    normed(i + 1)
                if not last:
                    dve.wait_ge(weighed, i + 1)
                    nc.vector.tensor_copy(v_before[:, :], v[WIN:P, :]).then_inc(v_kept, 1)
                dve.wait_ge(projected, i + 1)
                nc.vector.tensor_tensor(dst[:, bass.ds(i, 1), :].squeeze(1), ps_o[:, 0, :],
                                        src[:, bass.ds(i, 1), :].squeeze(1), ALU.add).then_inc(result, 1)

            make(0)
            normed(0)
            tiles(dve, tile)


def feed_forward(nc, mem, name, dst):
    NH = len(HCH)
    with stage(nc, name) as (ctx, sem):
        def sb(n, shape, dt=F32):
            return ctx.enter_context(nc.sbuf_tensor(f"{name}_{n}", shape, dt))


        hT = sb("hT", [P, 2, CH])
        gate = sb("gate", [P, NH, CH])
        hidden = sb("hidden", [P, 2, NH, CH])
        ps = [ctx.enter_context(nc.psum_tensor(f"{name}_ps{b}", [P, CH], F32)) for b in range(8)]
        ps_a, ps_g, ps_t, ps_y = ps[0:NH], ps[NH:2 * NH], ps[6], ps[7]
        turned = sem("turned")
        hT_ready = sem("hT_ready")
        biased = sem("biased")
        widened = sem("widened")
        gated = sem("gated")
        hidden_ready = sem("hidden_ready")
        narrowed = sem("narrowed")
        result = sem("result")
        block = ctx.enter_context(nc.Block())

        @block.gpsimd
        def _(pool):
            for c in range(NC):
                t = slice(c * TPC, (c + 1) * TPC)
                nc.gpsimd.tensor_tensor(dst[:, t, :], dst[:, t, :],
                                        mem.b2[:, :].unsqueeze(1).broadcast_to([P, TPC, D]),
                                        ALU.add).then_inc(biased, 1)

        @block.tensor
        def _(pe):
            def turn(c):
                if c:
                    pe.wait_ge(hT_ready, c)
                for i in range(TPC):
                    mm = nc.tensor.transpose(ps_t[:, i * P:(i + 1) * P], mem.h[:, c * TPC + i, :], mem.ident[:, :])
                mm.then_inc(turned, 1)

            def narrow(c):
                pe.wait_ge(hidden_ready, NH * (c + 1))
                if c:
                    pe.wait_ge(result, c)
                for i in range(TPC):
                    for m, (_, n) in enumerate(HCH):
                        mm = nc.tensor.matmul(ps_y[:, i * P:(i + 1) * P], hidden[0:n, c % 2, m, i * P:(i + 1) * P],
                                              mem.w2[0:n, m, :], start=(i == 0 and m == 0),
                                              stop=(m == NH - 1), skip_group_check=True)
                mm.then_inc(narrowed, 1)

            turn(0)
            for c in range(NC):
                pe.wait_ge(hT_ready, c + 1)
                for m, (h0, n) in enumerate(HCH):
                    if c:
                        pe.wait_ge(hidden_ready, NH * (c - 1) + m + 1)
                    for half, bank in ((1, ps_g[m]), (0, ps_a[m])):
                        mm = nc.tensor.matmul(bank[0:n, :], mem.w1[:, half * HID + h0:half * HID + h0 + n],
                                              hT[:, c % 2, :], start=True, stop=True)
                    mm.then_inc(widened, 1)
                if c + 1 < NC:
                    turn(c + 1)
                if c:
                    narrow(c - 1)
            narrow(NC - 1)

        @block.scalar
        def _(act):
            def turn(c):
                act.wait_ge(turned, c + 1)
                if c >= 2:
                    act.wait_ge(widened, NH * (c - 1))
                nc.scalar.activation(hT[:, c % 2, :], ps_t[:, :], ACT.Identity, bias=mem.ln[:, 1:2],
                                     scale=mem.ln[:, 0:1]).then_inc(hT_ready, 1)
            turn(0)
            for c in range(NC):
                for m, (h0, n) in enumerate(HCH):
                    act.wait_ge(widened, NH * c + m + 1)
                    if c:
                        act.wait_ge(hidden_ready, NH * (c - 1) + m + 1)
                    nc.scalar.activation(gate[0:n, m, :], ps_g[m][0:n, :], ACT.Gelu,
                                         bias=mem.b1[0:n, 1, m:m + 1]).then_inc(gated, 1)
                if c + 1 < NC:
                    turn(c + 1)

        @block.vector
        def _(dve):
            def add(c):
                t = slice(c * TPC, (c + 1) * TPC)
                dve.wait_ge(biased, c + 1)
                dve.wait_ge(narrowed, c + 1)
                nc.vector.tensor_tensor(dst[:, t, :], dst[:, t, :], ps_y[:, :].rearrange("p (i d) -> p i d", d=D),
                                        ALU.add).then_inc(result, 1)
            for c in range(NC):
                for m, (h0, n) in enumerate(HCH):
                    dve.wait_ge(gated, NH * c + m + 1)
                    if c >= 2:
                        dve.wait_ge(narrowed, c - 1)
                    nc.vector.scalar_tensor_tensor(out=hidden[0:n, c % 2, m, :], in0=ps_a[m][0:n, :],
                                                   scalar=mem.b1[0:n, 0, m:m + 1], in1=gate[0:n, m, :],
                                                   op0=ALU.add, op1=ALU.mult).then_inc(hidden_ready, 1)
                if c:
                    add(c - 1)
            add(NC - 1)


def linear_out(nc, mem, name, src, w, dst, add):
    with stage(nc, name) as (ctx, sem):

        wide = ctx.enter_context(nc.sbuf_tensor(f"{name}_wide", [P, T], F32))
        ps = [ctx.enter_context(nc.psum_tensor(f"{name}_ps{b}", [P, CH], F32)) for b in range(8)]
        turned = sem("turned")
        wide_ready = sem("wide_ready")
        product = sem("product")
        result = sem("result")
        block = ctx.enter_context(nc.Block())

        @block.tensor
        def _(pe):
            for c in range(NC):
                for i in range(TPC):
                    mm = nc.tensor.transpose(ps[c][:, i * P:(i + 1) * P], src[:, c * TPC + i, :], mem.ident[:, :])
                mm.then_inc(turned, 1)
            for c in range(NC):
                pe.wait_ge(wide_ready, c + 1)
                for i in range(TPC):
                    t = c * TPC + i
                    mm = nc.tensor.matmul(ps[4 + c][:, i * P:(i + 1) * P], wide[:, t * P:(t + 1) * P], w[:, :],
                                          start=(i == 0), stop=(i == TPC - 1), skip_group_check=True)
                mm.then_inc(product, 1)

        @block.scalar
        def _(act):
            for c in range(NC):
                act.wait_ge(turned, c + 1)
                nc.scalar.activation(wide[:, c * CH:(c + 1) * CH], ps[c][:, :], ACT.Copy).then_inc(wide_ready, 1)

        @block.vector
        def _(dve):
            for c in range(NC):
                t = slice(c * TPC, (c + 1) * TPC)
                y = ps[4 + c][:, :].rearrange("p (i d) -> p i d", d=D)
                dve.wait_ge(product, c + 1)
                if add:
                    nc.vector.tensor_tensor(dst[:, t, :], dst[:, t, :], y, ALU.add).then_inc(result, 1)
                else:
                    nc.vector.tensor_copy(dst[:, t, :], y).then_inc(result, 1)


def gate_residual(nc, mem, name, f, s, x):
    with stage(nc, name) as (ctx, sem):
        gated = sem("gated")
        product = sem("product")
        result = sem("result")
        block = ctx.enter_context(nc.Block())

        @block.scalar
        def _(act):
            for c in range(NC):
                t = slice(c * TPC, (c + 1) * TPC)
                nc.scalar.activation(f[:, t, :], f[:, t, :], ACT.Silu).then_inc(gated, 1)

        @block.vector
        def _(dve):
            for c in range(NC):
                t = slice(c * TPC, (c + 1) * TPC)
                dve.wait_ge(gated, c + 1)
                nc.vector.tensor_tensor(s[:, t, :], s[:, t, :], f[:, t, :], ALU.mult).then_inc(product, 1)
                dve.wait_ge(product, c + 1)
                nc.vector.tensor_tensor(x[:, t, :], x[:, t, :], s[:, t, :], ALU.add).then_inc(result, 1)


E = 8
TOP = 2
EH = 4 * D // E
PAIRS = E // 2
GROUPS = PAIRS + 1


def experts(nc, mem, a, name, wide, s, x, out):
    with stage(nc, name) as (ctx, sem):
        def sb(n, shape, dt=F32):
            return ctx.enter_context(nc.sbuf_tensor(f"{name}_{n}", shape, dt))

        def psum(n, shape):
            return ctx.enter_context(nc.psum_tensor(f"{name}_{n}", shape, F32))


        w_route = sb("w_route", [P, E])
        route_bias = sb("route_bias", [P, E])
        w_in = sb("w_in", [P, GROUPS, 2, EH])
        b_in = sb("b_in", [P, GROUPS])
        w_out = sb("w_out", [P, GROUPS, D])
        b_out = sb("b_out", [E + 1, D])
        lower = sb("lower", [P, E, E])
        spread = sb("spread", [E, PAIRS, P])
        logits = sb("logits", [P, NT, E])
        size = sb("size", [P, NT, E])
        one_plus = sb("one_plus", [P, NT, E])
        over = sb("over", [P, NT, E])
        exact = sb("exact", [P, NT, E])
        log_term = sb("log_term", [P, NT, E])
        half = sb("half", [P, NT, E])
        value = sb("value", [P, NT, E])
        above = sb("above", [P, NT, E, E])
        level = sb("level", [P, NT, E, E])
        rank = sb("rank", [P, NT, E])
        weight = sb("weight", [P, NT, E + 1])
        weightT = sb("weightT", [E + 1, T])
        hidden = sb("hidden", [P, 2, GROUPS, CH])
        gate = sb("gate", [P, 2, CH])

        ps_r = psum("ps_r", [P, CH])
        ps_t = psum("ps_t", [E + 1, CH])
        ps_h = [psum(f"ps_h{b}", [P, CH]) for b in range(2)]
        ps_w = [psum(f"ps_w{b}", [P, CH]) for b in range(2)]
        ps_y = [psum(f"ps_y{b}", [P, CH]) for b in range(2)]

        loaded = sem("loaded")
        set_up = sem("set_up")
        routed = sem("routed")
        step = sem("step")
        exped = sem("exped")
        rooted = sem("rooted")
        weighed = sem("weighed")
        w_turned = sem("w_turned")
        weightT_ready = sem("weightT_ready")
        hid_made = sem("hid_made")
        activated = sem("activated")
        spread_made = sem("spread_made")
        hid_weighed = sem("hid_weighed")
        mixed = sem("mixed")
        gated = sem("gated")
        multiplied = sem("multiplied")
        result = sem("result")
        stored = sem("stored")
        block = ctx.enter_context(nc.Block())
        N_LOADS = 14

        @block.sync
        def _(sp):
            pairs = a["rW1"].rearrange("(g o) d h -> d g o h", o=2)
            loads = [
                (w_route[:, :], a["w_route"]),
                (route_bias[:, :], a["expert_bias"].partition_broadcast(P)),
                (lower[:, :, :], a["lower"].partition_broadcast(P)),
                (spread[:, :, :], a["spread"]),
                (w_in[:, PAIRS, 0, :], a["sW1"]),
                (b_in[0:EH, PAIRS:GROUPS], a["sb1"].unsqueeze(1)),
                (b_in[:, 0:PAIRS], a["rb1"]),
                (w_out[:, 0:PAIRS, :], a["rW2"]),
                (w_out[0:EH, PAIRS, :], a["sW2"]),
                (b_out[0:E, :], a["rb2"]),
                (b_out[E:E + 1, :], a["sb2"].unsqueeze(0)),
            ] + [(w_in[:, g, :, :], pairs[:, g, :, :]) for g in range(PAIRS)]
            assert len(loads) == N_LOADS + 1
            for dst, src in loads:
                sp.dma_start(dst, src).then_inc(loaded, 16)
            for c in range(NC):
                sp.wait_ge(result, c + 1)
                sp.dma_start(tiles_of(out)[:, c * TPC:(c + 1) * TPC, :],
                             x[:, c * TPC:(c + 1) * TPC, :]).then_inc(stored, 16)
            sp.wait_ge(stored, 16 * NC)

        @block.gpsimd
        def _(pool):
            nc.gpsimd.memset(half[:], 0.5).then_inc(set_up, 1)
            nc.gpsimd.memset(weight[:, :, E:E + 1], 1.0).then_inc(set_up, 1)
            pool.wait_ge(set_up, 2)
            pool.wait_ge(step, 10)
            nc.gpsimd.tensor_tensor(value[:, :, :], log_term[:, :, :], half[:, :, :], ALU.pow).then_inc(rooted, 1)

        @block.tensor
        def _(pe):
            pe.wait_ge(loaded, 16 * (N_LOADS + 1))
            for i in range(NT):
                mm = nc.tensor.matmul(ps_r[:, i * E:(i + 1) * E], wide[:, i * P:(i + 1) * P], w_route[:, :],
                                      start=(i == 0), stop=(i == NT - 1), skip_group_check=True)
            mm.then_inc(routed, 1)
            pe.wait_ge(weighed, 1)
            pe.wait_ge(set_up, 2)
            for c in range(NC):
                if c:
                    pe.wait_ge(weightT_ready, c)
                for i in range(TPC):
                    mm = nc.tensor.transpose(ps_t[:, i * P:(i + 1) * P], weight[:, c * TPC + i, :], mem.ident[:, :])
                mm.then_inc(w_turned, 1)

            def mix(c):
                pe.wait_ge(activated, GROUPS * (c + 1))
                pe.wait_ge(hid_weighed, PAIRS * (c + 1))
                if c >= 2:
                    pe.wait_ge(gated, c - 1)
                for i in range(TPC):
                    col = slice(i * P, (i + 1) * P)
                    for g in range(GROUPS):
                        k = P if g < PAIRS else EH
                        nc.tensor.matmul(ps_y[c % 2][:, col], hidden[0:k, c % 2, g, col], w_out[0:k, g, :],
                                         start=(i == 0 and g == 0), stop=False, skip_group_check=True)
                    mm = nc.tensor.matmul(ps_y[c % 2][:, col], weightT[:, c * CH + i * P:c * CH + (i + 1) * P],
                                          b_out[:, :], start=False, stop=True, skip_group_check=True)
                mm.then_inc(mixed, 1)

            for c in range(NC):
                for g in range(GROUPS):
                    k = P if g < PAIRS else EH
                    n, p = c * GROUPS + g, c * PAIRS + g
                    if n >= 2:
                        pe.wait_ge(activated, n - 1)
                    nc.tensor.matmul(ps_h[n % 2][0:k, :],
                                     w_in[:, g, :, :].rearrange("p o h -> p (o h)")[:, 0:k],
                                     wide[:, c * CH:(c + 1) * CH], start=True, stop=True).then_inc(hid_made, 1)
                    if g < PAIRS:
                        pe.wait_ge(weightT_ready, c + 1)
                        if p >= 2:
                            pe.wait_ge(hid_weighed, p - 1)
                        nc.tensor.matmul(ps_w[p % 2][:, :], spread[:, g, :], weightT[0:E, c * CH:(c + 1) * CH],
                                         start=True, stop=True).then_inc(spread_made, 1)
                if c:
                    mix(c - 1)
            mix(NC - 1)

        @block.scalar
        def _(act):
            act.wait_ge(step, 1)
            nc.scalar.activation(size[:, :, :], logits[:, :, :], ACT.Abs).then_inc(exped, 1)
            act.wait_ge(exped, 1)
            nc.scalar.activation(size[:, :, :], size[:, :, :], ACT.Exp, scale=-1.0).then_inc(exped, 1)
            act.wait_ge(step, 2)
            nc.scalar.activation(log_term[:, :, :], one_plus[:, :, :], ACT.Ln).then_inc(exped, 1)
            for c in range(NC):
                act.wait_ge(w_turned, c + 1)
                nc.scalar.activation(weightT[:, c * CH:(c + 1) * CH], ps_t[:, :], ACT.Copy).then_inc(weightT_ready, 1)

            def open_gate(c):
                act.wait_ge(mixed, c + 1)
                if c >= 2:
                    act.wait_ge(multiplied, c - 1)
                nc.scalar.activation(gate[:, c % 2, :], ps_y[c % 2][:, :], ACT.Silu).then_inc(gated, 1)

            for c in range(NC):
                if c >= 2:
                    act.wait_ge(mixed, c - 1)
                for g in range(GROUPS):
                    k = P if g < PAIRS else EH
                    n = c * GROUPS + g
                    act.wait_ge(hid_made, n + 1)
                    nc.scalar.activation(hidden[0:k, c % 2, g, :], ps_h[n % 2][0:k, :], ACT.Silu,
                                         bias=b_in[0:k, g:g + 1]).then_inc(activated, 1)
                if c:
                    open_gate(c - 1)
            open_gate(NC - 1)

        @block.vector
        def _(dve):
            done = [0]

            def link(ins):
                done[0] += 1
                ins.then_inc(step, 1)
                dve.wait_ge(step, done[0])

            dve.wait_ge(routed, 1)
            dve.wait_ge(loaded, 16 * (N_LOADS + 1))
            link(nc.vector.tensor_tensor(logits[:, :, :], ps_r[:, 0:NT * E].rearrange("p (i e) -> p i e", e=E),
                                         route_bias[:, :].unsqueeze(1).broadcast_to([P, NT, E]), ALU.add))
            dve.wait_ge(exped, 2)
            link(nc.vector.tensor_scalar(one_plus[:, :, :], size[:, :, :], 1.0, None, ALU.add))
            link(nc.vector.tensor_scalar(over[:, :, :], one_plus[:, :, :], 1.0, None, ALU.subtract))
            link(nc.vector.tensor_scalar(exact[:, :, :], over[:, :, :], 0.0, None, ALU.is_equal))
            link(nc.vector.tensor_tensor(over[:, :, :], over[:, :, :], exact[:, :, :], ALU.add))
            link(nc.vector.reciprocal(over[:, :, :], over[:, :, :]))
            dve.wait_ge(exped, 3)
            link(nc.vector.tensor_tensor(over[:, :, :], over[:, :, :], log_term[:, :, :], ALU.mult))
            link(nc.vector.tensor_tensor(over[:, :, :], over[:, :, :], exact[:, :, :], ALU.add))
            link(nc.vector.tensor_tensor(over[:, :, :], over[:, :, :], size[:, :, :], ALU.mult))
            link(nc.vector.scalar_tensor_tensor(out=log_term[:, :, :], in0=logits[:, :, :], scalar=0.0,
                                                in1=over[:, :, :], op0=ALU.max, op1=ALU.add))
            dve.wait_ge(rooted, 1)
            mine = value[:, :, :].unsqueeze(3).broadcast_to([P, NT, E, E])
            other = value[:, :, :].unsqueeze(2).broadcast_to([P, NT, E, E])
            link(nc.vector.tensor_tensor(above[:, :, :, :], other, mine, ALU.is_gt))
            link(nc.vector.tensor_tensor(level[:, :, :, :], other, mine, ALU.is_equal))
            link(nc.vector.tensor_tensor(level[:, :, :, :], level[:, :, :, :],
                                         lower[:, :, :].unsqueeze(1).broadcast_to([P, NT, E, E]), ALU.mult))
            link(nc.vector.tensor_tensor(above[:, :, :, :], above[:, :, :, :], level[:, :, :, :], ALU.add))
            link(nc.vector.tensor_reduce(rank[:, :, :], above[:, :, :, :], AX.X, ALU.add))
            nc.vector.scalar_tensor_tensor(out=weight[:, :, 0:E], in0=rank[:, :, :], scalar=float(TOP),
                                           in1=value[:, :, :], op0=ALU.is_lt, op1=ALU.mult).then_inc(weighed, 1)

            def finish(c):
                t = slice(c * TPC, (c + 1) * TPC)
                dve.wait_ge(gated, c + 1)
                nc.vector.tensor_tensor(s[:, t, :], s[:, t, :], gate[:, c % 2, :].rearrange("p (i d) -> p i d", d=D),
                                        ALU.mult).then_inc(multiplied, 1)
                dve.wait_ge(multiplied, c + 1)
                nc.vector.tensor_tensor(x[:, t, :], x[:, t, :], s[:, t, :], ALU.add).then_inc(result, 1)

            for c in range(NC):
                for g in range(PAIRS):
                    n, p = c * GROUPS + g, c * PAIRS + g
                    dve.wait_ge(activated, n + 1)
                    dve.wait_ge(spread_made, p + 1)
                    nc.vector.tensor_tensor(hidden[:, c % 2, g, :], hidden[:, c % 2, g, :], ps_w[p % 2][:, :],
                                            ALU.mult).then_inc(hid_weighed, 1)
                if c:
                    finish(c - 1)
            finish(NC - 1)


def constants():
    later = np.arange(P)[None, :] > np.arange(P)[:, None]
    spread = np.zeros((E, PAIRS, 2, EH), np.float32)
    for e in range(E):
        spread[e, e // 2, e % 2, :] = 1.0
    return {
        "ident": np.eye(P, dtype=np.float32),
        "masks": np.stack([np.eye(P), np.where(later, NEG, 0.0), np.where(later.T, NEG, 0.0)]).astype(np.float32),
        "rotary": rotary_tables(),
        "window_masks": window_masks(),
        "lower": np.tril(np.ones((E, E), np.float32), -1),
        "spread": spread.reshape(E, PAIRS, P),
        "fill": np.stack([np.full((MROW - ROWS, T), bits, np.uint16) for bits in (0, 0x3F80)]),
    }


def layout(inputs):
    g = lambda n: np.asarray(inputs[n])
    arrays = {
        "x": g("L0_attn_z").reshape(T, D),
        "ln_scale0": g("L0_attn_ln_scale"),
        "ln_bias0": g("L0_attn_ln_bias"),
        "w_qkv0": g("L0_attn_w_qkv").reshape(D, D, 3).transpose(2, 0, 1),
        "w_proj0": g("L0_attn_w_proj"),
        "b_proj0": g("L0_attn_b_proj"),
        "w_qkv1": g("L1_attn_w_qkv").reshape(3, D, D).transpose(0, 2, 1),
        "w_out1": g("L1_attn_w_out").T,
        "w_route": g("L1_ffn_routing_W").T,
        "expert_bias": g("L1_ffn_expert_bias"),
        "sW1": g("L1_ffn_sW1"), "sb1": g("L1_ffn_sb1"), "sW2": g("L1_ffn_sW2"), "sb2": g("L1_ffn_sb2"),
        "rW1": g("L1_ffn_rW1"),
        "rb1": g("L1_ffn_rb1").reshape(PAIRS, P).T,
        "rW2": g("L1_ffn_rW2").reshape(PAIRS, P, D).transpose(1, 0, 2),
        "rb2": g("L1_ffn_rb2"),
    }
    for n in ("wqkv", "q_scale", "k_scale", "wo", "ln_g", "ln_b", "w1", "b1", "w2", "b2"):
        arrays[n] = g("L0_ffn_" + n)
    arrays.update(constants())
    return {k: np.ascontiguousarray(v) for k, v in arrays.items()}


def load(nc, name, *pairs):
    with stage(nc, name) as (ctx, sem):
        loaded = sem("loaded")
        block = ctx.enter_context(nc.Block())

        @block.sync
        def _(sp):
            for dst, src in pairs:
                sp.dma_start(dst, src).then_inc(loaded, 16)
            sp.wait_ge(loaded, 16 * len(pairs))


def add_bias(nc, name, src, bias, dst):
    with stage(nc, name) as (ctx, sem):
        added = sem("added")
        block = ctx.enter_context(nc.Block())

        @block.vector
        def _(dve):
            nc.vector.tensor_tensor(dst[:, :, :], src[:, :, :], bias[:, :].unsqueeze(1).broadcast_to([P, NT, D]),
                                    ALU.add).then_inc(added, 1)


def gate_layers(nc, mem, a, xn, f):
    with ExitStack() as s1:
        u = lambda n, shape, dt=F32: s1.enter_context(nc.sbuf_tensor(n, shape, dt))
        mem.h = u("h", [P, NT, D])
        mem.rot_cos = u("rot_cos", [P, NT, 2, FD])
        mem.rot_sin = u("rot_sin", [P, NT, 2, FD])
        mem.wqkv = u("wqkv", [P, 3 * INNER])
        mem.wo = u("wo", [P, INNER // P, D])
        mem.w1 = u("w1", [P, 2 * HID])
        mem.w2 = u("w2", [P, len(HCH), D])
        mem.b1 = u("b1", [P, 2, len(HCH)])
        mem.b2 = u("b2", [P, D])
        mem.ln = u("ln", [P, 2])
        mem.window_masks = u("window_masks_sb", [P, 2, KEYS], BF16)
        load(nc, "window_masks", (mem.window_masks[:, :, :], a["window_masks"].bitcast(BF16).rearrange("m p q -> p m q")))
        src = xn
        for layer in range(DEPTH):
            load_layer(nc, mem, a, f"load{layer}", layer)
            shift_tokens(nc, mem, f"shift_a{layer}", src)
            local_attention(nc, mem, f"local{layer}", src, f)
            shift_tokens(nc, mem, f"shift_b{layer}", f)
            normalise(nc, mem, f"ln_f{layer}", [(mem.h, mem.h)])
            feed_forward(nc, mem, f"ff{layer}", f)
            src = f


def mixer(nc, mem, name, causal, project_heads, out_tok):
    with ExitStack() as s0:
        t = lambda n, shape, dt=F32: s0.enter_context(nc.sbuf_tensor(f"{name}_{n}", shape, dt))
        mem.v_tok = out_tok
        project_heads()
        mem.heads_out = t("heads_out", [P, H * CH])
        with ExitStack() as s1:
            mem.QS = s1.enter_context(nc.sbuf_tensor(f"{name}_QS", [P, H * T], BF16))
            mem.KS = s1.enter_context(nc.sbuf_tensor(f"{name}_KS", [P, H * T], BF16))
            attention(nc, mem, name, causal)
        gather_heads(nc, mem, f"{name}_gather", out_tok)


def build(nc, a, out):
    with ExitStack() as ctx:
        def sb(n, shape, dt=F32):
            return ctx.enter_context(nc.sbuf_tensor(n, shape, dt))

        mem = Memory()
        mem.q_parts_dram = nc.dram_tensor("q_parts", (PARTS, D, T), BF16).ap()
        mem.k_parts_dram = nc.dram_tensor("k_parts", (PARTS, D, T), BF16).ap()
        mem.fill = a["fill"].bitcast(BF16)
        x = sb("x", [P, NT, D])
        s = sb("s", [P, NT, D])
        mem.ident = sb("identity", [P, P])
        mem.ident_bf = sb("identity_bf", [P, P], BF16)
        mem.hide_later_keys = sb("hide_later_keys", [P, P], BF16)
        mem.hide_earlier_queries = sb("hide_earlier_queries", [P, P], BF16)
        mem.sums = sb("sums", [P, NT, 6])
        mem.moments = sb("moments", [P, NT, 2])
        mem.rstd = sb("rstd", [P, NT])
        mem.minus_half = sb("minus_half", [P, NT])

        with nc.sbuf_tensor("masks_sb", [P, 3, P], F32) as masks, nc.semaphore("cast") as cast:
            load(nc, "x", (x[:, :, :], tiles_of(a["x"])), (mem.ident[:, :], a["ident"]),
                 (masks[:, :, :], a["masks"].rearrange("m p q -> p m q")))
            with nc.Block() as block:
                @block.vector
                def _(dve):
                    for n, m in enumerate((mem.ident_bf, mem.hide_later_keys, mem.hide_earlier_queries)):
                        nc.vector.tensor_copy(m[:, :], masks[:, n, :]).then_inc(cast, 1)

        with ExitStack() as s0:
            xn = s0.enter_context(nc.sbuf_tensor("xn", [P, NT, D], F32))
            normalise(nc, mem, "ln_x0", [(x, xn)])

            def project0():
                with ExitStack() as s1:
                    u = lambda n, shape: s1.enter_context(nc.sbuf_tensor(n, shape, F32))
                    zn = u("zn", [P, NT, D])
                    wide = u("zn_wide", [P, T])
                    w = [u(f"w0_{n}", [P, D]) for n in range(3)]
                    ls = u("ls", [P, 2])
                    load(nc, "w0", *[(w[n][:, :], a["w_qkv0"][n]) for n in range(3)],
                         (ls[:, 0:1], a["ln_scale0"].unsqueeze(1)), (ls[:, 1:2], a["ln_bias0"].unsqueeze(1)))
                    normalise(nc, mem, "ln_z0", [(xn, zn)])
                    project(nc, mem, "proj0", zn, wide, *w, affine=(ls[:, 0:1], ls[:, 1:2]))

            mixer(nc, mem, "mix0", False, project0, s)
            with ExitStack() as s1:
                u = lambda n, shape: s1.enter_context(nc.sbuf_tensor(n, shape, F32))
                w_proj, b_proj, o = u("w_proj", [P, D]), u("b_proj", [P, D]), u("xnb", [P, NT, D])
                load(nc, "w_proj", (w_proj[:, :], a["w_proj0"]), (b_proj[:, :], a["b_proj0"].partition_broadcast(P)))
                add_bias(nc, "bias0", xn, b_proj, o)
                linear_out(nc, mem, "out0", s, w_proj, o, True)
                f = u("f", [P, NT, D])
                gate_layers(nc, mem, a, xn, f)
                gate_residual(nc, mem, "gate0", f, o, x)

        with ExitStack() as s0:
            wide = s0.enter_context(nc.sbuf_tensor("xn_wide", [P, T], F32))
            w_out = s0.enter_context(nc.sbuf_tensor("w_out1", [P, D], F32))

            def project1():
                with ExitStack() as s1:
                    u = lambda n, shape: s1.enter_context(nc.sbuf_tensor(n, shape, F32))
                    xn = u("xn1", [P, NT, D])
                    w = [u(f"w1_{n}", [P, D]) for n in range(3)]
                    load(nc, "w1", *[(w[n][:, :], a["w_qkv1"][n]) for n in range(3)], (w_out[:, :], a["w_out1"]))
                    normalise(nc, mem, "ln_x1", [(x, xn)])
                    project(nc, mem, "proj1", xn, wide, *w)

            o = s
            mixer(nc, mem, "mix1", True, project1, o)
            linear_out(nc, mem, "out1", o, w_out, s, False)
            experts(nc, mem, a, "moe", wide, s, x, out)


def kernel(**inputs):
    import concourse.bacc as bacc
    from concourse.bass_utils import run_bass_kernel_spmd

    arrays = {f"in_{n}": v for n, v in layout(inputs).items()}
    nc = bacc.Bacc("TRN2", target_bir_lowering=False, num_devices=1)
    a = {n[3:]: nc.dram_tensor(n, v.shape, mybir.dt.from_np(v.dtype), kind="ExternalInput").ap()
         for n, v in arrays.items()}
    out = nc.dram_tensor("out_0", (T, D), F32, kind="ExternalOutput").ap()
    build(nc, a, out)
    r = run_bass_kernel_spmd(nc, [arrays], core_ids=[0])
    return r.results[0]["out_0"].reshape(1, T, D)
```

```python
from contextlib import ExitStack, contextmanager

import concourse.bass as bass
import numpy as np
from concourse import mybir

F32 = mybir.dt.float32
BF16 = mybir.dt.bfloat16
ALU = mybir.AluOpType
ACT = mybir.ActivationFunctionType
AX = mybir.AxisListType

P = 128
T = 2048
D = 128
NT = T // P
CH = 512
NC = T // CH
TPC = CH // P
EPS = 1e-5
NEG = -30000.0

H = 16
HD = D // H
PARTS = 3
ROWS = PARTS * PARTS * HD
MROW = 96
KROWS = MROW + PARTS
VW = 32
SCALE = 1.0 / float(np.sqrt(HD))


class Memory:
    pass


def tiles_of(ap):
    return ap.rearrange("(i p) d -> p i d", p=P)


@contextmanager
def stage(nc, name):
    with ExitStack() as ctx:
        used = []

        def sem(n):
            used.append(nc.alloc_semaphore(f"{name}_{n}"))
            return used[-1]

        def give_back():
            nc.clear_and_free_semaphores(used)
            nc.all_engine_barrier()

        ctx.callback(give_back)
        yield ctx, sem


def attention_units(causal):
    units = []
    for kb in range(NT):
        for c in range(kb // TPC if causal else 0, NC):
            first = max(0, kb * P - c * CH) if causal else 0
            units.append((kb, c, first))
    return units


def max_tiles(causal):
    tiles = []
    for i in range(NT):
        keys = (i + 1) * P if causal else T
        for half in range(2):
            n = min(2 * CH, keys - half * 2 * CH)
            if n > 0:
                tiles.append((i, half, half * 2 * CH, n))
    return tiles


def attention(nc, mem, name, causal):
    units = attention_units(causal)
    mtiles = max_tiles(causal)
    NU, NM = len(units), len(mtiles)
    assert NM % 2 == 0
    group_of = [[u for u, x in enumerate(units) if x[0] == kb] for kb in range(NT)]
    LEAD = 0.84

    with stage(nc, name) as (ctx, sem):
        def sb(n, shape, dt):
            return ctx.enter_context(nc.sbuf_tensor(f"{name}_{n}", shape, dt))


        QS, KS = mem.QS, mem.KS
        v_head = sb("v_head", [P, NT, VW], F32)
        probs = sb("probs", [P, 2, NC, CH], F32)
        part_max = sb("part_max", [P, NT, 2], F32)
        neg_max = sb("neg_max", [P, NT], F32)
        m_rest = sb("m_rest", [NT, P], F32)
        m_parts = sb("m_parts", [NT, PARTS, P], BF16)

        ps_max = [ctx.enter_context(nc.psum_tensor(f"{name}_ps_max{s}", [P, 2 * CH], F32)) for s in range(2)]
        ps_exp = [ctx.enter_context(nc.psum_tensor(f"{name}_ps_exp{s}", [P, CH], F32)) for s in range(3)]
        ps_out = ctx.enter_context(nc.psum_tensor(f"{name}_ps_out", [P, CH], F32))

        filled_first = sem("filled_first")
        filled_rest = sem("filled_rest")
        loads = [sem(f"loads{s}") for s in range(2)]
        heads_loaded = sem("heads_loaded")
        v_cleared = sem("v_cleared")
        v_staged = sem("v_staged")
        max_cleared = sem("max_cleared")
        max_scores = sem("max_scores")
        max_taken = sem("max_taken")
        max_folded = sem("max_folded")
        split = sem("split")
        m_ready = sem("m_ready")
        m_loaded = sem("m_loaded")
        exp_scores = sem("exp_scores")
        probs_ready = sem("probs_ready")
        pv_done = sem("pv_done")
        out_taken = sem("out_taken")

        block = ctx.enter_context(nc.Block())

        @block.sync
        def _(sp):
            def load_rows(h, s):
                for g in range(PARTS):
                    for j in range(PARTS):
                        r = (g * PARTS + j) * HD
                        for stack, parts, n in ((QS, mem.q_parts_dram, g), (KS, mem.k_parts_dram, j)):
                            sp.dma_start(stack[r:r + HD, bass.ds(h * T, T)],
                                         parts[n, bass.ds(h * HD, HD), :]).then_inc(loads[s], 16)

            n_dma = 2 * PARTS * PARTS * 16
            def fill_rows(h, heads, filled):
                for stack, r0, r1, n in ((QS, ROWS, MROW, 0), (KS, ROWS, MROW, 0), (KS, MROW, KROWS, 1)):
                    sp.dma_start(stack[r0:r1, h * T:(h + heads) * T].rearrange("p (h t) -> p h t", t=T),
                                 mem.fill[n, 0:r1 - r0, :].unsqueeze(1).broadcast_to([r1 - r0, heads, T])
                                 ).then_inc(filled, 16)

            load_rows(0, 0)
            fill_rows(0, 1, filled_first)
            load_rows(1, 1)
            fill_rows(1, H - 1, filled_rest)
            with sp.Fori(0, H // 2 - 1) as i:
                for s in range(2):
                    sp.wait_ge(loads[s], i * n_dma + n_dma)
                    sp.sem_inc(heads_loaded, 1)
                    load_rows(i * 2 + (s + 2), s)
            for s in range(2):
                sp.wait_ge(loads[s], n_dma * (H // 2))
                sp.sem_inc(heads_loaded, 1)

        @block.gpsimd
        def _(pool):
            nc.gpsimd.memset(v_head[:], 0.0).then_inc(v_cleared, 1)
            pool.wait_ge(v_cleared, 1)
            nc.gpsimd.memset(v_head[:, :, HD:HD + 1], 1.0).then_inc(v_cleared, 1)
            pool.wait_ge(v_cleared, 2)

            def stage(h):
                nc.gpsimd.tensor_copy(v_head[:, :, 0:HD],
                                      mem.v_tok[:, :, bass.ds(h * HD, HD)]).then_inc(v_staged, 1)
            stage(0)

            def load_max(h):
                pool.wait_ge(m_ready, h + 1)
                for g in range(PARTS):
                    pool.dma_start(
                        QS[MROW + g:MROW + g + 1, bass.ds(h * T, T)].rearrange("o (i p) -> o i p", p=P),
                        m_parts[:, g, :]).then_inc(m_loaded, 16)
            load_max(0)
            with pool.Fori(1, H) as h:
                load_max(h)
                pool.wait_ge(pv_done, h * NT)
                stage(h)

        @block.tensor
        def _(pe):
            def max_tile(h, k):
                i, half, key0, n = mtiles[k]
                if k == 0:
                    if not (isinstance(h, int) and h == 0):
                        pe.wait_ge(m_ready, h)
                    pe.wait_ge(heads_loaded, h + 1)
                    if isinstance(h, int) and h < 2:
                        pe.wait_ge(filled_rest if h else filled_first, 48)
                elif k >= 2:
                    pe.wait_ge(max_taken, h * NM + (k - 1))
                out = ps_max[k % 2]
                last = causal and key0 + n == (i + 1) * P
                for a in range(0, n, CH):
                    m = min(CH, n - a)
                    masked = last and a + m == n
                    mm = nc.tensor.matmul(out[:, a:a + m],
                                          QS[0:MROW, bass.ds(h * T + i * P, P)],
                                          KS[0:MROW, bass.ds(h * T + (key0 + a), m)],
                                          start=True, stop=not masked)
                    if masked:
                        mm = nc.tensor.matmul(out[:, n - P:n], mem.ident_bf[:, :], mem.hide_later_keys[:, :],
                                              start=False, stop=True)
                mm.then_inc(max_scores, 1)

            def transpose_max(h):
                pe.wait_ge(max_folded, h + 1)
                nc.tensor.transpose(ps_max[0][0:NT, 0:P], neg_max[:, :], mem.ident[:, :]).then_inc(max_scores, 1)

            def exp_unit(h, u):
                kb, c, first = units[u]
                if u >= 3:
                    pe.wait_ge(probs_ready, h * NU + (u - 2))
                out = ps_exp[u % 3]
                masked = causal and c == kb // TPC
                mm = nc.tensor.matmul(out[:, 0:CH - first],
                                      KS[0:KROWS, bass.ds(h * T + kb * P, P)],
                                      QS[0:KROWS, bass.ds(h * T + (c * CH + first), CH - first)],
                                      start=True, stop=not masked)
                if masked:
                    mm = nc.tensor.matmul(out[:, 0:P], mem.ident_bf[:, :], mem.hide_earlier_queries[:, :],
                                          start=False, stop=True)
                mm.then_inc(exp_scores, 1)

            def pv(h, kb):
                pe.wait_ge(probs_ready, h * NU + (group_of[kb][-1] + 1))
                if kb == 0:
                    pe.wait_ge(v_staged, h + 1)
                    if not (isinstance(h, int) and h == 0):
                        pe.wait_ge(out_taken, h)
                for u in group_of[kb]:
                    _, c, first = units[u]
                    last = (kb == (c + 1) * TPC - 1) if causal else kb == NT - 1
                    mm = nc.tensor.matmul(ps_out[32 * c:32 * c + VW, first:CH], v_head[:, kb, :],
                                          probs[:, kb % 2, c, first:CH], start=(kb == 0), stop=last,
                                          skip_group_check=True)
                mm.then_inc(pv_done, 1)

            def head(h, next_max):
                pe.wait_ge(m_loaded, h * (16 * PARTS) + 16 * PARTS)
                tiles_done = 0
                for u in range(NU):
                    exp_unit(h, u)
                    kb = units[u][0]
                    if next_max:
                        want = min(NM, int(round(NM * (u + 1) / (LEAD * NU))))
                        while tiles_done < want:
                            max_tile(h + 1, tiles_done)
                            tiles_done += 1
                    if kb >= 1 and u == group_of[kb][min(1, len(group_of[kb]) - 1)]:
                        pv(h, kb - 1)
                if next_max:
                    transpose_max(h + 1)
                pv(h, NT - 1)

            for k in range(NM):
                max_tile(0, k)
            transpose_max(0)
            head(0, True)
            with pe.Fori(1, H - 1) as h:
                head(h, True)
            head(H - 1, False)

        @block.scalar
        def _(act):
            def head(h):
                for u, (kb, c, first) in enumerate(units):
                    if u == group_of[kb][0]:
                        if kb >= 2:
                            act.wait_ge(pv_done, h * NT + (kb - 1))
                        elif kb == 0 and not (isinstance(h, int) and h == 0):
                            act.wait_ge(pv_done, h * NT)
                    act.wait_ge(exp_scores, h * NU + (u + 1))
                    nc.scalar.activation(probs[:, kb % 2, c, first:CH], ps_exp[u % 3][:, 0:CH - first],
                                         ACT.Exp, scale=SCALE).then_inc(probs_ready, 1)
            head(0)
            with act.Fori(1, H) as h:
                head(h)

        @block.vector
        def _(dve):
            def maxima(h):
                for k, (i, half, _, n) in enumerate(mtiles):
                    dve.wait_ge(max_scores, h * (NM + 1) + (k + 1))
                    nc.vector.tensor_reduce(part_max[:, i, half:half + 1], ps_max[k % 2][:, 0:n], AX.X,
                                            ALU.max).then_inc(max_taken, 1)
                dve.wait_ge(max_taken, (h + 1) * NM)
                nc.vector.tensor_reduce(neg_max[:, :], part_max[:, :, :], AX.X, ALU.max,
                                        negate=True).then_inc(max_folded, 1)
                dve.wait_ge(max_scores, (h + 1) * (NM + 1))
                turned = ps_max[0][0:NT, 0:P]
                if not (isinstance(h, int) and h == 0):
                    dve.wait_ge(m_loaded, h * (16 * PARTS))
                nc.vector.tensor_copy(m_parts[:, 0, :], turned).then_inc(split, 1)
                dve.wait_ge(split, h * 3 + 1)
                nc.vector.tensor_tensor(m_rest[:, :], turned, m_parts[:, 0, :], ALU.subtract).then_inc(split, 1)
                dve.wait_ge(split, h * 3 + 2)
                nc.vector.tensor_copy(m_parts[:, 1, :], m_rest[:, :]).then_inc(split, 1)
                dve.wait_ge(split, h * 3 + 3)
                nc.vector.tensor_tensor(m_parts[:, 2, :], m_rest[:, :], m_parts[:, 1, :],
                                        ALU.subtract).then_inc(m_ready, 1)

            def save(h):
                dve.wait_ge(pv_done, (h + 1) * NT)
                nc.vector.tensor_copy(mem.heads_out[:, bass.ds(h * CH, CH)], ps_out[:, :]).then_inc(out_taken, 1)

            nc.vector.memset(part_max[:], -3.0e38).then_inc(max_cleared, 1)
            dve.wait_ge(max_cleared, 1)
            maxima(0)
            with dve.Fori(0, H - 1) as h:
                maxima(h + 1)
                save(h)
            save(H - 1)


def normalise(nc, mem, name, steps):
    with stage(nc, name) as (ctx, sem):

        summed = sem("summed")
        moments_ready = sem("moments_ready")
        widened = sem("widened")
        rstd_ready = sem("rstd_ready")
        scaled = sem("scaled")
        half_set = sem("half_set")
        block = ctx.enter_context(nc.Block())

        @block.vector
        def _(dve):
            for n, (src, dst) in enumerate(steps):
                if n:
                    dve.wait_ge(scaled, n * NT)
                for i in range(NT):
                    nc.vector.bn_stats(mem.sums[:, i, :], src[:, i, :]).then_inc(summed, 1)
                dve.wait_ge(summed, (n + 1) * NT)
                for i in range(NT):
                    nc.vector.bn_aggr(mem.moments[:, i, :], mem.sums[:, i, :]).then_inc(moments_ready, 1)
                dve.wait_ge(rstd_ready, n + 1)
                for i in range(NT):
                    nc.vector.tensor_scalar(dst[:, i, :], src[:, i, :], mem.moments[:, i, 0:1],
                                            mem.rstd[:, i:i + 1], ALU.subtract, ALU.mult).then_inc(scaled, 1)

        @block.gpsimd
        def _(pool):
            nc.gpsimd.memset(mem.minus_half[:], -0.5).then_inc(half_set, 1)
            pool.wait_ge(half_set, 1)
            for n in range(len(steps)):
                pool.wait_ge(moments_ready, (n + 1) * NT)
                if n:
                    pool.wait_ge(scaled, n * NT)
                nc.gpsimd.tensor_scalar(mem.rstd[:, :], mem.moments[:, :, 1], 1.0, EPS, ALU.mult,
                                        ALU.add).then_inc(widened, 1)
                pool.wait_ge(widened, n + 1)
                nc.gpsimd.tensor_tensor(mem.rstd[:, :], mem.rstd[:, :], mem.minus_half[:, :],
                                        ALU.pow).then_inc(rstd_ready, 1)


def project(nc, mem, name, src, wide, wq, wk, wv, affine=None):
    with stage(nc, name) as (ctx, sem):

        parts = [ctx.enter_context(nc.sbuf_tensor(f"{name}_parts{n}", [P, PARTS, T], BF16)) for n in range(2)]
        rest = ctx.enter_context(nc.sbuf_tensor(f"{name}_rest", [P, T], F32))
        ps = [ctx.enter_context(nc.psum_tensor(f"{name}_ps{b}", [P, CH], F32)) for b in range(8)]
        turned = sem("turned")
        wide_ready = sem("wide_ready")
        product = sem("product")
        first_part = sem("first_part")
        rest_ready = sem("rest_ready")
        second_part = sem("second_part")
        third_part = sem("third_part")
        v_ready = sem("v_ready")
        parts_stored = sem("parts_stored")
        block = ctx.enter_context(nc.Block())

        @block.sync
        def _(sp):
            for n, dram in enumerate((mem.q_parts_dram, mem.k_parts_dram)):
                sp.wait_ge(third_part, NC * (n + 1))
                sp.dma_start(dram.rearrange("g p t -> p g t"), parts[n][:, :, :]).then_inc(parts_stored, 16)
            sp.wait_ge(parts_stored, 32)

        @block.tensor
        def _(pe):
            for c in range(NC):
                for i in range(TPC):
                    mm = nc.tensor.transpose(ps[c][:, i * P:(i + 1) * P], src[:, c * TPC + i, :], mem.ident[:, :])
                mm.then_inc(turned, 1)
            for n, w in enumerate((wq, wk)):
                for c in range(NC):
                    if n == 0:
                        pe.wait_ge(wide_ready, c + 1)
                    if n == 1 and c == 0:
                        pe.wait_ge(wide_ready, NC)
                    nc.tensor.matmul(ps[4 * (1 - n) + c][:, :], w[:, :], wide[:, c * CH:(c + 1) * CH],
                                     start=True, stop=True).then_inc(product, 1)
            for c in range(NC):
                pe.wait_ge(rest_ready, c + 1)
                for i in range(TPC):
                    t = c * TPC + i
                    mm = nc.tensor.matmul(ps[4 + c][:, i * P:(i + 1) * P], wide[:, t * P:(t + 1) * P], wv[:, :],
                                          start=(i == 0), stop=(i == TPC - 1), skip_group_check=True)
                mm.then_inc(product, 1)

        @block.scalar
        def _(act):
            for c in range(NC):
                act.wait_ge(turned, c + 1)
                out = wide[:, c * CH:(c + 1) * CH]
                if affine is None:
                    nc.scalar.activation(out, ps[c][:, :], ACT.Copy).then_inc(wide_ready, 1)
                else:
                    nc.scalar.activation(out, ps[c][:, :], ACT.Identity, bias=affine[1],
                                         scale=affine[0]).then_inc(wide_ready, 1)
            for n in range(2):
                for c in range(NC):
                    act.wait_ge(product, n * NC + c + 1)
                    nc.scalar.activation(parts[n][:, 0, c * CH:(c + 1) * CH], ps[4 * (1 - n) + c][:, :],
                                         ACT.Copy).then_inc(first_part, 1)
                for c in range(NC):
                    act.wait_ge(rest_ready, n * NC + c + 1)
                    nc.scalar.activation(parts[n][:, 1, c * CH:(c + 1) * CH], rest[:, c * CH:(c + 1) * CH],
                                         ACT.Copy).then_inc(second_part, 1)

        @block.vector
        def _(dve):
            for n in range(2):
                for c in range(NC):
                    col = slice(c * CH, (c + 1) * CH)
                    dve.wait_ge(first_part, n * NC + c + 1)
                    if n == 1:
                        dve.wait_ge(third_part, c + 1)
                    nc.vector.tensor_tensor(rest[:, col], ps[4 * (1 - n) + c][:, :], parts[n][:, 0, col],
                                            ALU.subtract).then_inc(rest_ready, 1)
                for c in range(NC):
                    col = slice(c * CH, (c + 1) * CH)
                    dve.wait_ge(second_part, n * NC + c + 1)
                    nc.vector.tensor_tensor(parts[n][:, 2, col], rest[:, col], parts[n][:, 1, col],
                                            ALU.subtract).then_inc(third_part, 1)
            for c in range(NC):
                dve.wait_ge(product, 2 * NC + c + 1)
                nc.vector.tensor_copy(mem.v_tok[:, c * TPC:(c + 1) * TPC, :],
                                      ps[4 + c][:, :].rearrange("p (i d) -> p i d", d=D)).then_inc(v_ready, 1)


def gather_heads(nc, mem, name, out_tok):
    with stage(nc, name) as (ctx, sem):

        inv = ctx.enter_context(nc.sbuf_tensor(f"{name}_inv", [P, 4, NT], F32))
        ps = [ctx.enter_context(nc.psum_tensor(f"{name}_ps{b}", [P, TPC, NC, VW], F32)) for b in range(4)]
        turned = sem("turned")
        inverted = sem("inverted")
        divided = sem("divided")
        block = ctx.enter_context(nc.Block())

        @block.tensor
        def _(pe):
            for h in range(H):
                if h >= 4:
                    pe.wait_ge(divided, h - 3)
                for s in range(TPC):
                    mm = nc.tensor.transpose(ps[h % 4][:, s, :, :].rearrange("p c r -> p (c r)"),
                                             mem.heads_out[:, h * CH + s * P:h * CH + (s + 1) * P], mem.ident[:, :])
                mm.then_inc(turned, 1)

        @block.vector
        def _(dve):
            def divide(h):
                dve.wait_ge(inverted, h + 1)
                nc.vector.tensor_tensor(
                    out_tok[:, :, h * HD:(h + 1) * HD].rearrange("p (c s) d -> p c s d", c=NC),
                    ps[h % 4][:, :, :, 0:HD].rearrange("p s c d -> p c s d"),
                    inv[:, h % 4, :].rearrange("p (c s) -> p c s", c=NC).unsqueeze(3).broadcast_to([P, NC, TPC, HD]),
                    ALU.mult).then_inc(divided, 1)

            for h in range(H):
                dve.wait_ge(turned, h + 1)
                if h >= 4:
                    dve.wait_ge(divided, h - 3)
                nc.vector.reciprocal(inv[:, h % 4, :].rearrange("p (c s) -> p c s", c=NC),
                                     ps[h % 4][:, :, :, HD].rearrange("p s c -> p c s")).then_inc(inverted, 1)
                if h >= 1:
                    divide(h - 1)
            divide(H - 1)


DEPTH = 2
FH = 8
FD = 64
WIN = 64
INNER = FH * FD
HID = int(D * 4 * 2 / 3)
HCH = [(m, min(P, HID - m)) for m in range(0, HID, P)]
QK_SCALE = 8.0
HIDE = -1.0e30
TINY = 1e-24


def rotary_tables():
    half = np.arange(0, FD, 2, dtype=np.float32)
    inv_freq = (1.0 / np.float32(10000.0) ** (half / np.float32(FD))).astype(np.float32)
    t = np.arange(T, dtype=np.float32)
    freqs = (t[:, None] * inv_freq[None, :]).astype(np.float32)
    base = ((half + np.float32(0.4 * FD)) / np.float32(1.4 * FD)).astype(np.float32)
    power = ((t - T // 2) / np.float32(WIN // 2)).astype(np.float32)
    scale = (base[None, :] ** power[:, None]).astype(np.float32)
    cos, sin = np.cos(freqs), np.sin(freqs)
    out = np.empty((2, T, 2, FD), np.float32)
    for n, s in enumerate((scale, 1 / scale)):
        out[0, :, n, :] = np.concatenate([cos * s, cos * s], -1)
        out[1, :, n, :] = np.concatenate([-sin * s, sin * s], -1)
    return out


def window_masks():
    i = np.arange(P)[:, None]
    slot = np.arange(2 * WIN)[None, :]
    hidden = (i % WIN < slot - WIN) | (i % WIN > slot)
    both = np.stack([np.where(hidden | ((i < WIN) & (slot < WIN)), HIDE, 0.0), np.where(hidden, HIDE, 0.0)])
    return (both.astype(np.float32).view(np.uint32) >> 16).astype(np.uint16)


def local_attention(nc, mem, name, layer, src, dst):
    SLOTS = 2 * WIN
    hf, half_d = FD // 2, D // 2
    with stage(nc, name) as (ctx, sem):
        def sb(n, shape, dt=F32):
            return ctx.enter_context(nc.sbuf_tensor(f"{name}_{n}", shape, dt))

        def psum(n, shape):
            return ctx.enter_context(nc.psum_tensor(f"{name}_{n}", shape, F32))

        gains = sb("gains", [P, 2, FD])
        cos = sb("cos", [P, NT, 2, FD])
        sin = sb("sin", [P, NT, 2, FD])
        src_tile = sb("src_tile", [P, D])
        hT = sb("hT", [P, 1 + P])
        minus_half = sb("minus_half", [P, FH])
        squares, norms, inv_norm, straight, turned = ({
            "q": sb(f"{n}_q", shape), "k": sb(f"{n}_k", shape)} for n, shape in (
                ("squares", [P, FH, FD]), ("norms", [P, FH]), ("inv_norm", [P, FH]),
                ("straight", [P, FH, FD]), ("turned", [P, FH, FD])))
        k_normed = sb("k_normed", [P, FH, FD])
        qT = sb("qT", [P, FH // 2, P])
        kT = sb("kT", [P, FH // 2, WIN + P])
        v = sb("v", [P, 2, INNER])
        v_shift = sb("v_shift", [P, 2, INNER])
        neg_top = sb("neg_top", [P, FH])
        neg_max = sb("neg_max", [P, FH])
        sums = sb("sums", [P, FH])
        inv_sum = sb("inv_sum", [P, FH])
        probs = sb("probs", [P, FH, SLOTS])
        pT = sb("pT", [P, FH, P])
        o = sb("o", [P, INNER])
        oT = sb("oT", [P, FH // 2, P])

        ps_q = psum("ps_q", [P, FH, FD])
        ps_k = psum("ps_k", [P, FH, FD])
        ps_v = psum("ps_v", [P, INNER])
        ps_s = psum("ps_s", [P, 2, 4, P])
        ps_kT = psum("ps_kT", [P, FH // 2, P])
        ps_qT = psum("ps_qT", [P, FH // 2, P])
        ps_o = psum("ps_o", [P, INNER])

        gains_loaded = sem("gains_loaded")
        scaled = sem("scaled")
        first_set = sem("first_set")
        src_copied = sem("src_copied")
        src_turned = sem("src_turned")
        carried = sem("carried")
        hT_ready = sem("hT_ready")
        made = {x: sem(f"{x}_made") for x in "kqv"}
        squared = {x: sem(f"{x}_squared") for x in "kq"}
        rotated = {x: sem(f"{x}_rotated") for x in "kq"}
        summed = {x: sem(f"{x}_summed") for x in "kq"}
        norms_ready = {x: sem(f"{x}_norms_ready") for x in "kq"}
        inverted = {x: sem(f"{x}_inverted") for x in "kq"}
        added = {x: sem(f"{x}_added") for x in "kq"}
        k_scaled = sem("k_scaled")
        turned_T = {x: sem(f"{x}_turned_T") for x in "kq"}
        T_ready = {x: sem(f"{x}T_ready") for x in "kq"}
        k_kept = sem("k_kept")
        v_ready = sem("v_ready")
        own_shifted = sem("own_shifted")
        next_shifted = sem("next_shifted")
        scored = sem("scored")
        topped = sem("topped")
        negated = sem("negated")
        exped = sem("exped")
        p_turned = sem("p_turned")
        pT_ready = sem("pT_ready")
        weighed = sem("weighed")
        sum_inverted = sem("sum_inverted")
        divided = sem("divided")
        o_turned = sem("o_turned")
        oT_ready = sem("oT_ready")
        projected = sem("projected")
        result = sem("result")
        h_shifted = sem("h_shifted")
        h_edges = sem("h_edges")
        block = ctx.enter_context(nc.Block())

        def tiles(eng, body):
            body(0, 0, True, False)
            with eng.Fori(0, NT // 2 - 1) as n:
                body(2 * n + 1, 1, False, False)
                body(2 * n + 2, 0, False, False)
            body(NT - 1, 1, False, True)

        head_of = [[2 * j + half for j in range(4)] for half in range(2)]

        def at(x, i):
            return x[:, bass.ds(i, 1), :].squeeze(1)

        @block.sync
        def _(sp):
            for n, x in enumerate(("q_scale", "k_scale")):
                sp.dma_start(gains[:, n, :], mem.gains_dram[x][layer].partition_broadcast(P)
                             ).then_inc(gains_loaded, 16)

            def tile(n, s, first, last):
                if not last:
                    sp.wait_ge(v_ready, n + 1)
                    if not first:
                        sp.wait_ge(weighed, n)
                        sp.wait_ge(next_shifted, n * 16)
                    sp.dma_start(v_shift[0:WIN, 1 - s, :], v[WIN:P, s, :]).then_inc(next_shifted, 16)
                    sp.wait_ge(v_ready, n + 2)
                    sp.wait_ge(own_shifted, n * 16 + 16)
                    sp.dma_start(v_shift[WIN:P, 1 - s, :], v[0:WIN, 1 - s, :]).then_inc(own_shifted, 16)
                if not first:
                    shift_result(n - 1)

            sp.wait_ge(result, 2 * NT)
            sp.dma_start(mem.h[0:1, 1:NT, half_d:D], dst[P - 1:P, 0:NT - 1, half_d:D]).then_inc(h_edges, 16)
            sp.wait_ge(own_shifted, 16 * NT)
            sp.wait_ge(next_shifted, 16 * (NT - 1))
            sp.wait_ge(h_shifted, 16 * NT)
            sp.wait_ge(h_edges, 16)

        @block.gpsimd
        def _(pool):
            def copy_src(n):
                if not isinstance(n, int) or n > 0:
                    pool.wait_ge(src_turned, n)
                nc.gpsimd.tensor_copy(src_tile[:, :], at(src, n)).then_inc(src_copied, 1)

            def work(n, s, first, last):
                pool.wait_ge(rotated["k"], 3 * n + 3)
                nc.gpsimd.tensor_tensor(straight["k"][:, :, :], straight["k"][:, :, :], turned["k"][:, :, :],
                                        ALU.add).then_inc(added["k"], 1)
                if not first:
                    pool.wait_ge(k_scaled, n)
                pool.wait_ge(norms_ready["k"], n + 1)
                nc.gpsimd.tensor_tensor(inv_norm["k"][:, :], norms["k"][:, :], minus_half[:, :],
                                        ALU.pow).then_inc(inverted["k"], 1)
                if not last:
                    copy_src(n + 1)
                pool.wait_ge(rotated["q"], 3 * n + 3)
                nc.gpsimd.tensor_tensor(straight["q"][:, :, :], straight["q"][:, :, :], turned["q"][:, :, :],
                                        ALU.add).then_inc(added["q"], 1)
                if not first:
                    pool.wait_ge(exped, n * FH)
                pool.wait_ge(norms_ready["q"], n + 1)
                nc.gpsimd.tensor_tensor(inv_norm["q"][:, :], norms["q"][:, :], minus_half[:, :],
                                        ALU.pow).then_inc(inverted["q"], 1)

            nc.gpsimd.memset(hT[half_d:P, 0:1], 0.0).then_inc(first_set, 1)
            pool.wait_ge(first_set, 1)
            nc.gpsimd.memset(minus_half[:], -0.5).then_inc(first_set, 1)
            nc.gpsimd.memset(v_shift[0:WIN, 0, :], 0.0).then_inc(first_set, 1)
            nc.gpsimd.memset(mem.h[0:1, 0, half_d:D], 0.0).then_inc(first_set, 1)
            nc.gpsimd.memset(kT[:, :, 0:WIN], 0.0).then_inc(k_kept, 1)
            pool.wait_ge(first_set, 4)
            copy_src(0)
            tiles(pool, work)

        @block.tensor
        def _(pe):
            def turn_src(n):
                pe.wait_ge(src_copied, n + 1)
                if not isinstance(n, int) or n > 0:
                    pe.wait_ge(v_ready, n)
                nc.tensor.transpose(ps_v[:, 0:P], src_tile[:, :], mem.ident[:, :]).then_inc(src_turned, 1)

            def make(x, out):
                col = "qkv".index(x) * INNER
                nc.tensor.matmul(out, hT[:, 0:P], mem.wqkv[:, layer, col:col + INNER], start=True,
                                 stop=True).then_inc(made[x], 1)

            def make_kq(n):
                pe.wait_ge(hT_ready, 2 * n + 2)
                if not isinstance(n, int) or n > 0:
                    pe.wait_ge(rotated["q"], 3 * n)
                make("k", ps_k[:, :, :].rearrange("p h d -> p (h d)"))
                make("q", ps_q[:, :, :].rearrange("p h d -> p (h d)"))

            def turn(x, what, out):
                for j in range(FH // 2):
                    mm = nc.tensor.transpose(out[:, j, :],
                                             what[:, 2 * j:2 * j + 2, :].rearrange("p h d -> p (h d)"),
                                             mem.ident[:, :])
                mm.then_inc(turned_T[x], 1)

            def turn_kq(n, first):
                pe.wait_ge(k_scaled, n + 1)
                turn("k", k_normed, ps_kT)
                if not first:
                    pe.wait_ge(result, 2 * n - 2)
                pe.wait_ge(added["q"], n + 1)
                turn("q", straight["q"], ps_qT)

            def project(n):
                pe.wait_ge(oT_ready, n + 1)
                for j in range(FH // 2):
                    mm = nc.tensor.matmul(ps_qT[:, 0, :], oT[:, j, :], mem.wo[:, layer, j, :], start=(j == 0),
                                          stop=(j == FH // 2 - 1))
                mm.then_inc(projected, 1)

            def turn_o(n):
                pe.wait_ge(divided, n + 1)
                for j in range(FH // 2):
                    mm = nc.tensor.transpose(ps_kT[:, j, :], o[:, j * P:(j + 1) * P], mem.ident[:, :])
                mm.then_inc(o_turned, 1)

            def tile(i, s, first, last):
                if not last:
                    turn_src(i + 1)
                pe.wait_ge(T_ready["k"], i + 1)
                pe.wait_ge(T_ready["q"], i + 1)
                pe.wait_ge(k_kept, i + 1)
                if not first:
                    pe.wait_ge(pT_ready, 2 * i)
                mask = mem.window_masks[:, 0 if first else 1, :].unsqueeze(1).broadcast_to([P, 4, SLOTS])
                for half, heads in enumerate(head_of):
                    r = slice(half * FD, (half + 1) * FD)
                    nc.tensor.matmul(ps_s[:, half, :, :], mem.ident_bf[:, :], mask, start=True, stop=False,
                                     skip_group_check=True)
                    for j in range(4):
                        for w in range(2):
                            q = slice(w * WIN, (w + 1) * WIN)
                            mm = nc.tensor.matmul(ps_s[q, half, j, :], qT[r, j, q],
                                                  kT[r, j, w * WIN:w * WIN + SLOTS], start=False, stop=(j == 3),
                                                  skip_group_check=True)
                    mm.then_inc(scored, 1)
                if not last:
                    make_kq(i + 1)
                if not first:
                    turn_o(i - 1)
                if not last:
                    make("v", ps_v[:, :])
                for half in range(2):
                    pe.wait_ge(exped, i * FH + 4 * half + 4)
                    for j in range(4):
                        mm = nc.tensor.transpose(ps_s[:, half, j, :], probs[:, 4 * half + j, :], mem.ident[:, :])
                    mm.then_inc(p_turned, 1)
                if not first:
                    project(i - 1)
                pe.wait_ge(v_ready, i + 1)
                pe.wait_ge(own_shifted, i * 16 + 16)
                if not first:
                    pe.wait_ge(next_shifted, i * 16)
                pe.wait_ge(pT_ready, 2 * i + 2)
                for hd in range(FH):
                    n = hd % 2 * 4 + hd // 2
                    for w, values in enumerate((v_shift, v)):
                        q = slice(w * WIN, (w + 1) * WIN)
                        mm = nc.tensor.matmul(ps_o[q, hd * FD:(hd + 1) * FD], pT[:, n, q],
                                              values[:, s, hd * FD:(hd + 1) * FD],
                                              start=(hd == 0), stop=(hd == FH - 1), skip_group_check=True)
                mm.then_inc(weighed, 1)
                if not last:
                    turn_kq(i + 1, first)

            pe.wait_ge(first_set, 4)
            turn_src(0)
            make_kq(0)
            make("v", ps_v[:, :])
            turn_kq(0, True)
            tiles(pe, tile)
            turn_o(NT - 1)
            project(NT - 1)

        @block.scalar
        def _(act):
            def copy(out, src, done):
                nc.scalar.activation(out, src, ACT.Copy).then_inc(done, 1)

            def keep_hT(n):
                act.wait_ge(src_turned, n + 1)
                if not isinstance(n, int) or n > 0:
                    copy(hT[half_d:P, 0:1], hT[half_d:P, P:P + 1], carried)
                copy(hT[0:half_d, 0:P], ps_v[0:half_d, 0:P], hT_ready)
                if not isinstance(n, int) or n > 0:
                    act.wait_ge(carried, n)
                copy(hT[half_d:P, 1:P + 1], ps_v[half_d:P, 0:P], hT_ready)

            def square(x, n):
                act.wait_ge(made[x], n + 1)
                if not isinstance(n, int) or n > 0:
                    act.wait_ge(summed[x], n)
                nc.scalar.activation(squares[x][:, :, :], (ps_k if x == "k" else ps_q)[:, :, :],
                                     ACT.Square).then_inc(squared[x], 1)

            def keep_v(n, s):
                act.wait_ge(made["v"], n + 1)
                if not isinstance(n, int):
                    act.wait_ge(weighed, n - 1)
                    act.wait_ge(own_shifted, 16 * n)
                    act.wait_ge(next_shifted, 16 * n - 16)
                copy(v[:, s, :], ps_v[:, :], v_ready)

            def shift_own(n, s):
                if not isinstance(n, int) or n > 0:
                    act.wait_ge(own_shifted, 16 * n)
                act.wait_ge(v_ready, n + 1)
                act.dma_start(v_shift[WIN:P, s, :], v[0:WIN, s, :]).then_inc(own_shifted, 16)

            def shift_next(n, s):
                if not isinstance(n, int) or n > 0:
                    act.wait_ge(next_shifted, 16 * n)
                act.dma_start(v_shift[0:WIN, 1 - s, :], v[WIN:P, s, :]).then_inc(next_shifted, 16)

            def shift_result(n):
                act.wait_ge(result, 2 * n + 2)
                if not isinstance(n, int) or n > 0:
                    act.wait_ge(h_shifted, 16 * n)
                act.dma_start(mem.h[1:P, bass.ds(n, 1), half_d:D],
                              dst[0:P - 1, bass.ds(n, 1), half_d:D]).then_inc(h_shifted, 16)

            def keep_kq(n):
                act.wait_ge(turned_T["k"], n + 1)
                act.wait_ge(k_kept, n + 1)
                copy(kT[:, :, WIN:WIN + P], ps_kT[:, :, :], T_ready["k"])
                act.wait_ge(turned_T["q"], n + 1)
                copy(qT[:, :, :], ps_qT[:, :, :], T_ready["q"])

            def tile(i, s, first, last):
                if not last:
                    keep_hT(i + 1)
                if not first:
                    act.wait_ge(sum_inverted, i)
                for half, heads in enumerate(head_of):
                    act.wait_ge(negated, 2 * i + half + 1)
                    for j, hd in enumerate(heads):
                        n = 4 * half + j
                        nc.scalar.activation(probs[:, n, :], ps_s[:, half, j, :], ACT.Exp, bias=neg_max[:, n:n + 1],
                                             scale=inv_norm["q"][:, hd:hd + 1],
                                             accum_out=sums[:, n:n + 1]).then_inc(exped, 1)
                    if not last:
                        square("kq"[half], i + 1)
                if not first:
                    act.wait_ge(o_turned, i)
                    copy(oT[:, :, :], ps_kT[:, :, :], oT_ready)
                if not last:
                    keep_v(i + 1, 1 - s)
                for half in range(2):
                    act.wait_ge(p_turned, 2 * i + half + 1)
                    copy(pT[:, 4 * half:4 * half + 4, :], ps_s[:, half, :, :], pT_ready)
                if not last:
                    shift_own(i + 1, 1 - s)
                    shift_next(i, s)
                if not first:
                    shift_result(i - 1)
                if not last:
                    keep_kq(i + 1)

            act.wait_ge(first_set, 4)
            keep_hT(0)
            square("k", 0)
            square("q", 0)
            keep_v(0, 0)
            shift_own(0, 0)
            keep_kq(0)
            tiles(act, tile)
            act.wait_ge(o_turned, NT)
            copy(oT[:, :, :], ps_kT[:, :, :], oT_ready)
            shift_result(NT - 1)

        @block.vector
        def _(dve):
            def rotate(x, n):
                which, ps = "qk".index(x), (ps_k if x == "k" else ps_q)
                dve.wait_ge(squared[x], n + 1)
                if x == "q" and (not isinstance(n, int) or n > 0):
                    dve.wait_ge(turned_T["q"], n)
                nc.vector.tensor_tensor(straight[x][:, :, :], ps[:, :, :],
                                        cos[:, bass.ds(n, 1), which, :].broadcast_to([P, FH, FD]),
                                        ALU.mult).then_inc(rotated[x], 1)
                for half in range(2):
                    d = slice(half * hf, (half + 1) * hf)
                    partner = slice((1 - half) * hf, (2 - half) * hf)
                    nc.vector.tensor_tensor(turned[x][:, :, d], ps[:, :, partner],
                                            sin[:, bass.ds(n, 1), which, d].broadcast_to([P, FH, hf]),
                                            ALU.mult).then_inc(rotated[x], 1)

            def norm(x, n):
                nc.vector.tensor_reduce(norms[x][:, :], squares[x][:, :, :], AX.X, ALU.add).then_inc(summed[x], 1)
                dve.wait_ge(summed[x], n + 1)
                nc.vector.tensor_scalar(norms[x][:, :], norms[x][:, :], TINY, None,
                                        ALU.max).then_inc(norms_ready[x], 1)

            def make(n):
                rotate("k", n)
                norm("k", n)
                rotate("q", n)
                norm("q", n)
                dve.wait_ge(inverted["k"], n + 1)
                dve.wait_ge(added["k"], n + 1)
                if not isinstance(n, int) or n > 0:
                    dve.wait_ge(turned_T["k"], n)
                nc.vector.tensor_tensor(k_normed[:, :, :], straight["k"][:, :, :],
                                        inv_norm["k"][:, :].unsqueeze(2).broadcast_to([P, FH, FD]),
                                        ALU.mult).then_inc(k_scaled, 1)

            def add(n):
                dve.wait_ge(projected, n + 1)
                nc.vector.tensor_tensor(mem.h[:, bass.ds(n, 1), 0:half_d].squeeze(1), ps_qT[:, 0, 0:half_d],
                                        src[:, bass.ds(n, 1), 0:half_d].squeeze(1), ALU.add).then_inc(result, 1)
                if src is dst:
                    dve.wait_ge(result, 2 * n + 1)
                nc.vector.tensor_tensor(at(dst, n), ps_qT[:, 0, :], at(src, n), ALU.add).then_inc(result, 1)

            def tile(i, s, first, last):
                for half in range(2):
                    four = slice(4 * half, 4 * half + 4)
                    dve.wait_ge(scored, 2 * i + half + 1)
                    nc.vector.tensor_reduce(neg_top[:, four], ps_s[:, half, :, :], AX.X, ALU.max,
                                            negate=True).then_inc(topped, 1)
                    dve.wait_ge(inverted["q"], i + 1)
                    dve.wait_ge(topped, 2 * i + half + 1)
                    nc.vector.tensor_tensor(
                        neg_max[:, four], neg_top[:, four],
                        inv_norm["q"][:, :].rearrange("p (j b) -> p b j", b=2)[:, half, :],
                        ALU.mult).then_inc(negated, 1)
                if not last:
                    nc.vector.tensor_copy(kT[:, :, 0:WIN], kT[:, :, P:P + WIN]).then_inc(k_kept, 1)
                    make(i + 1)
                if not first:
                    add(i - 1)
                dve.wait_ge(exped, i * FH + FH)
                nc.vector.reciprocal(inv_sum[:, :], sums[:, :]).then_inc(sum_inverted, 1)
                dve.wait_ge(sum_inverted, i + 1)
                dve.wait_ge(weighed, i + 1)
                if not first:
                    dve.wait_ge(o_turned, i)
                nc.vector.tensor_tensor(
                    o[:, :].rearrange("p (j b d) -> p j b d", b=2, d=FD),
                    ps_o[:, :].rearrange("p (j b d) -> p j b d", b=2, d=FD),
                    inv_sum[:, :].rearrange("p (b j) -> p j b", b=2).unsqueeze(3).broadcast_to([P, 4, 2, FD]),
                    ALU.mult).then_inc(divided, 1)

            dve.wait_ge(gains_loaded, 32)
            nc.vector.tensor_scalar(gains[:, 0, :], gains[:, 0, :], QK_SCALE, None, ALU.mult).then_inc(scaled, 1)
            dve.wait_ge(scaled, 1)
            nc.vector.tensor_tensor(cos[:, :, :, :], mem.rot_cos[:, :, :, :],
                                    gains[:, :, :].unsqueeze(1).broadcast_to([P, NT, 2, FD]),
                                    ALU.mult).then_inc(scaled, 1)
            for half in range(2):
                d = slice(half * hf, (half + 1) * hf)
                partner = slice((1 - half) * hf, (2 - half) * hf)
                nc.vector.tensor_tensor(sin[:, :, :, d], mem.rot_sin[:, :, :, d],
                                        gains[:, :, partner].unsqueeze(1).broadcast_to([P, NT, 2, hf]),
                                        ALU.mult).then_inc(scaled, 1)
            dve.wait_ge(scaled, 4)
            make(0)
            tiles(dve, tile)
            add(NT - 1)


def feed_forward(nc, mem, name, layer, dst):
    NH = len(HCH)
    with stage(nc, name) as (ctx, sem):
        def sb(n, shape, dt=F32):
            return ctx.enter_context(nc.sbuf_tensor(f"{name}_{n}", shape, dt))


        hT = sb("hT", [P, 2, CH])
        gate = sb("gate", [P, NH, CH])
        hidden = sb("hidden", [P, 2, NH, CH])
        ps = [ctx.enter_context(nc.psum_tensor(f"{name}_ps{b}", [P, CH], F32)) for b in range(8)]
        ps_a, ps_g, ps_t, ps_y = ps[0:NH], ps[NH:2 * NH], ps[6], ps[7]
        turned = sem("turned")
        hT_ready = sem("hT_ready")
        biased = sem("biased")
        widened = sem("widened")
        gated = sem("gated")
        hidden_ready = sem("hidden_ready")
        narrowed = sem("narrowed")
        result = sem("result")
        block = ctx.enter_context(nc.Block())

        @block.gpsimd
        def _(pool):
            for c in range(NC):
                t = slice(c * TPC, (c + 1) * TPC)
                nc.gpsimd.tensor_tensor(dst[:, t, :], dst[:, t, :],
                                        mem.b2[:, layer, :].unsqueeze(1).broadcast_to([P, TPC, D]),
                                        ALU.add).then_inc(biased, 1)

        @block.tensor
        def _(pe):
            def turn(c):
                if c:
                    pe.wait_ge(hT_ready, c)
                for i in range(TPC):
                    mm = nc.tensor.transpose(ps_t[:, i * P:(i + 1) * P], mem.h[:, c * TPC + i, :], mem.ident[:, :])
                mm.then_inc(turned, 1)

            def narrow(c):
                pe.wait_ge(hidden_ready, NH * (c + 1))
                if c:
                    pe.wait_ge(result, c)
                for i in range(TPC):
                    for m, (_, n) in enumerate(HCH):
                        mm = nc.tensor.matmul(ps_y[:, i * P:(i + 1) * P], hidden[0:n, c % 2, m, i * P:(i + 1) * P],
                                              mem.w2[0:n, layer, m, :], start=(i == 0 and m == 0),
                                              stop=(m == NH - 1), skip_group_check=True)
                mm.then_inc(narrowed, 1)

            turn(0)
            for c in range(NC):
                pe.wait_ge(hT_ready, c + 1)
                for m, (h0, n) in enumerate(HCH):
                    if c:
                        pe.wait_ge(hidden_ready, NH * (c - 1) + m + 1)
                    for half, bank in ((1, ps_g[m]), (0, ps_a[m])):
                        mm = nc.tensor.matmul(bank[0:n, :], mem.w1[:, layer, half * HID + h0:half * HID + h0 + n],
                                              hT[:, c % 2, :], start=True, stop=True)
                    mm.then_inc(widened, 1)
                if c + 1 < NC:
                    turn(c + 1)
                if c:
                    narrow(c - 1)
            narrow(NC - 1)

        @block.scalar
        def _(act):
            def turn(c):
                act.wait_ge(turned, c + 1)
                if c >= 2:
                    act.wait_ge(widened, NH * (c - 1))
                nc.scalar.activation(hT[:, c % 2, :], ps_t[:, :], ACT.Identity, bias=mem.ln[:, layer, 1:2],
                                     scale=mem.ln[:, layer, 0:1]).then_inc(hT_ready, 1)
            turn(0)
            for c in range(NC):
                for m, (h0, n) in enumerate(HCH):
                    act.wait_ge(widened, NH * c + m + 1)
                    if c:
                        act.wait_ge(hidden_ready, NH * (c - 1) + m + 1)
                    nc.scalar.activation(gate[0:n, m, :], ps_g[m][0:n, :], ACT.Gelu,
                                         bias=mem.b1[0:n, layer, 1, m:m + 1]).then_inc(gated, 1)
                if c + 1 < NC:
                    turn(c + 1)

        @block.vector
        def _(dve):
            def add(c):
                t = slice(c * TPC, (c + 1) * TPC)
                dve.wait_ge(biased, c + 1)
                dve.wait_ge(narrowed, c + 1)
                nc.vector.tensor_tensor(dst[:, t, :], dst[:, t, :], ps_y[:, :].rearrange("p (i d) -> p i d", d=D),
                                        ALU.add).then_inc(result, 1)
            for c in range(NC):
                for m, (h0, n) in enumerate(HCH):
                    dve.wait_ge(gated, NH * c + m + 1)
                    if c >= 2:
                        dve.wait_ge(narrowed, c - 1)
                    nc.vector.scalar_tensor_tensor(out=hidden[0:n, c % 2, m, :], in0=ps_a[m][0:n, :],
                                                   scalar=mem.b1[0:n, layer, 0, m:m + 1], in1=gate[0:n, m, :],
                                                   op0=ALU.add, op1=ALU.mult).then_inc(hidden_ready, 1)
                if c:
                    add(c - 1)
            add(NC - 1)


def linear_out(nc, mem, name, src, w, dst, add):
    with stage(nc, name) as (ctx, sem):

        wide = ctx.enter_context(nc.sbuf_tensor(f"{name}_wide", [P, T], F32))
        ps = [ctx.enter_context(nc.psum_tensor(f"{name}_ps{b}", [P, CH], F32)) for b in range(8)]
        turned = sem("turned")
        wide_ready = sem("wide_ready")
        product = sem("product")
        result = sem("result")
        block = ctx.enter_context(nc.Block())

        @block.tensor
        def _(pe):
            for c in range(NC):
                for i in range(TPC):
                    mm = nc.tensor.transpose(ps[c][:, i * P:(i + 1) * P], src[:, c * TPC + i, :], mem.ident[:, :])
                mm.then_inc(turned, 1)
            for c in range(NC):
                pe.wait_ge(wide_ready, c + 1)
                for i in range(TPC):
                    t = c * TPC + i
                    mm = nc.tensor.matmul(ps[4 + c][:, i * P:(i + 1) * P], wide[:, t * P:(t + 1) * P], w[:, :],
                                          start=(i == 0), stop=(i == TPC - 1), skip_group_check=True)
                mm.then_inc(product, 1)

        @block.scalar
        def _(act):
            for c in range(NC):
                act.wait_ge(turned, c + 1)
                nc.scalar.activation(wide[:, c * CH:(c + 1) * CH], ps[c][:, :], ACT.Copy).then_inc(wide_ready, 1)

        @block.vector
        def _(dve):
            for c in range(NC):
                t = slice(c * TPC, (c + 1) * TPC)
                y = ps[4 + c][:, :].rearrange("p (i d) -> p i d", d=D)
                dve.wait_ge(product, c + 1)
                if add:
                    nc.vector.tensor_tensor(dst[:, t, :], dst[:, t, :], y, ALU.add).then_inc(result, 1)
                else:
                    nc.vector.tensor_copy(dst[:, t, :], y).then_inc(result, 1)


def gate_residual(nc, mem, name, f, s, x):
    with stage(nc, name) as (ctx, sem):
        gated = sem("gated")
        product = sem("product")
        result = sem("result")
        block = ctx.enter_context(nc.Block())

        @block.scalar
        def _(act):
            for c in range(NC):
                t = slice(c * TPC, (c + 1) * TPC)
                nc.scalar.activation(f[:, t, :], f[:, t, :], ACT.Silu).then_inc(gated, 1)

        @block.vector
        def _(dve):
            for c in range(NC):
                t = slice(c * TPC, (c + 1) * TPC)
                dve.wait_ge(gated, c + 1)
                nc.vector.tensor_tensor(s[:, t, :], s[:, t, :], f[:, t, :], ALU.mult).then_inc(product, 1)
                dve.wait_ge(product, c + 1)
                nc.vector.tensor_tensor(x[:, t, :], x[:, t, :], s[:, t, :], ALU.add).then_inc(result, 1)


E = 8
TOP = 2
EH = 4 * D // E
PAIRS = E // 2
GROUPS = PAIRS + 1


def experts(nc, mem, a, name, wide, s, x, out):
    with stage(nc, name) as (ctx, sem):
        def sb(n, shape, dt=F32):
            return ctx.enter_context(nc.sbuf_tensor(f"{name}_{n}", shape, dt))

        def psum(n, shape):
            return ctx.enter_context(nc.psum_tensor(f"{name}_{n}", shape, F32))


        w_route = sb("w_route", [P, E])
        route_bias = sb("route_bias", [P, E])
        w_in = sb("w_in", [P, GROUPS, 2, EH])
        b_in = sb("b_in", [P, GROUPS])
        w_out = sb("w_out", [P, GROUPS, D])
        b_out = sb("b_out", [E + 1, D])
        lower = sb("lower", [P, E, E])
        spread = sb("spread", [E, PAIRS, P])
        logits = sb("logits", [P, NT, E])
        size = sb("size", [P, NT, E])
        one_plus = sb("one_plus", [P, NT, E])
        over = sb("over", [P, NT, E])
        exact = sb("exact", [P, NT, E])
        log_term = sb("log_term", [P, NT, E])
        half = sb("half", [P, NT, E])
        value = sb("value", [P, NT, E])
        above = sb("above", [P, NT, E, E])
        level = sb("level", [P, NT, E, E])
        rank = sb("rank", [P, NT, E])
        weight = sb("weight", [P, NT, E + 1])
        weightT = sb("weightT", [E + 1, T])
        hidden = sb("hidden", [P, 2, GROUPS, CH])
        gate = sb("gate", [P, 2, CH])

        ps_r = psum("ps_r", [P, CH])
        ps_t = psum("ps_t", [E + 1, CH])
        ps_h = [psum(f"ps_h{b}", [P, CH]) for b in range(2)]
        ps_w = [psum(f"ps_w{b}", [P, CH]) for b in range(2)]
        ps_y = [psum(f"ps_y{b}", [P, CH]) for b in range(2)]

        loaded = sem("loaded")
        set_up = sem("set_up")
        routed = sem("routed")
        step = sem("step")
        exped = sem("exped")
        rooted = sem("rooted")
        weighed = sem("weighed")
        w_turned = sem("w_turned")
        weightT_ready = sem("weightT_ready")
        hid_made = sem("hid_made")
        activated = sem("activated")
        spread_made = sem("spread_made")
        hid_weighed = sem("hid_weighed")
        mixed = sem("mixed")
        gated = sem("gated")
        multiplied = sem("multiplied")
        result = sem("result")
        stored = sem("stored")
        block = ctx.enter_context(nc.Block())
        N_LOADS = 14

        @block.sync
        def _(sp):
            pairs = a["rW1"].rearrange("(g o) d h -> d g o h", o=2)
            loads = [
                (w_route[:, :], a["w_route"]),
                (route_bias[:, :], a["expert_bias"].partition_broadcast(P)),
                (lower[:, :, :], a["lower"].partition_broadcast(P)),
                (spread[:, :, :], a["spread"]),
                (w_in[:, PAIRS, 0, :], a["sW1"]),
                (b_in[0:EH, PAIRS:GROUPS], a["sb1"].unsqueeze(1)),
                (b_in[:, 0:PAIRS], a["rb1"]),
                (w_out[:, 0:PAIRS, :], a["rW2"]),
                (w_out[0:EH, PAIRS, :], a["sW2"]),
                (b_out[0:E, :], a["rb2"]),
                (b_out[E:E + 1, :], a["sb2"].unsqueeze(0)),
            ] + [(w_in[:, g, :, :], pairs[:, g, :, :]) for g in range(PAIRS)]
            assert len(loads) == N_LOADS + 1
            for dst, src in loads:
                sp.dma_start(dst, src).then_inc(loaded, 16)
            for c in range(NC):
                sp.wait_ge(result, c + 1)
                sp.dma_start(tiles_of(out)[:, c * TPC:(c + 1) * TPC, :],
                             x[:, c * TPC:(c + 1) * TPC, :]).then_inc(stored, 16)
            sp.wait_ge(stored, 16 * NC)

        @block.gpsimd
        def _(pool):
            nc.gpsimd.memset(half[:], 0.5).then_inc(set_up, 1)
            nc.gpsimd.memset(weight[:, :, E:E + 1], 1.0).then_inc(set_up, 1)
            pool.wait_ge(set_up, 2)
            pool.wait_ge(step, 10)
            nc.gpsimd.tensor_tensor(value[:, :, :], log_term[:, :, :], half[:, :, :], ALU.pow).then_inc(rooted, 1)

        @block.tensor
        def _(pe):
            pe.wait_ge(loaded, 16 * (N_LOADS + 1))
            for i in range(NT):
                mm = nc.tensor.matmul(ps_r[:, i * E:(i + 1) * E], wide[:, i * P:(i + 1) * P], w_route[:, :],
                                      start=(i == 0), stop=(i == NT - 1), skip_group_check=True)
            mm.then_inc(routed, 1)
            pe.wait_ge(weighed, 1)
            pe.wait_ge(set_up, 2)
            for c in range(NC):
                if c:
                    pe.wait_ge(weightT_ready, c)
                for i in range(TPC):
                    mm = nc.tensor.transpose(ps_t[:, i * P:(i + 1) * P], weight[:, c * TPC + i, :], mem.ident[:, :])
                mm.then_inc(w_turned, 1)

            def mix(c):
                pe.wait_ge(activated, GROUPS * (c + 1))
                pe.wait_ge(hid_weighed, PAIRS * (c + 1))
                if c >= 2:
                    pe.wait_ge(gated, c - 1)
                for i in range(TPC):
                    col = slice(i * P, (i + 1) * P)
                    for g in range(GROUPS):
                        k = P if g < PAIRS else EH
                        nc.tensor.matmul(ps_y[c % 2][:, col], hidden[0:k, c % 2, g, col], w_out[0:k, g, :],
                                         start=(i == 0 and g == 0), stop=False, skip_group_check=True)
                    mm = nc.tensor.matmul(ps_y[c % 2][:, col], weightT[:, c * CH + i * P:c * CH + (i + 1) * P],
                                          b_out[:, :], start=False, stop=True, skip_group_check=True)
                mm.then_inc(mixed, 1)

            for c in range(NC):
                for g in range(GROUPS):
                    k = P if g < PAIRS else EH
                    n, p = c * GROUPS + g, c * PAIRS + g
                    if n >= 2:
                        pe.wait_ge(activated, n - 1)
                    nc.tensor.matmul(ps_h[n % 2][0:k, :],
                                     w_in[:, g, :, :].rearrange("p o h -> p (o h)")[:, 0:k],
                                     wide[:, c * CH:(c + 1) * CH], start=True, stop=True).then_inc(hid_made, 1)
                    if g < PAIRS:
                        pe.wait_ge(weightT_ready, c + 1)
                        if p >= 2:
                            pe.wait_ge(hid_weighed, p - 1)
                        nc.tensor.matmul(ps_w[p % 2][:, :], spread[:, g, :], weightT[0:E, c * CH:(c + 1) * CH],
                                         start=True, stop=True).then_inc(spread_made, 1)
                if c:
                    mix(c - 1)
            mix(NC - 1)

        @block.scalar
        def _(act):
            act.wait_ge(step, 1)
            nc.scalar.activation(size[:, :, :], logits[:, :, :], ACT.Abs).then_inc(exped, 1)
            act.wait_ge(exped, 1)
            nc.scalar.activation(size[:, :, :], size[:, :, :], ACT.Exp, scale=-1.0).then_inc(exped, 1)
            act.wait_ge(step, 2)
            nc.scalar.activation(log_term[:, :, :], one_plus[:, :, :], ACT.Ln).then_inc(exped, 1)
            for c in range(NC):
                act.wait_ge(w_turned, c + 1)
                nc.scalar.activation(weightT[:, c * CH:(c + 1) * CH], ps_t[:, :], ACT.Copy).then_inc(weightT_ready, 1)

            def open_gate(c):
                act.wait_ge(mixed, c + 1)
                if c >= 2:
                    act.wait_ge(multiplied, c - 1)
                nc.scalar.activation(gate[:, c % 2, :], ps_y[c % 2][:, :], ACT.Silu).then_inc(gated, 1)

            for c in range(NC):
                if c >= 2:
                    act.wait_ge(mixed, c - 1)
                for g in range(GROUPS):
                    k = P if g < PAIRS else EH
                    n = c * GROUPS + g
                    act.wait_ge(hid_made, n + 1)
                    nc.scalar.activation(hidden[0:k, c % 2, g, :], ps_h[n % 2][0:k, :], ACT.Silu,
                                         bias=b_in[0:k, g:g + 1]).then_inc(activated, 1)
                if c:
                    open_gate(c - 1)
            open_gate(NC - 1)

        @block.vector
        def _(dve):
            done = [0]

            def link(ins):
                done[0] += 1
                ins.then_inc(step, 1)
                dve.wait_ge(step, done[0])

            dve.wait_ge(routed, 1)
            dve.wait_ge(loaded, 16 * (N_LOADS + 1))
            link(nc.vector.tensor_tensor(logits[:, :, :], ps_r[:, 0:NT * E].rearrange("p (i e) -> p i e", e=E),
                                         route_bias[:, :].unsqueeze(1).broadcast_to([P, NT, E]), ALU.add))
            dve.wait_ge(exped, 2)
            link(nc.vector.tensor_scalar(one_plus[:, :, :], size[:, :, :], 1.0, None, ALU.add))
            link(nc.vector.tensor_scalar(over[:, :, :], one_plus[:, :, :], 1.0, None, ALU.subtract))
            link(nc.vector.tensor_scalar(exact[:, :, :], over[:, :, :], 0.0, None, ALU.is_equal))
            link(nc.vector.tensor_tensor(over[:, :, :], over[:, :, :], exact[:, :, :], ALU.add))
            link(nc.vector.reciprocal(over[:, :, :], over[:, :, :]))
            dve.wait_ge(exped, 3)
            link(nc.vector.tensor_tensor(over[:, :, :], over[:, :, :], log_term[:, :, :], ALU.mult))
            link(nc.vector.tensor_tensor(over[:, :, :], over[:, :, :], exact[:, :, :], ALU.add))
            link(nc.vector.tensor_tensor(over[:, :, :], over[:, :, :], size[:, :, :], ALU.mult))
            link(nc.vector.scalar_tensor_tensor(out=log_term[:, :, :], in0=logits[:, :, :], scalar=0.0,
                                                in1=over[:, :, :], op0=ALU.max, op1=ALU.add))
            dve.wait_ge(rooted, 1)
            mine = value[:, :, :].unsqueeze(3).broadcast_to([P, NT, E, E])
            other = value[:, :, :].unsqueeze(2).broadcast_to([P, NT, E, E])
            link(nc.vector.tensor_tensor(above[:, :, :, :], other, mine, ALU.is_gt))
            link(nc.vector.tensor_tensor(level[:, :, :, :], other, mine, ALU.is_equal))
            link(nc.vector.tensor_tensor(level[:, :, :, :], level[:, :, :, :],
                                         lower[:, :, :].unsqueeze(1).broadcast_to([P, NT, E, E]), ALU.mult))
            link(nc.vector.tensor_tensor(above[:, :, :, :], above[:, :, :, :], level[:, :, :, :], ALU.add))
            link(nc.vector.tensor_reduce(rank[:, :, :], above[:, :, :, :], AX.X, ALU.add))
            nc.vector.scalar_tensor_tensor(out=weight[:, :, 0:E], in0=rank[:, :, :], scalar=float(TOP),
                                           in1=value[:, :, :], op0=ALU.is_lt, op1=ALU.mult).then_inc(weighed, 1)

            def finish(c):
                t = slice(c * TPC, (c + 1) * TPC)
                dve.wait_ge(gated, c + 1)
                nc.vector.tensor_tensor(s[:, t, :], s[:, t, :], gate[:, c % 2, :].rearrange("p (i d) -> p i d", d=D),
                                        ALU.mult).then_inc(multiplied, 1)
                dve.wait_ge(multiplied, c + 1)
                nc.vector.tensor_tensor(x[:, t, :], x[:, t, :], s[:, t, :], ALU.add).then_inc(result, 1)

            for c in range(NC):
                for g in range(PAIRS):
                    n, p = c * GROUPS + g, c * PAIRS + g
                    dve.wait_ge(activated, n + 1)
                    dve.wait_ge(spread_made, p + 1)
                    nc.vector.tensor_tensor(hidden[:, c % 2, g, :], hidden[:, c % 2, g, :], ps_w[p % 2][:, :],
                                            ALU.mult).then_inc(hid_weighed, 1)
                if c:
                    finish(c - 1)
            finish(NC - 1)


def constants():
    later = np.arange(P)[None, :] > np.arange(P)[:, None]
    spread = np.zeros((E, PAIRS, 2, EH), np.float32)
    for e in range(E):
        spread[e, e // 2, e % 2, :] = 1.0
    return {
        "ident": np.eye(P, dtype=np.float32),
        "masks": np.stack([np.eye(P), np.where(later, NEG, 0.0), np.where(later.T, NEG, 0.0)]).astype(np.float32),
        "rotary": rotary_tables(),
        "window_masks": window_masks(),
        "lower": np.tril(np.ones((E, E), np.float32), -1),
        "spread": spread.reshape(E, PAIRS, P),
        "fill": np.stack([np.full((MROW - ROWS, T), bits, np.uint16) for bits in (0, 0x3F80)]),
    }


def layout(inputs):
    g = lambda n: np.asarray(inputs[n])
    arrays = {
        "x": g("L0_attn_z").reshape(T, D),
        "ln_scale0": g("L0_attn_ln_scale"),
        "ln_bias0": g("L0_attn_ln_bias"),
        "w_qkv0": g("L0_attn_w_qkv").reshape(D, D, 3).transpose(2, 0, 1),
        "w_proj0": g("L0_attn_w_proj"),
        "b_proj0": g("L0_attn_b_proj"),
        "w_qkv1": g("L1_attn_w_qkv").reshape(3, D, D).transpose(0, 2, 1),
        "w_out1": g("L1_attn_w_out").T,
        "w_route": g("L1_ffn_routing_W").T,
        "expert_bias": g("L1_ffn_expert_bias"),
        "sW1": g("L1_ffn_sW1"), "sb1": g("L1_ffn_sb1"), "sW2": g("L1_ffn_sW2"), "sb2": g("L1_ffn_sb2"),
        "rW1": g("L1_ffn_rW1"),
        "rb1": g("L1_ffn_rb1").reshape(PAIRS, P).T,
        "rW2": g("L1_ffn_rW2").reshape(PAIRS, P, D).transpose(1, 0, 2),
        "rb2": g("L1_ffn_rb2"),
    }
    for n in ("wqkv", "q_scale", "k_scale", "wo", "ln_g", "ln_b", "w1", "b1", "w2", "b2"):
        arrays[n] = g("L0_ffn_" + n)
    arrays.update(constants())
    return {k: np.ascontiguousarray(v) for k, v in arrays.items()}


def load(nc, name, *pairs):
    with stage(nc, name) as (ctx, sem):
        loaded = sem("loaded")
        block = ctx.enter_context(nc.Block())

        @block.sync
        def _(sp):
            for dst, src in pairs:
                sp.dma_start(dst, src).then_inc(loaded, 16)
            sp.wait_ge(loaded, 16 * len(pairs))


def add_bias(nc, name, src, bias, dst):
    with stage(nc, name) as (ctx, sem):
        added = sem("added")
        block = ctx.enter_context(nc.Block())

        @block.vector
        def _(dve):
            nc.vector.tensor_tensor(dst[:, :, :], src[:, :, :], bias[:, :].unsqueeze(1).broadcast_to([P, NT, D]),
                                    ALU.add).then_inc(added, 1)


def gate_layers(nc, mem, a, xn, f):
    with ExitStack() as s1:
        u = lambda n, shape, dt=F32: s1.enter_context(nc.sbuf_tensor(n, shape, dt))
        mem.h = u("h", [P, NT, D])
        mem.rot_cos = u("rot_cos", [P, NT, 2, FD])
        mem.rot_sin = u("rot_sin", [P, NT, 2, FD])
        mem.window_masks = u("window_masks_sb", [P, 2, 2 * WIN], BF16)
        mem.wqkv = u("wqkv", [P, DEPTH, 3 * INNER])
        mem.wo = u("wo", [P, DEPTH, INNER // P, D])
        mem.w1 = u("w1", [P, DEPTH, 2 * HID])
        mem.w2 = u("w2", [P, DEPTH, len(HCH), D])
        mem.b1 = u("b1", [P, DEPTH, 2, len(HCH)])
        mem.b2 = u("b2", [P, DEPTH, D])
        mem.ln = u("ln", [P, DEPTH, 2])
        mem.gains_dram = a
        pairs = [
            (mem.window_masks[:, :, :], a["window_masks"].bitcast(BF16).rearrange("m p q -> p m q")),
            (mem.wqkv[:, :, :], a["wqkv"].rearrange("l p n -> p l n")),
            (mem.rot_cos[:, :, :, :], a["rotary"][0].rearrange("(i p) n d -> p i n d", p=P)),
            (mem.rot_sin[:, :, :, :], a["rotary"][1].rearrange("(i p) n d -> p i n d", p=P)),
            (mem.w1[:, :, :], a["w1"].rearrange("l p n -> p l n")),
            (mem.b2[:, :, :], a["b2"].partition_broadcast(P)),
        ]
        for layer in range(DEPTH):
            for n, x in enumerate(("ln_g", "ln_b")):
                pairs.append((mem.ln[:, layer, n:n + 1], a[x][layer].unsqueeze(1)))
            pairs.append((mem.wo[:, layer, :, :], a["wo"][layer].rearrange("(j p) n -> p j n", p=P)))
            for m, (h0, n) in enumerate(HCH):
                pairs.append((mem.w2[0:n, layer, m, :], a["w2"][layer][h0:h0 + n, :]))
                for half in range(2):
                    pairs.append((mem.b1[0:n, layer, half, m:m + 1],
                                  a["b1"][layer][half * HID + h0:half * HID + h0 + n].unsqueeze(1)))
        load(nc, "layers", *pairs)
        for layer in range(DEPTH):
            local_attention(nc, mem, f"local{layer}", layer, f if layer else xn, f)
            normalise(nc, mem, f"ln_f{layer}", [(mem.h, mem.h)])
            feed_forward(nc, mem, f"ff{layer}", layer, f)


def mixer(nc, mem, name, causal, project_heads, out_tok):
    with ExitStack() as s0:
        t = lambda n, shape, dt=F32: s0.enter_context(nc.sbuf_tensor(f"{name}_{n}", shape, dt))
        mem.v_tok = out_tok
        project_heads()
        mem.heads_out = t("heads_out", [P, H * CH])
        with ExitStack() as s1:
            mem.QS = s1.enter_context(nc.sbuf_tensor(f"{name}_QS", [P, H * T], BF16))
            mem.KS = s1.enter_context(nc.sbuf_tensor(f"{name}_KS", [P, H * T], BF16))
            attention(nc, mem, name, causal)
        gather_heads(nc, mem, f"{name}_gather", out_tok)


def build(nc, a, out):
    with ExitStack() as ctx:
        def sb(n, shape, dt=F32):
            return ctx.enter_context(nc.sbuf_tensor(n, shape, dt))

        mem = Memory()
        mem.q_parts_dram = nc.dram_tensor("q_parts", (PARTS, D, T), BF16).ap()
        mem.k_parts_dram = nc.dram_tensor("k_parts", (PARTS, D, T), BF16).ap()
        mem.fill = a["fill"].bitcast(BF16)
        x = sb("x", [P, NT, D])
        s = sb("s", [P, NT, D])
        mem.ident = sb("identity", [P, P])
        mem.ident_bf = sb("identity_bf", [P, P], BF16)
        mem.hide_later_keys = sb("hide_later_keys", [P, P], BF16)
        mem.hide_earlier_queries = sb("hide_earlier_queries", [P, P], BF16)
        mem.sums = sb("sums", [P, NT, 6])
        mem.moments = sb("moments", [P, NT, 2])
        mem.rstd = sb("rstd", [P, NT])
        mem.minus_half = sb("minus_half", [P, NT])

        with nc.sbuf_tensor("masks_sb", [P, 3, P], F32) as masks, nc.semaphore("cast") as cast:
            load(nc, "x", (x[:, :, :], tiles_of(a["x"])), (mem.ident[:, :], a["ident"]),
                 (masks[:, :, :], a["masks"].rearrange("m p q -> p m q")))
            with nc.Block() as block:
                @block.vector
                def _(dve):
                    for n, m in enumerate((mem.ident_bf, mem.hide_later_keys, mem.hide_earlier_queries)):
                        nc.vector.tensor_copy(m[:, :], masks[:, n, :]).then_inc(cast, 1)

        with ExitStack() as s0:
            xn = s0.enter_context(nc.sbuf_tensor("xn", [P, NT, D], F32))
            normalise(nc, mem, "ln_x0", [(x, xn)])

            def project0():
                with ExitStack() as s1:
                    u = lambda n, shape: s1.enter_context(nc.sbuf_tensor(n, shape, F32))
                    zn = u("zn", [P, NT, D])
                    wide = u("zn_wide", [P, T])
                    w = [u(f"w0_{n}", [P, D]) for n in range(3)]
                    ls = u("ls", [P, 2])
                    load(nc, "w0", *[(w[n][:, :], a["w_qkv0"][n]) for n in range(3)],
                         (ls[:, 0:1], a["ln_scale0"].unsqueeze(1)), (ls[:, 1:2], a["ln_bias0"].unsqueeze(1)))
                    normalise(nc, mem, "ln_z0", [(xn, zn)])
                    project(nc, mem, "proj0", zn, wide, *w, affine=(ls[:, 0:1], ls[:, 1:2]))

            mixer(nc, mem, "mix0", False, project0, s)
            with ExitStack() as s1:
                u = lambda n, shape: s1.enter_context(nc.sbuf_tensor(n, shape, F32))
                w_proj, b_proj, o = u("w_proj", [P, D]), u("b_proj", [P, D]), u("xnb", [P, NT, D])
                load(nc, "w_proj", (w_proj[:, :], a["w_proj0"]), (b_proj[:, :], a["b_proj0"].partition_broadcast(P)))
                add_bias(nc, "bias0", xn, b_proj, o)
                linear_out(nc, mem, "out0", s, w_proj, o, True)
                f = u("f", [P, NT, D])
                gate_layers(nc, mem, a, xn, f)
                gate_residual(nc, mem, "gate0", f, o, x)

        with ExitStack() as s0:
            wide = s0.enter_context(nc.sbuf_tensor("xn_wide", [P, T], F32))
            w_out = s0.enter_context(nc.sbuf_tensor("w_out1", [P, D], F32))

            def project1():
                with ExitStack() as s1:
                    u = lambda n, shape: s1.enter_context(nc.sbuf_tensor(n, shape, F32))
                    xn = u("xn1", [P, NT, D])
                    w = [u(f"w1_{n}", [P, D]) for n in range(3)]
                    load(nc, "w1", *[(w[n][:, :], a["w_qkv1"][n]) for n in range(3)], (w_out[:, :], a["w_out1"]))
                    normalise(nc, mem, "ln_x1", [(x, xn)])
                    project(nc, mem, "proj1", xn, wide, *w)

            o = s
            mixer(nc, mem, "mix1", True, project1, o)
            linear_out(nc, mem, "out1", o, w_out, s, False)
            experts(nc, mem, a, "moe", wide, s, x, out)


def kernel(**inputs):
    import concourse.bacc as bacc
    from concourse.bass_utils import run_bass_kernel_spmd

    arrays = {f"in_{n}": v for n, v in layout(inputs).items()}
    nc = bacc.Bacc("TRN2", target_bir_lowering=False, num_devices=1)
    a = {n[3:]: nc.dram_tensor(n, v.shape, mybir.dt.from_np(v.dtype), kind="ExternalInput").ap()
         for n, v in arrays.items()}
    out = nc.dram_tensor("out_0", (T, D), F32, kind="ExternalOutput").ap()
    build(nc, a, out)
    r = run_bass_kernel_spmd(nc, [arrays], core_ids=[0])
    return r.results[0]["out_0"].reshape(1, T, D)
```

```python
from contextlib import ExitStack, contextmanager

import concourse.bass as bass
import numpy as np
from concourse import mybir

F32 = mybir.dt.float32
BF16 = mybir.dt.bfloat16
ALU = mybir.AluOpType
ACT = mybir.ActivationFunctionType
AX = mybir.AxisListType

P = 128
T = 2048
D = 128
NT = T // P
CH = 512
NC = T // CH
TPC = CH // P
EPS = 1e-5
NEG = -30000.0

H = 16
HD = D // H
PARTS = 3
ROWS = PARTS * PARTS * HD
MROW = 96
KROWS = MROW + PARTS
VW = 32
SCALE = 1.0 / float(np.sqrt(HD))


class Memory:
    pass


def tiles_of(ap):
    return ap.rearrange("(i p) d -> p i d", p=P)


@contextmanager
def stage(nc, name):
    with ExitStack() as ctx:
        used = []

        def sem(n):
            used.append(nc.alloc_semaphore(f"{name}_{n}"))
            return used[-1]

        def give_back():
            nc.clear_and_free_semaphores(used)
            nc.all_engine_barrier()

        ctx.callback(give_back)
        yield ctx, sem


def mixed_order(n):
    return [x for i in range(n // 2) for x in (i, n - 1 - i)]


def attention_units(causal):
    units = []
    for kb in mixed_order(NT) if causal else range(NT):
        for c in range(NC):
            first = max(0, -((c - kb) // NC)) if causal else 0
            if first < TPC:
                units.append((kb, c, first))
    return units


def max_tiles(causal):
    tiles = []
    for i in mixed_order(NT) if causal else range(NT):
        keys = (i + 1) * P if causal else T
        for half in range(T // MAX_KEYS):
            n = min(MAX_KEYS, keys - half * MAX_KEYS)
            if n > 0:
                tiles.append((i, half, half * MAX_KEYS, n))
    return tiles


def turns(n, slots):
    order = [i % slots for i in range(n)]
    if n % slots == 1:
        order[-1] = 1
    return order


def had_before(order):
    n = len(order)
    return [max(v for v in range(i - n, i) if order[v % n] == slot) for i, slot in enumerate(order)]


def max_schedule(causal):
    units, mtiles = attention_units(causal), max_tiles(causal)
    ends = lambda w: np.cumsum(w) / np.sum(w)
    unit_end = ends([(TPC - first) * P + 32 for _, _, first in units])
    tile_end = ends([n + 64 for _, _, _, n in mtiles])
    share, turn_lag, _ = PACE[causal]
    ahead = int(np.sum(tile_end <= share))
    stream = [(1, k) for k in range(ahead, len(mtiles))] + [(2, k) for k in range(ahead)]
    plan, last = [], None
    for u, at in enumerate(unit_end):
        now = []
        while stream:
            heads, k = stream[0]
            if heads - 1 + tile_end[k] > at + share:
                break
            if heads == 2 and (last is None or u < last + 2 * turn_lag):
                break
            now.append(stream.pop(0))
            if now[-1] == (1, len(mtiles) - 1):
                last = u
        if last is not None and u == last + turn_lag:
            now.append((1, TURN))
        plan.append(now)
    plan[-1] += stream
    return plan, ahead


TURN = -1
MAX_KEYS = 512
MAX_SLOTS = 3
EXP_SLOTS = 4
PROB_SLOTS = 3
PACE = [(0.25, 3, 4), (0.25, 3, 4)]


def attention(nc, mem, name, causal):
    units = attention_units(causal)
    mtiles = max_tiles(causal)
    NU, NM = len(units), len(mtiles)
    first_head = lambda h: isinstance(h, int) and h == 0
    blocks = list(dict.fromkeys(kb for kb, _, _ in units))
    group_of = [[u for u, x in enumerate(units) if x[0] == kb] for kb in blocks]
    plan, ahead = max_schedule(causal)
    slot_of = turns(NU, EXP_SLOTS)
    before = had_before(slot_of)
    mslot_of = turns(NM, MAX_SLOTS)
    mbefore = had_before(mslot_of)
    pslot_of = turns(NT, PROB_SLOTS)
    pbefore = had_before(pslot_of)
    pv_plan, latest = [[] for _ in range(NU)], 2 * NU
    for b in reversed(range(NT)):
        after = min(c for c in range(b + 1, b + 1 + NT) if pslot_of[c % NT] == pslot_of[b])
        limit = group_of[after % NT][0] + (NU if after >= NT else 0)
        latest = min(group_of[b][-1] + PACE[causal][2], limit, latest)
        pv_plan[latest % NU].insert(0, b - NT if latest >= NU else b)
    last_pv = max(u for u, now in enumerate(pv_plan) if -1 in now)
    early = ahead + sum(heads == 1 for now in plan[:last_pv + 1] for heads, _ in now)

    with stage(nc, name) as (ctx, sem):
        def sb(n, shape, dt):
            return ctx.enter_context(nc.sbuf_tensor(f"{name}_{n}", shape, dt))


        QS, KS = mem.QS, mem.KS
        v_head = sb("v_head", [P, NT, VW], F32)
        probs = sb("probs", [P, PROB_SLOTS, NC, CH], F32)
        part_max = sb("part_max", [P, NT, T // MAX_KEYS], F32)
        neg_max = sb("neg_max", [P, NT], F32)
        m_rest = sb("m_rest", [NT, P], F32)
        m_parts = sb("m_parts", [NT, PARTS, P], BF16)

        ps_max = [ctx.enter_context(nc.psum_tensor(f"{name}_ps_max{s}", [P, MAX_KEYS], F32))
                  for s in range(MAX_SLOTS)]
        ps_exp = [ctx.enter_context(nc.psum_tensor(f"{name}_ps_exp{s}", [P, CH], F32)) for s in range(EXP_SLOTS)]
        ps_out = ctx.enter_context(nc.psum_tensor(f"{name}_ps_out", [P, CH], F32))

        filled_first = sem("filled_first")
        filled_rest = sem("filled_rest")
        loads = [sem(f"loads{s}") for s in range(2)]
        heads_loaded = sem("heads_loaded")
        v_cleared = sem("v_cleared")
        v_staged = sem("v_staged")
        max_cleared = sem("max_cleared")
        max_scores = sem("max_scores")
        max_taken = sem("max_taken")
        max_folded = sem("max_folded")
        split = sem("split")
        m_ready = sem("m_ready")
        m_loaded = sem("m_loaded")
        exp_scores = sem("exp_scores")
        probs_ready = sem("probs_ready")
        pv_done = sem("pv_done")
        out_taken = sem("out_taken")

        block = ctx.enter_context(nc.Block())

        @block.sync
        def _(sp):
            def load_rows(h, s):
                rows = bass.ds(h * HD, HD)
                for g in range(PARTS):
                    r = slice(g * PARTS * HD, (g + 1) * PARTS * HD)
                    sp.dma_start(QS[r, bass.ds(h * T, T)], mem.q_parts_dram[g:g + 1, rows, :].broadcast_to(
                        [PARTS, HD, T])).then_inc(loads[s], 16)
                    sp.dma_start(KS[r, bass.ds(h * T, T)], mem.k_parts_dram[:, rows, :]).then_inc(loads[s], 16)

            n_dma = 2 * PARTS * 16

            load_rows(0, 0)
            load_rows(1, 1)
            with sp.Fori(0, H // 2 - 1) as i:
                for s in range(2):
                    sp.wait_ge(loads[s], i * n_dma + n_dma)
                    sp.sem_inc(heads_loaded, 1)
                    load_rows(i * 2 + (s + 2), s)
            for s in range(2):
                sp.wait_ge(loads[s], n_dma * (H // 2))
                sp.sem_inc(heads_loaded, 1)

        @block.gpsimd
        def _(pool):
            nc.gpsimd.memset(v_head[:], 0.0).then_inc(v_cleared, 1)
            pool.wait_ge(v_cleared, 1)
            nc.gpsimd.memset(v_head[:, :, HD:HD + 1], 1.0).then_inc(v_cleared, 1)
            pool.wait_ge(v_cleared, 2)

            def stage(h):
                nc.gpsimd.tensor_copy(v_head[:, :, 0:HD],
                                      mem.v_tok[:, :, bass.ds(h * HD, HD)]).then_inc(v_staged, 1)
            stage(0)

            def load_max(h):
                pool.wait_ge(m_ready, h + 1)
                for g in range(PARTS):
                    pool.dma_start(
                        QS[MROW + g:MROW + g + 1, bass.ds(h * T, T)].rearrange("o (i p) -> o i p", p=P),
                        m_parts[:, g, :]).then_inc(m_loaded, 16)
            load_max(0)
            with pool.Fori(1, H) as h:
                load_max(h)
                pool.wait_ge(pv_done, h * NT)
                stage(h)

        @block.tensor
        def _(pe):
            def max_tile(h, k):
                i, half, key0, n = mtiles[k]
                if k == 0:
                    if not first_head(h):
                        pe.wait_ge(m_ready, h)
                    pe.wait_ge(heads_loaded, h + 1)
                    if isinstance(h, int) and h < 2:
                        pe.wait_ge(filled_rest if h else filled_first, 48)
                elif mbefore[k] >= 0:
                    pe.wait_ge(max_taken, h * NM + (mbefore[k] + 1))
                out = ps_max[mslot_of[k]]
                last = causal and key0 + n == (i + 1) * P
                for a in range(0, n, CH):
                    m = min(CH, n - a)
                    masked = last and a + m == n
                    mm = nc.tensor.matmul(out[:, a:a + m],
                                          QS[0:MROW, bass.ds(h * T + i * P, P)],
                                          KS[0:MROW, bass.ds(h * T + (key0 + a), m)],
                                          start=True, stop=not masked)
                    if masked:
                        mm = nc.tensor.matmul(out[:, n - P:n], mem.ident_bf[:, :], mem.hide_later_keys[:, :],
                                              start=False, stop=True)
                mm.then_inc(max_scores, 1)

            def transpose_max(h):
                pe.wait_ge(max_folded, h + 1)
                nc.tensor.transpose(ps_max[0][0:NT, 0:P], neg_max[:, :], mem.ident[:, :]).then_inc(max_scores, 1)

            def exp_unit(h, u):
                kb, c, first = units[u]
                if not first_head(h) or before[u] >= 0:
                    pe.wait_ge(probs_ready, h * NU + (before[u] + 1))
                out, n = ps_exp[slot_of[u]], (TPC - first) * P
                masked = causal and c == kb % NC
                queries = QS[0:KROWS, bass.ds(h * T, T)].rearrange("r (j c p) -> r c j p", c=NC, p=P)
                mm = nc.tensor.matmul(out[:, 0:n].rearrange("k (j p) -> k j p", p=P),
                                      KS[0:KROWS, bass.ds(h * T + kb * P, P)],
                                      queries[:, c, first:TPC, :], start=True, stop=not masked)
                if masked:
                    mm = nc.tensor.matmul(out[:, 0:P], mem.ident_bf[:, :], mem.hide_earlier_queries[:, :],
                                          start=False, stop=True)
                mm.then_inc(exp_scores, 1)

            def pv(h, b):
                pe.wait_ge(probs_ready, h * NU + (group_of[b][-1] + 1))
                if b == 0:
                    pe.wait_ge(v_staged, h + 1)
                    if not first_head(h):
                        pe.wait_ge(out_taken, h)
                for u in group_of[b]:
                    kb, c, first = units[u]
                    last = u == max(v for v in range(NU) if units[v][1] == c)
                    mm = nc.tensor.matmul(ps_out[32 * c:32 * c + VW, first * P:CH], v_head[:, kb, :],
                                          probs[:, pslot_of[b], c, first * P:CH], start=(b == 0), stop=last,
                                          skip_group_check=True)
                mm.then_inc(pv_done, 1)

            def head(h, heads_after):
                pe.wait_ge(m_loaded, h * (16 * PARTS) + 16 * PARTS)
                for u in range(NU):
                    exp_unit(h, u)
                    for heads, k in plan[u]:
                        if heads <= heads_after:
                            if k == TURN:
                                transpose_max(h + 1)
                            else:
                                max_tile(h + heads, k)
                    for b in pv_plan[u]:
                        if b >= 0:
                            pv(h, b)
                        elif not first_head(h):
                            pv(h - 1, NT + b)

            for k in range(NM):
                max_tile(0, k)
            transpose_max(0)
            for k in range(ahead):
                max_tile(1, k)
            head(0, 2)
            with pe.Fori(1, H - 2) as h:
                head(h, 2)
            head(H - 2, 1)
            head(H - 1, 0)
            for b in sorted(b for late in pv_plan for b in late if b < 0):
                pv(H - 1, NT + b)

        @block.scalar
        def _(act):
            def fill_rows(h, heads, filled):
                for stack, r0, r1, n in ((QS, ROWS, MROW, 0), (KS, ROWS, MROW, 0), (KS, MROW, KROWS, 1)):
                    act.dma_start(stack[r0:r1, h * T:(h + heads) * T].rearrange("p (h t) -> p h t", t=T),
                                 mem.fill[n, 0:r1 - r0, :].unsqueeze(1).broadcast_to([r1 - r0, heads, T])
                                 ).then_inc(filled, 16)

            fill_rows(0, 1, filled_first)
            act.wait_ge(heads_loaded, 1)
            fill_rows(1, H - 1, filled_rest)

            def head(h):
                for u, (kb, c, first) in enumerate(units):
                    b = blocks.index(kb)
                    if u == group_of[b][0] and (pbefore[b] >= 0 or not first_head(h)):
                        act.wait_ge(pv_done, h * NT + (pbefore[b] + 1))
                    act.wait_ge(exp_scores, h * NU + (u + 1))
                    nc.scalar.activation(probs[:, pslot_of[b], c, first * P:CH],
                                         ps_exp[slot_of[u]][:, 0:(TPC - first) * P],
                                         ACT.Exp, scale=SCALE).then_inc(probs_ready, 1)
            head(0)
            with act.Fori(1, H) as h:
                head(h)

        @block.vector
        def _(dve):
            def maxima(h, tiles):
                for k in tiles:
                    i, half, _, n = mtiles[k]
                    dve.wait_ge(max_scores, h * (NM + 1) + (k + 1))
                    nc.vector.tensor_reduce(part_max[:, i, half:half + 1], ps_max[mslot_of[k]][:, 0:n], AX.X,
                                            ALU.max).then_inc(max_taken, 1)

            def fold(h):
                dve.wait_ge(max_taken, (h + 1) * NM)
                nc.vector.tensor_reduce(neg_max[:, :], part_max[:, :, :], AX.X, ALU.max,
                                        negate=True).then_inc(max_folded, 1)
                dve.wait_ge(max_scores, (h + 1) * (NM + 1))
                turned = ps_max[0][0:NT, 0:P]
                if not first_head(h):
                    dve.wait_ge(m_loaded, h * (16 * PARTS))
                nc.vector.tensor_copy(m_parts[:, 0, :], turned).then_inc(split, 1)
                dve.wait_ge(split, h * 3 + 1)
                nc.vector.tensor_tensor(m_rest[:, :], turned, m_parts[:, 0, :], ALU.subtract).then_inc(split, 1)
                dve.wait_ge(split, h * 3 + 2)
                nc.vector.tensor_copy(m_parts[:, 1, :], m_rest[:, :]).then_inc(split, 1)
                dve.wait_ge(split, h * 3 + 3)
                nc.vector.tensor_tensor(m_parts[:, 2, :], m_rest[:, :], m_parts[:, 1, :],
                                        ALU.subtract).then_inc(m_ready, 1)

            def save(h):
                dve.wait_ge(pv_done, (h + 1) * NT)
                nc.vector.tensor_copy(mem.heads_out[:, bass.ds(h * CH, CH)], ps_out[:, :]).then_inc(out_taken, 1)

            nc.vector.memset(part_max[:], -3.0e38).then_inc(max_cleared, 1)
            dve.wait_ge(max_cleared, 1)
            maxima(0, range(NM))
            fold(0)
            maxima(1, range(ahead))
            maxima(1, range(ahead, NM))
            fold(1)
            maxima(2, range(ahead))
            with dve.Fori(1, H - 2) as h:
                maxima(h + 1, range(ahead, early))
                save(h - 1)
                maxima(h + 1, range(early, NM))
                fold(h + 1)
                maxima(h + 2, range(ahead))
            maxima(H - 1, range(ahead, early))
            save(H - 3)
            maxima(H - 1, range(early, NM))
            fold(H - 1)
            save(H - 2)
            save(H - 1)


class Norm:

    def __init__(self, nc, mem, sem, src, dst, name="norm"):
        self.nc, self.mem, self.src, self.dst = nc, mem, src, dst
        self.summed = sem(f"{name}_summed")
        self.moments_ready = sem(f"{name}_moments_ready")
        self.widened = sem(f"{name}_widened")
        self.rstd_ready = sem(f"{name}_rstd_ready")
        self.scaled = sem(f"{name}_scaled")
        self.half_set = sem(f"{name}_half_set")

    def vector(self, dve):
        nc, mem = self.nc, self.mem

        def moments(c):
            for i in range(c * TPC, (c + 1) * TPC):
                nc.vector.bn_stats(mem.sums[:, i, :], self.src[:, i, :]).then_inc(self.summed, 1)
            dve.wait_ge(self.summed, (c + 1) * TPC)
            for i in range(c * TPC, (c + 1) * TPC):
                nc.vector.bn_aggr(mem.moments[:, i, :], mem.sums[:, i, :]).then_inc(self.moments_ready, 1)

        def scale(c):
            dve.wait_ge(self.rstd_ready, c + 1)
            for i in range(c * TPC, (c + 1) * TPC):
                nc.vector.tensor_scalar(self.dst[:, i, :], self.src[:, i, :], mem.moments[:, i, 0:1],
                                        mem.rstd[:, i:i + 1], ALU.subtract, ALU.mult).then_inc(self.scaled, 1)

        for c in range(NC):
            moments(c)
            if c:
                scale(c - 1)
        scale(NC - 1)

    def gpsimd(self, pool):
        nc, mem = self.nc, self.mem
        nc.gpsimd.memset(mem.minus_half[:], -0.5).then_inc(self.half_set, 1)
        pool.wait_ge(self.half_set, 1)
        for c in range(NC):
            t = slice(c * TPC, (c + 1) * TPC)
            pool.wait_ge(self.moments_ready, (c + 1) * TPC)
            nc.gpsimd.tensor_scalar(mem.rstd[:, t], mem.moments[:, t, 1], 1.0, EPS, ALU.mult,
                                    ALU.add).then_inc(self.widened, 1)
            pool.wait_ge(self.widened, c + 1)
            nc.gpsimd.tensor_tensor(mem.rstd[:, t], mem.rstd[:, t], mem.minus_half[:, t],
                                    ALU.pow).then_inc(self.rstd_ready, 1)


def normalise(nc, mem, name, src, dst):
    with stage(nc, name) as (ctx, sem):
        norm = Norm(nc, mem, sem, src, dst)
        block = ctx.enter_context(nc.Block())

        @block.vector
        def _(dve):
            norm.vector(dve)

        @block.gpsimd
        def _(pool):
            norm.gpsimd(pool)


def project(nc, mem, name, src, xn, wide, wq, wk, wv, keep, affine=None):
    with stage(nc, name) as (ctx, sem):

        parts = [ctx.enter_context(nc.sbuf_tensor(f"{name}_parts{n}", [P, PARTS, T], BF16)) for n in range(2)]
        rest = ctx.enter_context(nc.sbuf_tensor(f"{name}_rest", [P, T], F32))
        ps = [ctx.enter_context(nc.psum_tensor(f"{name}_ps{b}", [P, CH], F32)) for b in range(8)]
        turned = sem("turned")
        wide_ready = sem("wide_ready")
        product = sem("product")
        first_part = sem("first_part")
        rest_ready = sem("rest_ready")
        second_part = sem("second_part")
        third_part = sem("third_part")
        v_ready = sem("v_ready")
        parts_stored = sem("parts_stored")
        kept = sem("kept")
        norm = Norm(nc, mem, sem, src, xn)
        block = ctx.enter_context(nc.Block())

        @block.sync
        def _(sp):
            if keep[1] is wide:
                sp.wait_ge(wide_ready, NC)
            sp.dma_start(keep[0], keep[1][:]).then_inc(kept, 16)
            for n, dram in enumerate((mem.q_parts_dram, mem.k_parts_dram)):
                for g, part_ready in enumerate((first_part, second_part, third_part)):
                    sp.wait_ge(part_ready, NC * (n + 1))
                    sp.dma_start(dram[g], parts[n][:, g, :]).then_inc(parts_stored, 16)
            sp.wait_ge(parts_stored, 2 * PARTS * 16)
            sp.wait_ge(kept, 16)

        @block.gpsimd
        def _(pool):
            norm.gpsimd(pool)

        @block.tensor
        def _(pe):
            for c in range(NC):
                pe.wait_ge(norm.scaled, (c + 1) * TPC)
                for i in range(TPC):
                    mm = nc.tensor.transpose(ps[c][:, i * P:(i + 1) * P], xn[:, c * TPC + i, :], mem.ident[:, :])
                mm.then_inc(turned, 1)
            for n, w in enumerate((wq, wk)):
                for c in range(NC):
                    if n == 0:
                        pe.wait_ge(wide_ready, c + 1)
                    if n == 1 and c == 0:
                        pe.wait_ge(wide_ready, NC)
                    nc.tensor.matmul(ps[4 * (1 - n) + c][:, :], w[:, :], wide[:, c * CH:(c + 1) * CH],
                                     start=True, stop=True).then_inc(product, 1)
            for c in range(NC):
                pe.wait_ge(rest_ready, c + 1)
                for i in range(TPC):
                    t = c * TPC + i
                    mm = nc.tensor.matmul(ps[4 + c][:, i * P:(i + 1) * P], wide[:, t * P:(t + 1) * P], wv[:, :],
                                          start=(i == 0), stop=(i == TPC - 1), skip_group_check=True)
                mm.then_inc(product, 1)

        @block.scalar
        def _(act):
            for c in range(NC):
                act.wait_ge(turned, c + 1)
                out = wide[:, c * CH:(c + 1) * CH]
                if affine is None:
                    nc.scalar.activation(out, ps[c][:, :], ACT.Copy).then_inc(wide_ready, 1)
                else:
                    nc.scalar.activation(out, ps[c][:, :], ACT.Identity, bias=affine[1],
                                         scale=affine[0]).then_inc(wide_ready, 1)
            for n in range(2):
                for c in range(NC):
                    act.wait_ge(product, n * NC + c + 1)
                    nc.scalar.activation(parts[n][:, 0, c * CH:(c + 1) * CH], ps[4 * (1 - n) + c][:, :],
                                         ACT.Copy).then_inc(first_part, 1)
                for c in range(NC):
                    act.wait_ge(rest_ready, n * NC + c + 1)
                    nc.scalar.activation(parts[n][:, 1, c * CH:(c + 1) * CH], rest[:, c * CH:(c + 1) * CH],
                                         ACT.Copy).then_inc(second_part, 1)
            for c in range(NC):
                act.wait_ge(product, 2 * NC + c + 1)
                nc.scalar.activation(mem.v_tok[:, c * TPC:(c + 1) * TPC, :],
                                     ps[4 + c][:, :].rearrange("p (i d) -> p i d", d=D),
                                     ACT.Copy).then_inc(v_ready, 1)

        @block.vector
        def _(dve):
            norm.vector(dve)
            for n in range(2):
                for c in range(NC):
                    col = slice(c * CH, (c + 1) * CH)
                    dve.wait_ge(first_part, n * NC + c + 1)
                    if n == 1:
                        dve.wait_ge(third_part, c + 1)
                    nc.vector.tensor_tensor(rest[:, col], ps[4 * (1 - n) + c][:, :], parts[n][:, 0, col],
                                            ALU.subtract).then_inc(rest_ready, 1)
                for c in range(NC):
                    col = slice(c * CH, (c + 1) * CH)
                    dve.wait_ge(second_part, n * NC + c + 1)
                    nc.vector.tensor_tensor(parts[n][:, 2, col], rest[:, col], parts[n][:, 1, col],
                                            ALU.subtract).then_inc(third_part, 1)


def gather_heads(nc, mem, name, out_tok, loads, later_loads=(), later=None):
    with stage(nc, name) as (ctx, sem):

        inv = ctx.enter_context(nc.sbuf_tensor(f"{name}_inv", [P, 4, NT], F32))
        ps = [ctx.enter_context(nc.psum_tensor(f"{name}_ps{b}", [P, TPC, NC, VW], F32)) for b in range(4)]
        turned = sem("turned")
        inverted = sem("inverted")
        divided = sem("divided")
        loaded = sem("loaded")
        block = ctx.enter_context(nc.Block())

        @block.sync
        def _(sp):
            for dst, src in loads:
                sp.dma_start(dst, src).then_inc(loaded, 16)
            for dst, src in later_loads:
                sp.dma_start(dst, src).then_inc(later, 16)
            sp.wait_ge(loaded, 16 * len(loads))

        @block.tensor
        def _(pe):
            for h in range(H):
                if h >= 4:
                    pe.wait_ge(divided, h - 3)
                for s in range(TPC):
                    mm = nc.tensor.transpose(ps[h % 4][:, s, :, :].rearrange("p c r -> p (c r)"),
                                             mem.heads_out[:, h * CH + s * P:h * CH + (s + 1) * P], mem.ident[:, :])
                mm.then_inc(turned, 1)

        @block.vector
        def _(dve):
            def divide(h):
                dve.wait_ge(inverted, h + 1)
                nc.vector.tensor_tensor(
                    out_tok[:, :, h * HD:(h + 1) * HD].rearrange("p (s c) d -> p s c d", c=NC),
                    ps[h % 4][:, :, :, 0:HD],
                    inv[:, h % 4, :].rearrange("p (s c) -> p s c", c=NC).unsqueeze(3).broadcast_to([P, TPC, NC, HD]),
                    ALU.mult).then_inc(divided, 1)

            for h in range(H):
                dve.wait_ge(turned, h + 1)
                if h >= 4:
                    dve.wait_ge(divided, h - 3)
                nc.vector.reciprocal(inv[:, h % 4, :].rearrange("p (s c) -> p s c", c=NC),
                                     ps[h % 4][:, :, :, HD]).then_inc(inverted, 1)
                if h >= 1:
                    divide(h - 1)
            divide(H - 1)


DEPTH = 2
FH = 8
FD = 64
WIN = 64
INNER = FH * FD
HID = int(D * 4 * 2 / 3)
HCH = [(m, min(P, HID - m)) for m in range(0, HID, P)]
QK_SCALE = 8.0
HIDE = -1.0e30
TINY = 1e-24


def rotary_tables():
    half = np.arange(0, FD, 2, dtype=np.float32)
    inv_freq = (1.0 / np.float32(10000.0) ** (half / np.float32(FD))).astype(np.float32)
    t = np.arange(T, dtype=np.float32)
    freqs = (t[:, None] * inv_freq[None, :]).astype(np.float32)
    base = ((half + np.float32(0.4 * FD)) / np.float32(1.4 * FD)).astype(np.float32)
    power = ((t - T // 2) / np.float32(WIN // 2)).astype(np.float32)
    scale = (base[None, :] ** power[:, None]).astype(np.float32)
    cos, sin = np.cos(freqs), np.sin(freqs)
    out = np.empty((2, T, 2, FD), np.float32)
    for n, s in enumerate((scale, 1 / scale)):
        out[0, :, n, :] = np.concatenate([cos * s, cos * s], -1)
        out[1, :, n, :] = np.concatenate([-sin * s, sin * s], -1)
    return out


def window_masks():
    i = np.arange(P)[:, None]
    slot = np.arange(2 * WIN)[None, :]
    hidden = (i % WIN < slot - WIN) | (i % WIN > slot)
    both = np.stack([np.where(hidden | ((i < WIN) & (slot < WIN)), HIDE, 0.0), np.where(hidden, HIDE, 0.0)])
    return (both.astype(np.float32).view(np.uint32) >> 16).astype(np.uint16)


def local_attention(nc, mem, name, layer, src, dst):
    SLOTS = 2 * WIN
    hf, half_d = FD // 2, D // 2
    with stage(nc, name) as (ctx, sem):
        def sb(n, shape, dt=F32):
            return ctx.enter_context(nc.sbuf_tensor(f"{name}_{n}", shape, dt))

        def psum(n, shape):
            return ctx.enter_context(nc.psum_tensor(f"{name}_{n}", shape, F32))

        cos = sb("cos", [P, NT, 2, FD])
        sin = sb("sin", [P, NT, 2, FD])
        src_tile = sb("src_tile", [P, D])
        hT = sb("hT", [P, 1 + P])
        minus_half = sb("minus_half", [P, FH])
        squares, norms, inv_norm, straight, turned = ({
            "q": sb(f"{n}_q", shape), "k": sb(f"{n}_k", shape)} for n, shape in (
                ("squares", [P, FH, FD]), ("norms", [P, FH]), ("inv_norm", [P, FH]),
                ("straight", [P, FH, FD]), ("turned", [P, FH, FD])))
        k_normed = sb("k_normed", [P, FH, FD])
        qT = sb("qT", [P, FH // 2, P])
        kT = sb("kT", [P, FH // 2, WIN + P])
        v = sb("v", [P, 2, INNER])
        v_shift = sb("v_shift", [P, 2, INNER])
        neg_top = sb("neg_top", [P, FH])
        neg_max = sb("neg_max", [P, FH])
        sums = sb("sums", [P, FH])
        inv_sum = sb("inv_sum", [P, FH])
        probs = sb("probs", [P, FH, SLOTS])
        pT = sb("pT", [P, FH, P])
        o = sb("o", [P, INNER])
        oT = sb("oT", [P, FH // 2, P])

        ps_q = psum("ps_q", [P, FH, FD])
        ps_k = psum("ps_k", [P, FH, FD])
        ps_v = psum("ps_v", [P, INNER])
        ps_s = psum("ps_s", [P, 2, 4, P])
        ps_kT = psum("ps_kT", [P, FH // 2, P])
        ps_qT = psum("ps_qT", [P, FH // 2, P])
        ps_o = psum("ps_o", [P, INNER])

        scaled = sem("scaled")
        first_set = sem("first_set")
        src_copied = sem("src_copied")
        src_turned = sem("src_turned")
        carried = sem("carried")
        hT_ready = sem("hT_ready")
        made = {x: sem(f"{x}_made") for x in "kqv"}
        squared = {x: sem(f"{x}_squared") for x in "kq"}
        rotated = {x: sem(f"{x}_rotated") for x in "kq"}
        summed = {x: sem(f"{x}_summed") for x in "kq"}
        norms_ready = {x: sem(f"{x}_norms_ready") for x in "kq"}
        inverted = {x: sem(f"{x}_inverted") for x in "kq"}
        added = {x: sem(f"{x}_added") for x in "kq"}
        k_scaled = sem("k_scaled")
        turned_T = {x: sem(f"{x}_turned_T") for x in "kq"}
        T_ready = {x: sem(f"{x}T_ready") for x in "kq"}
        k_kept = sem("k_kept")
        v_ready = sem("v_ready")
        own_shifted = sem("own_shifted")
        next_shifted = sem("next_shifted")
        scored = sem("scored")
        topped = sem("topped")
        negated = sem("negated")
        exped = sem("exped")
        p_turned = sem("p_turned")
        pT_ready = sem("pT_ready")
        weighed = sem("weighed")
        sum_inverted = sem("sum_inverted")
        divided = sem("divided")
        o_turned = sem("o_turned")
        oT_ready = sem("oT_ready")
        projected = sem("projected")
        result = sem("result")
        h_shifted = sem("h_shifted")
        passed = sem("passed")
        h_edges = sem("h_edges")
        block = ctx.enter_context(nc.Block())

        def tiles(eng, body):
            body(0, 0)
            body(1, 1)
            with eng.Fori(1, NT // 2 - 1) as n:
                body(2 * n, 0)
                body(2 * n + 1, 1)
            body(NT - 2, 0)
            body(NT - 1, 1)

        def is_tile(i, ahead):
            return not isinstance(i, int) or 0 <= i + ahead < NT

        head_of = [[2 * j + half for j in range(4)] for half in range(2)]

        def at(x, i):
            return x[:, bass.ds(i, 1), :].squeeze(1)

        @block.sync
        def _(sp):
            def after(signal, count):
                sp.wait_ge(signal, count)
                sp.sem_inc(passed, 1)

            def shift_own(n, s):
                if is_tile(n, -1):
                    after(own_shifted, 16 * n)
                after(v_ready, n + 1)
                sp.dma_start(v_shift[WIN:P, s, :], v[0:WIN, s, :]).then_inc(own_shifted, 16)

            def shift_next(n, s):
                if is_tile(n, -1):
                    after(next_shifted, 16 * n)
                sp.dma_start(v_shift[0:WIN, 1 - s, :], v[WIN:P, s, :]).then_inc(next_shifted, 16)

            def shift_result(n):
                if is_tile(n, -1):
                    after(h_shifted, 16 * n)
                after(result, 2 * n + 2)
                sp.dma_start(mem.h[1:P, bass.ds(n, 1), half_d:D],
                             dst[0:P - 1, bass.ds(n, 1), half_d:D]).then_inc(h_shifted, 16)

            def tile(i, s):
                if is_tile(i, 1):
                    shift_own(i + 1, 1 - s)
                    shift_next(i, s)
                if is_tile(i, -2):
                    shift_result(i - 2)

            shift_own(0, 0)
            tiles(sp, tile)
            shift_result(NT - 2)
            shift_result(NT - 1)
            sp.wait_ge(result, 2 * NT)
            sp.dma_start(mem.h[0:1, 1:NT, half_d:D], dst[P - 1:P, 0:NT - 1, half_d:D]).then_inc(h_edges, 16)
            sp.wait_ge(own_shifted, 16 * NT)
            sp.wait_ge(next_shifted, 16 * (NT - 1))
            sp.wait_ge(h_shifted, 16 * NT)
            sp.wait_ge(h_edges, 16)

        @block.gpsimd
        def _(pool):
            def copy_src(n):
                if is_tile(n, -1):
                    pool.wait_ge(src_turned, n)
                nc.gpsimd.tensor_copy(src_tile[:, :], at(src, n)).then_inc(src_copied, 1)

            def work(n, s):
                pool.wait_ge(rotated["k"], 3 * n + 3)
                nc.gpsimd.tensor_tensor(straight["k"][:, :, :], straight["k"][:, :, :], turned["k"][:, :, :],
                                        ALU.add).then_inc(added["k"], 1)
                if is_tile(n, -1):
                    pool.wait_ge(k_scaled, n)
                pool.wait_ge(norms_ready["k"], n + 1)
                nc.gpsimd.tensor_tensor(inv_norm["k"][:, :], norms["k"][:, :], minus_half[:, :],
                                        ALU.pow).then_inc(inverted["k"], 1)
                if is_tile(n, 1):
                    copy_src(n + 1)
                pool.wait_ge(rotated["q"], 3 * n + 3)
                nc.gpsimd.tensor_tensor(straight["q"][:, :, :], straight["q"][:, :, :], turned["q"][:, :, :],
                                        ALU.add).then_inc(added["q"], 1)
                if is_tile(n, -1):
                    pool.wait_ge(exped, n * FH)
                pool.wait_ge(norms_ready["q"], n + 1)
                nc.gpsimd.tensor_tensor(inv_norm["q"][:, :], norms["q"][:, :], minus_half[:, :],
                                        ALU.pow).then_inc(inverted["q"], 1)

            nc.gpsimd.memset(hT[half_d:P, 0:1], 0.0).then_inc(first_set, 1)
            pool.wait_ge(first_set, 1)
            nc.gpsimd.memset(minus_half[:], -0.5).then_inc(first_set, 1)
            nc.gpsimd.memset(v_shift[0:WIN, 0, :], 0.0).then_inc(first_set, 1)
            nc.gpsimd.memset(mem.h[0:1, 0, half_d:D], 0.0).then_inc(first_set, 1)
            nc.gpsimd.memset(kT[:, :, 0:WIN], 0.0).then_inc(k_kept, 1)
            pool.wait_ge(first_set, 4)
            copy_src(0)
            tiles(pool, work)

        @block.tensor
        def _(pe):
            def turn_src(n):
                pe.wait_ge(src_copied, n + 1)
                if is_tile(n, -1):
                    pe.wait_ge(v_ready, n)
                nc.tensor.transpose(ps_v[:, 0:P], src_tile[:, :], mem.ident[:, :]).then_inc(src_turned, 1)

            def make(x, out):
                col = "qkv".index(x) * INNER
                nc.tensor.matmul(out, hT[:, 0:P], mem.wqkv[:, layer, col:col + INNER], start=True,
                                 stop=True).then_inc(made[x], 1)

            def make_kq(n):
                pe.wait_ge(hT_ready, 2 * n + 2)
                if is_tile(n, -1):
                    pe.wait_ge(rotated["q"], 3 * n)
                make("k", ps_k[:, :, :].rearrange("p h d -> p (h d)"))
                make("q", ps_q[:, :, :].rearrange("p h d -> p (h d)"))

            def turn(x, what, out, n):
                pe.wait_ge(k_scaled if x == "k" else added[x], n + 1)
                for j in range(FH // 2):
                    mm = nc.tensor.transpose(out[:, j, :],
                                             what[:, 2 * j:2 * j + 2, :].rearrange("p h d -> p (h d)"),
                                             mem.ident[:, :])
                mm.then_inc(turned_T[x], 1)

            def score(i):
                pe.wait_ge(T_ready["k"], i + 1)
                pe.wait_ge(T_ready["q"], i + 1)
                pe.wait_ge(k_kept, i + 1)
                if is_tile(i, -1):
                    pe.wait_ge(pT_ready, 2 * i)
                mask = mem.window_masks[:, 1 if is_tile(i, -1) else 0, :].unsqueeze(1).broadcast_to([P, 4, SLOTS])
                for half in range(2):
                    r = slice(half * FD, (half + 1) * FD)
                    nc.tensor.matmul(ps_s[:, half, :, :], mem.ident_bf[:, :], mask, start=True, stop=False,
                                     skip_group_check=True)
                    for j in range(4):
                        for w in range(2):
                            q = slice(w * WIN, (w + 1) * WIN)
                            mm = nc.tensor.matmul(ps_s[q, half, j, :], qT[r, j, q],
                                                  kT[r, j, w * WIN:w * WIN + SLOTS], start=False, stop=(j == 3),
                                                  skip_group_check=True)
                    mm.then_inc(scored, 1)

            def turn_probs(i, half):
                pe.wait_ge(exped, i * FH + 4 * half + 4)
                for j in range(4):
                    mm = nc.tensor.transpose(ps_s[:, half, j, :], probs[:, 4 * half + j, :], mem.ident[:, :])
                mm.then_inc(p_turned, 1)

            def weigh(n, s):
                pe.wait_ge(v_ready, n + 1)
                pe.wait_ge(own_shifted, n * 16 + 16)
                if is_tile(n, -1):
                    pe.wait_ge(next_shifted, n * 16)
                    pe.wait_ge(oT_ready, n)
                pe.wait_ge(pT_ready, 2 * n + 2)
                for hd in range(FH):
                    head = hd % 2 * 4 + hd // 2
                    for w, values in enumerate((v_shift, v)):
                        q = slice(w * WIN, (w + 1) * WIN)
                        mm = nc.tensor.matmul(ps_o[q, hd * FD:(hd + 1) * FD], pT[:, head, q],
                                              values[:, s, hd * FD:(hd + 1) * FD],
                                              start=(hd == 0), stop=(hd == FH - 1), skip_group_check=True)
                mm.then_inc(weighed, 1)

            def turn_o(n):
                pe.wait_ge(divided, n + 1)
                for j in range(FH // 2):
                    mm = nc.tensor.transpose(ps_o[:, j * P:(j + 1) * P], o[:, j * P:(j + 1) * P], mem.ident[:, :])
                mm.then_inc(o_turned, 1)

            def project(n):
                pe.wait_ge(oT_ready, n + 1)
                for j in range(FH // 2):
                    mm = nc.tensor.matmul(ps_v[:, 0:D], oT[:, j, :], mem.wo[:, layer, j, :], start=(j == 0),
                                          stop=(j == FH // 2 - 1))
                mm.then_inc(projected, 1)

            def tile(i, s):
                if is_tile(i, 1):
                    make_kq(i + 1)
                score(i)
                if is_tile(i, -2):
                    project(i - 2)
                if is_tile(i, -1):
                    weigh(i - 1, 1 - s)
                if is_tile(i, 1):
                    if is_tile(i, -2):
                        pe.wait_ge(result, 2 * i - 2)
                    make("v", ps_v[:, :])
                turn_probs(i, 0)
                if is_tile(i, 1):
                    turn("k", k_normed, ps_kT, i + 1)
                if is_tile(i, 2):
                    turn_src(i + 2)
                turn_probs(i, 1)
                if is_tile(i, 1):
                    turn("q", straight["q"], ps_qT, i + 1)
                if is_tile(i, -1):
                    turn_o(i - 1)

            pe.wait_ge(first_set, 4)
            turn_src(0)
            make_kq(0)
            make("v", ps_v[:, :])
            turn("k", k_normed, ps_kT, 0)
            turn("q", straight["q"], ps_qT, 0)
            turn_src(1)
            tiles(pe, tile)
            project(NT - 2)
            weigh(NT - 1, 1)
            turn_o(NT - 1)
            pe.wait_ge(result, 2 * NT - 2)
            project(NT - 1)

        @block.scalar
        def _(act):
            def copy(out, src, done):
                nc.scalar.activation(out, src, ACT.Copy).then_inc(done, 1)

            def keep_hT(n):
                act.wait_ge(src_turned, n + 1)
                if is_tile(n, -1):
                    copy(hT[half_d:P, 0:1], hT[half_d:P, P:P + 1], carried)
                copy(hT[0:half_d, 0:P], ps_v[0:half_d, 0:P], hT_ready)
                if is_tile(n, -1):
                    act.wait_ge(carried, n)
                copy(hT[half_d:P, 1:P + 1], ps_v[half_d:P, 0:P], hT_ready)

            def square(x, n):
                act.wait_ge(made[x], n + 1)
                if is_tile(n, -1):
                    act.wait_ge(summed[x], n)
                nc.scalar.activation(squares[x][:, :, :], (ps_k if x == "k" else ps_q)[:, :, :],
                                     ACT.Square).then_inc(squared[x], 1)

            def keep_v(n, s):
                act.wait_ge(made["v"], n + 1)
                if is_tile(n, -2):
                    act.wait_ge(weighed, n - 1)
                    act.wait_ge(own_shifted, 16 * n)
                    act.wait_ge(next_shifted, 16 * n - 16)
                copy(v[:, s, :], ps_v[:, :], v_ready)

            def keep_k(n):
                act.wait_ge(turned_T["k"], n + 1)
                act.wait_ge(k_kept, n + 1)
                copy(kT[:, :, WIN:WIN + P], ps_kT[:, :, :], T_ready["k"])

            def keep_q(n):
                act.wait_ge(turned_T["q"], n + 1)
                copy(qT[:, :, :], ps_qT[:, :, :], T_ready["q"])

            def keep_probs(i, half):
                act.wait_ge(p_turned, 2 * i + half + 1)
                copy(pT[:, 4 * half:4 * half + 4, :], ps_s[:, half, :, :], pT_ready)

            def keep_o(n):
                act.wait_ge(o_turned, n + 1)
                if is_tile(n, -1):
                    act.wait_ge(projected, n)
                copy(oT[:, :, :], ps_o[:, :].rearrange("p (j t) -> p j t", t=P), oT_ready)

            def tile(i, s):
                if is_tile(i, 1):
                    square("k", i + 1)
                    square("q", i + 1)
                if is_tile(i, -1):
                    act.wait_ge(sum_inverted, i)
                for half, heads in enumerate(head_of):
                    act.wait_ge(negated, 2 * i + half + 1)
                    for j, hd in enumerate(heads):
                        n = 4 * half + j
                        nc.scalar.activation(probs[:, n, :], ps_s[:, half, j, :], ACT.Exp, bias=neg_max[:, n:n + 1],
                                             scale=inv_norm["q"][:, hd:hd + 1],
                                             accum_out=sums[:, n:n + 1]).then_inc(exped, 1)
                if is_tile(i, 1):
                    keep_v(i + 1, 1 - s)
                keep_probs(i, 0)
                if is_tile(i, 1):
                    keep_k(i + 1)
                if is_tile(i, 2):
                    keep_hT(i + 2)
                keep_probs(i, 1)
                if is_tile(i, 1):
                    keep_q(i + 1)
                if is_tile(i, -1):
                    keep_o(i - 1)

            act.wait_ge(first_set, 4)
            keep_hT(0)
            square("k", 0)
            square("q", 0)
            keep_v(0, 0)
            keep_k(0)
            keep_q(0)
            keep_hT(1)
            tiles(act, tile)
            keep_o(NT - 1)

        @block.vector
        def _(dve):
            def rotate(x, n):
                which, ps = "qk".index(x), (ps_k if x == "k" else ps_q)
                dve.wait_ge(squared[x], n + 1)
                if x == "q" and is_tile(n, -1):
                    dve.wait_ge(turned_T["q"], n)
                nc.vector.tensor_tensor(straight[x][:, :, :], ps[:, :, :],
                                        cos[:, bass.ds(n, 1), which, :].broadcast_to([P, FH, FD]),
                                        ALU.mult).then_inc(rotated[x], 1)
                for half in range(2):
                    d = slice(half * hf, (half + 1) * hf)
                    partner = slice((1 - half) * hf, (2 - half) * hf)
                    nc.vector.tensor_tensor(turned[x][:, :, d], ps[:, :, partner],
                                            sin[:, bass.ds(n, 1), which, d].broadcast_to([P, FH, hf]),
                                            ALU.mult).then_inc(rotated[x], 1)

            def norm(x, n):
                nc.vector.tensor_reduce(norms[x][:, :], squares[x][:, :, :], AX.X, ALU.add).then_inc(summed[x], 1)
                dve.wait_ge(summed[x], n + 1)
                nc.vector.tensor_scalar(norms[x][:, :], norms[x][:, :], TINY, None,
                                        ALU.max).then_inc(norms_ready[x], 1)

            def scale_k(n):
                dve.wait_ge(inverted["k"], n + 1)
                dve.wait_ge(added["k"], n + 1)
                if is_tile(n, -1):
                    dve.wait_ge(turned_T["k"], n)
                nc.vector.tensor_tensor(k_normed[:, :, :], straight["k"][:, :, :],
                                        inv_norm["k"][:, :].unsqueeze(2).broadcast_to([P, FH, FD]),
                                        ALU.mult).then_inc(k_scaled, 1)

            def find_max(i, half):
                four = slice(4 * half, 4 * half + 4)
                dve.wait_ge(scored, 2 * i + half + 1)
                nc.vector.tensor_reduce(neg_top[:, four], ps_s[:, half, :, :], AX.X, ALU.max,
                                        negate=True).then_inc(topped, 1)
                dve.wait_ge(inverted["q"], i + 1)
                dve.wait_ge(topped, 2 * i + half + 1)
                nc.vector.tensor_tensor(neg_max[:, four], neg_top[:, four],
                                        inv_norm["q"][:, :].rearrange("p (j b) -> p b j", b=2)[:, half, :],
                                        ALU.mult).then_inc(negated, 1)

            def add(n):
                dve.wait_ge(projected, n + 1)
                nc.vector.tensor_tensor(mem.h[:, bass.ds(n, 1), 0:half_d].squeeze(1), ps_v[:, 0:half_d],
                                        src[:, bass.ds(n, 1), 0:half_d].squeeze(1), ALU.add).then_inc(result, 1)
                if src is dst:
                    dve.wait_ge(result, 2 * n + 1)
                nc.vector.tensor_tensor(at(dst, n), ps_v[:, 0:D], at(src, n), ALU.add).then_inc(result, 1)

            def divide(n):
                dve.wait_ge(sum_inverted, n + 1)
                dve.wait_ge(weighed, n + 1)
                if is_tile(n, -1):
                    dve.wait_ge(o_turned, n)
                nc.vector.tensor_tensor(
                    o[:, :].rearrange("p (j b d) -> p j b d", b=2, d=FD),
                    ps_o[:, :].rearrange("p (j b d) -> p j b d", b=2, d=FD),
                    inv_sum[:, :].rearrange("p (b j) -> p j b", b=2).unsqueeze(3).broadcast_to([P, 4, 2, FD]),
                    ALU.mult).then_inc(divided, 1)

            def tile(i, s):
                if is_tile(i, 1):
                    rotate("k", i + 1)
                find_max(i, 0)
                if is_tile(i, 1):
                    norm("k", i + 1)
                find_max(i, 1)
                if is_tile(i, 1):
                    nc.vector.tensor_copy(kT[:, :, 0:WIN], kT[:, :, P:P + WIN]).then_inc(k_kept, 1)
                if is_tile(i, -2):
                    add(i - 2)
                if is_tile(i, 1):
                    rotate("q", i + 1)
                    scale_k(i + 1)
                if is_tile(i, -1):
                    divide(i - 1)
                if is_tile(i, 1):
                    norm("q", i + 1)
                dve.wait_ge(exped, i * FH + FH)
                if is_tile(i, -1):
                    dve.wait_ge(divided, i)
                nc.vector.reciprocal(inv_sum[:, :], sums[:, :]).then_inc(sum_inverted, 1)

            nc.vector.tensor_scalar(mem.gains[:, layer, 0, :], mem.gains[:, layer, 0, :], QK_SCALE, None,
                                    ALU.mult).then_inc(scaled, 1)
            dve.wait_ge(scaled, 1)

            def scale_cos(t, n):
                nc.vector.tensor_tensor(cos[:, t, :, :], mem.rot_cos[:, t, :, :],
                                        mem.gains[:, layer, :, :].unsqueeze(1).broadcast_to([P, n, 2, FD]),
                                        ALU.mult).then_inc(scaled, 1)

            def scale_sin(t, n):
                for half in range(2):
                    d = slice(half * hf, (half + 1) * hf)
                    partner = slice((1 - half) * hf, (2 - half) * hf)
                    nc.vector.tensor_tensor(sin[:, t, :, d], mem.rot_sin[:, t, :, d],
                                            mem.gains[:, layer, :, partner].unsqueeze(1).broadcast_to([P, n, 2, hf]),
                                            ALU.mult).then_inc(scaled, 1)

            scale_cos(slice(0, 1), 1)
            scale_sin(slice(0, 1), 1)
            dve.wait_ge(scaled, 4)
            rotate("k", 0)
            norm("k", 0)
            rotate("q", 0)
            scale_cos(slice(1, NT), NT - 1)
            scale_k(0)
            norm("q", 0)
            scale_sin(slice(1, NT), NT - 1)
            dve.wait_ge(scaled, 7)
            tiles(dve, tile)
            add(NT - 2)
            divide(NT - 1)
            add(NT - 1)


def feed_forward(nc, mem, name, layer, dst):
    NH = len(HCH)
    with stage(nc, name) as (ctx, sem):
        def sb(n, shape, dt=F32):
            return ctx.enter_context(nc.sbuf_tensor(f"{name}_{n}", shape, dt))


        hT = sb("hT", [P, 2, CH])
        gate = sb("gate", [P, NH, CH])
        hidden = sb("hidden", [P, 2, NH, CH])
        ps = [ctx.enter_context(nc.psum_tensor(f"{name}_ps{b}", [P, CH], F32)) for b in range(8)]
        ps_a, ps_g, ps_t, ps_y = ps[0:NH], ps[NH:2 * NH], ps[6], ps[7]
        turned = sem("turned")
        hT_ready = sem("hT_ready")
        biased = sem("biased")
        widened = sem("widened")
        gated = sem("gated")
        hidden_ready = sem("hidden_ready")
        narrowed = sem("narrowed")
        result = sem("result")
        norm = Norm(nc, mem, sem, mem.h, mem.h)
        block = ctx.enter_context(nc.Block())

        @block.gpsimd
        def _(pool):
            norm.gpsimd(pool)
            for c in range(NC):
                t = slice(c * TPC, (c + 1) * TPC)
                nc.gpsimd.tensor_tensor(dst[:, t, :], dst[:, t, :],
                                        mem.b2[:, layer, :].unsqueeze(1).broadcast_to([P, TPC, D]),
                                        ALU.add).then_inc(biased, 1)

        @block.tensor
        def _(pe):
            def turn(c):
                pe.wait_ge(norm.scaled, (c + 1) * TPC)
                if c:
                    pe.wait_ge(hT_ready, c)
                for i in range(TPC):
                    mm = nc.tensor.transpose(ps_t[:, i * P:(i + 1) * P], mem.h[:, c * TPC + i, :], mem.ident[:, :])
                mm.then_inc(turned, 1)

            def narrow(c):
                pe.wait_ge(hidden_ready, NH * (c + 1))
                if c:
                    pe.wait_ge(result, c)
                for i in range(TPC):
                    for m, (_, n) in enumerate(HCH):
                        mm = nc.tensor.matmul(ps_y[:, i * P:(i + 1) * P], hidden[0:n, c % 2, m, i * P:(i + 1) * P],
                                              mem.w2[0:n, layer, m, :], start=(i == 0 and m == 0),
                                              stop=(m == NH - 1), skip_group_check=True)
                mm.then_inc(narrowed, 1)

            turn(0)
            for c in range(NC):
                pe.wait_ge(hT_ready, c + 1)
                for m, (h0, n) in enumerate(HCH):
                    if c:
                        pe.wait_ge(hidden_ready, NH * (c - 1) + m + 1)
                    for half, bank in ((1, ps_g[m]), (0, ps_a[m])):
                        mm = nc.tensor.matmul(bank[0:n, :], mem.w1[:, layer, half * HID + h0:half * HID + h0 + n],
                                              hT[:, c % 2, :], start=True, stop=True)
                    mm.then_inc(widened, 1)
                if c + 1 < NC:
                    turn(c + 1)
                if c:
                    narrow(c - 1)
            narrow(NC - 1)

        @block.scalar
        def _(act):
            def turn(c):
                act.wait_ge(turned, c + 1)
                if c >= 2:
                    act.wait_ge(widened, NH * (c - 1))
                nc.scalar.activation(hT[:, c % 2, :], ps_t[:, :], ACT.Identity, bias=mem.ln[:, layer, 1:2],
                                     scale=mem.ln[:, layer, 0:1]).then_inc(hT_ready, 1)
            turn(0)
            for c in range(NC):
                for m, (h0, n) in enumerate(HCH):
                    act.wait_ge(widened, NH * c + m + 1)
                    if c:
                        act.wait_ge(hidden_ready, NH * (c - 1) + m + 1)
                    nc.scalar.activation(gate[0:n, m, :], ps_g[m][0:n, :], ACT.Gelu,
                                         bias=mem.b1[0:n, layer, 1, m:m + 1]).then_inc(gated, 1)
                if c + 1 < NC:
                    turn(c + 1)

        @block.vector
        def _(dve):
            norm.vector(dve)

            def add(c):
                t = slice(c * TPC, (c + 1) * TPC)
                dve.wait_ge(biased, c + 1)
                dve.wait_ge(narrowed, c + 1)
                nc.vector.tensor_tensor(dst[:, t, :], dst[:, t, :], ps_y[:, :].rearrange("p (i d) -> p i d", d=D),
                                        ALU.add).then_inc(result, 1)
            for c in range(NC):
                for m, (h0, n) in enumerate(HCH):
                    dve.wait_ge(gated, NH * c + m + 1)
                    if c >= 2:
                        dve.wait_ge(narrowed, c - 1)
                    nc.vector.scalar_tensor_tensor(out=hidden[0:n, c % 2, m, :], in0=ps_a[m][0:n, :],
                                                   scalar=mem.b1[0:n, layer, 0, m:m + 1], in1=gate[0:n, m, :],
                                                   op0=ALU.add, op1=ALU.mult).then_inc(hidden_ready, 1)
                if c:
                    add(c - 1)
            add(NC - 1)


def linear_out(nc, mem, name, src, w, dst, plus=None, bias=None, loads=None):
    with stage(nc, name) as (ctx, sem):

        wide = ctx.enter_context(nc.sbuf_tensor(f"{name}_wide", [P, T], F32))
        ps = [ctx.enter_context(nc.psum_tensor(f"{name}_ps{b}", [P, CH], F32)) for b in range(8)]
        turned = sem("turned")
        wide_ready = sem("wide_ready")
        product = sem("product")
        biased = sem("biased")
        result = sem("result")
        block = ctx.enter_context(nc.Block())

        @block.sync
        def _(sp):
            if loads:
                sp.wait_ge(*loads)

        @block.gpsimd
        def _(pool):
            if plus is not None:
                for c in range(NC):
                    t = slice(c * TPC, (c + 1) * TPC)
                    nc.gpsimd.tensor_tensor(dst[:, t, :], plus[:, t, :],
                                            bias[:, :].unsqueeze(1).broadcast_to([P, TPC, D]),
                                            ALU.add).then_inc(biased, 1)

        @block.tensor
        def _(pe):
            for c in range(NC):
                for i in range(TPC):
                    mm = nc.tensor.transpose(ps[c][:, i * P:(i + 1) * P], src[:, c * TPC + i, :], mem.ident[:, :])
                mm.then_inc(turned, 1)
            for c in range(NC):
                pe.wait_ge(wide_ready, c + 1)
                for i in range(TPC):
                    t = c * TPC + i
                    mm = nc.tensor.matmul(ps[4 + c][:, i * P:(i + 1) * P], wide[:, t * P:(t + 1) * P], w[:, :],
                                          start=(i == 0), stop=(i == TPC - 1), skip_group_check=True)
                mm.then_inc(product, 1)

        @block.scalar
        def _(act):
            for c in range(NC):
                act.wait_ge(turned, c + 1)
                nc.scalar.activation(wide[:, c * CH:(c + 1) * CH], ps[c][:, :], ACT.Copy).then_inc(wide_ready, 1)

        @block.vector
        def _(dve):
            for c in range(NC):
                t = slice(c * TPC, (c + 1) * TPC)
                y = ps[4 + c][:, :].rearrange("p (i d) -> p i d", d=D)
                dve.wait_ge(product, c + 1)
                if plus is not None:
                    dve.wait_ge(biased, c + 1)
                    nc.vector.tensor_tensor(dst[:, t, :], dst[:, t, :], y, ALU.add).then_inc(result, 1)
                else:
                    nc.vector.tensor_copy(dst[:, t, :], y).then_inc(result, 1)


def gate_residual(nc, mem, name, f, s, x):
    with stage(nc, name) as (ctx, sem):
        gated = sem("gated")
        product = sem("product")
        result = sem("result")
        block = ctx.enter_context(nc.Block())

        @block.scalar
        def _(act):
            for c in range(NC):
                t = slice(c * TPC, (c + 1) * TPC)
                nc.scalar.activation(f[:, t, :], f[:, t, :], ACT.Silu).then_inc(gated, 1)

        @block.vector
        def _(dve):
            for c in range(NC):
                t = slice(c * TPC, (c + 1) * TPC)
                dve.wait_ge(gated, c + 1)
                nc.vector.tensor_tensor(s[:, t, :], s[:, t, :], f[:, t, :], ALU.mult).then_inc(product, 1)
                dve.wait_ge(product, c + 1)
                nc.vector.tensor_tensor(x[:, t, :], x[:, t, :], s[:, t, :], ALU.add).then_inc(result, 1)


E = 8
TOP = 2
EH = 4 * D // E
PAIRS = E // 2
GROUPS = PAIRS + 1


def expert_buffers(a, mem, u):
    mem.w_route = u("w_route", [P, E])
    mem.route_bias = u("route_bias", [P, E])
    mem.w_in = u("w_in", [P, GROUPS, 2, EH])
    mem.b_in = u("b_in", [P, GROUPS])
    mem.w_out = u("w_out", [P, GROUPS, D])
    mem.b_out = u("b_out", [1 + PARTS * E, D])
    mem.lower = u("lower", [P, E, E])
    mem.spread = u("spread", [1 + PARTS * E, PAIRS, P], BF16)
    pairs = a["rW1"].rearrange("(g o) d h -> d g o h", o=2)
    return [
        (mem.w_route[:, :], a["w_route"]),
        (mem.route_bias[:, :], a["expert_bias"].partition_broadcast(P)),
        (mem.lower[:, :, :], a["lower"].partition_broadcast(P)),
        (mem.spread[:, :, :], a["spread"].bitcast(BF16)),
        (mem.w_in[:, PAIRS, 0, :], a["sW1"]),
        (mem.b_in[0:EH, PAIRS:GROUPS], a["sb1"].unsqueeze(1)),
        (mem.b_in[:, 0:PAIRS], a["rb1"]),
        (mem.w_out[:, 0:PAIRS, :], a["rW2"]),
        (mem.w_out[0:EH, PAIRS, :], a["sW2"]),
        (mem.b_out[0:1, :], a["sb2"].unsqueeze(0)),
    ] + [(mem.b_out[1 + n * E:1 + (n + 1) * E, :], a["rb2"]) for n in range(PARTS)
    ] + [(mem.w_in[:, g, :, :], pairs[:, g, :, :]) for g in range(PAIRS)]


def experts(nc, mem, name, wide, s, x, out):
    with stage(nc, name) as (ctx, sem):
        def sb(n, shape, dt=F32):
            return ctx.enter_context(nc.sbuf_tensor(f"{name}_{n}", shape, dt))

        def psum(n, shape):
            return ctx.enter_context(nc.psum_tensor(f"{name}_{n}", shape, F32))


        w_route, route_bias, w_in, b_in = mem.w_route, mem.route_bias, mem.w_in, mem.b_in
        w_out, b_out, lower, spread = mem.w_out, mem.b_out, mem.lower, mem.spread
        logits = sb("logits", [P, NT, E])
        size = sb("size", [P, NT, E])
        one_plus = sb("one_plus", [P, NT, E])
        over = sb("over", [P, NT, E])
        exact = sb("exact", [P, NT, E])
        log_term = sb("log_term", [P, NT, E])
        half = sb("half", [P, TOP, NT])
        best = sb("best", [P, TOP, NT])
        others = sb("others", [P, NT, E])
        is_best = sb("is_best", [P, TOP, NT, E])
        above = sb("above", [P, NT, E, E])
        level = sb("level", [P, NT, E, E])
        rank = sb("rank", [P, NT, E])
        weight = sb("weight", [P, NT, E])
        rest = sb("rest", [P, NT, E])
        parts = sb("parts", [P, NT, 1 + PARTS * E], BF16)
        weightT = sb("weightT", [1 + PARTS * E, T])
        weightT_bf = sb("weightT_bf", [1 + PARTS * E, T], BF16)
        hidden = sb("hidden", [P, NC, GROUPS, CH])
        gate = sb("gate", [P, 2, CH])

        ps_r = psum("ps_r", [P, CH])
        ps_t = psum("ps_t", [1 + PARTS * E, CH])
        ps_h = [psum(f"ps_h{b}", [P, CH]) for b in range(2)]
        ps_w = [psum(f"ps_w{b}", [P, CH]) for b in range(2)]
        ps_y = [psum(f"ps_y{b}", [P, CH]) for b in range(2)]

        set_up = sem("set_up")
        routed = sem("routed")
        step = sem("step")
        exped = sem("exped")
        found = sem("found")
        rooted = sem("rooted")
        weighed = sem("weighed")
        w_turned = sem("w_turned")
        weightT_ready = sem("weightT_ready")
        hid_made = sem("hid_made")
        activated = sem("activated")
        spread_made = sem("spread_made")
        hid_weighed = sem("hid_weighed")
        mixed = sem("mixed")
        gated = sem("gated")
        multiplied = sem("multiplied")
        result = sem("result")
        stored = sem("stored")
        block = ctx.enter_context(nc.Block())

        @block.sync
        def _(sp):
            for c in range(NC):
                sp.wait_ge(result, c + 1)
                sp.dma_start(tiles_of(out)[:, c * TPC:(c + 1) * TPC, :],
                             x[:, c * TPC:(c + 1) * TPC, :]).then_inc(stored, 16)
            sp.wait_ge(stored, 16 * NC)

        @block.gpsimd
        def _(pool):
            nc.gpsimd.memset(half[:], 0.5).then_inc(set_up, 1)
            nc.gpsimd.memset(parts[:, :, 0:1], 1.0).then_inc(set_up, 1)
            pool.wait_ge(set_up, 2)
            pool.wait_ge(found, 1)
            nc.gpsimd.tensor_tensor(best[:, :, :], best[:, :, :], half[:, :, :], ALU.pow).then_inc(rooted, 1)

        @block.tensor
        def _(pe):
            for i in range(NT):
                mm = nc.tensor.matmul(ps_r[:, i * E:(i + 1) * E], wide[:, i * P:(i + 1) * P], w_route[:, :],
                                      start=(i == 0), stop=(i == NT - 1), skip_group_check=True)
            mm.then_inc(routed, 1)
            for c in range(NC):
                for g in range(GROUPS):
                    k = P if g < PAIRS else EH
                    n = c * GROUPS + g
                    if n >= 2:
                        pe.wait_ge(activated, n - 1)
                    nc.tensor.matmul(ps_h[n % 2][0:k, :],
                                     w_in[:, g, :, :].rearrange("p o h -> p (o h)")[:, 0:k],
                                     wide[:, c * CH:(c + 1) * CH], start=True, stop=True).then_inc(hid_made, 1)
            pe.wait_ge(weighed, 1)
            pe.wait_ge(set_up, 2)
            for c in range(NC):
                if c:
                    pe.wait_ge(weightT_ready, 2 * c)
                for i in range(TPC):
                    mm = nc.tensor.matmul(ps_t[:, i * P:(i + 1) * P], parts[:, c * TPC + i, :], mem.ident_bf[:, :],
                                          start=(i == 0), stop=(i == TPC - 1), skip_group_check=True)
                mm.then_inc(w_turned, 1)

            def mix(c):
                pe.wait_ge(hid_weighed, PAIRS * (c + 1))
                if c >= 2:
                    pe.wait_ge(gated, c - 1)
                for i in range(TPC):
                    col = slice(i * P, (i + 1) * P)
                    for g in range(GROUPS):
                        k = P if g < PAIRS else EH
                        nc.tensor.matmul(ps_y[c % 2][:, col], hidden[0:k, c, g, col], w_out[0:k, g, :],
                                         start=(i == 0 and g == 0), stop=False, skip_group_check=True)
                    mm = nc.tensor.matmul(ps_y[c % 2][:, col], weightT[:, c * CH + i * P:c * CH + (i + 1) * P],
                                          b_out[:, :], start=False, stop=True, skip_group_check=True)
                mm.then_inc(mixed, 1)

            for c in range(NC):
                pe.wait_ge(weightT_ready, 2 * (c + 1))
                for g in range(PAIRS):
                    p = c * PAIRS + g
                    if p >= 2:
                        pe.wait_ge(hid_weighed, p - 1)
                    nc.tensor.matmul(ps_w[p % 2][:, :], spread[:, g, :], weightT_bf[:, c * CH:(c + 1) * CH],
                                     start=True, stop=True).then_inc(spread_made, 1)
                if c:
                    mix(c - 1)
            mix(NC - 1)

        @block.scalar
        def _(act):
            act.wait_ge(step, 1)
            nc.scalar.activation(size[:, :, :], logits[:, :, :], ACT.Abs).then_inc(exped, 1)
            act.wait_ge(exped, 1)
            nc.scalar.activation(size[:, :, :], size[:, :, :], ACT.Exp, scale=-1.0).then_inc(exped, 1)
            act.wait_ge(step, 2)
            nc.scalar.activation(log_term[:, :, :], one_plus[:, :, :], ACT.Ln).then_inc(exped, 1)
            for c in range(NC):
                for g in range(GROUPS):
                    k = P if g < PAIRS else EH
                    n = c * GROUPS + g
                    act.wait_ge(hid_made, n + 1)
                    nc.scalar.activation(hidden[0:k, c, g, :], ps_h[n % 2][0:k, :], ACT.Silu,
                                         bias=b_in[0:k, g:g + 1]).then_inc(activated, 1)
            for c in range(NC):
                act.wait_ge(w_turned, c + 1)
                for dst in (weightT_bf, weightT):
                    nc.scalar.activation(dst[:, c * CH:(c + 1) * CH], ps_t[:, :], ACT.Copy).then_inc(weightT_ready, 1)
            for c in range(NC):
                act.wait_ge(mixed, c + 1)
                if c >= 2:
                    act.wait_ge(multiplied, c - 1)
                nc.scalar.activation(gate[:, c % 2, :], ps_y[c % 2][:, :], ACT.Silu).then_inc(gated, 1)

        @block.vector
        def _(dve):
            done = [0]

            def link(ins):
                done[0] += 1
                ins.then_inc(step, 1)
                dve.wait_ge(step, done[0])

            dve.wait_ge(routed, 1)
            link(nc.vector.tensor_tensor(logits[:, :, :], ps_r[:, 0:NT * E].rearrange("p (i e) -> p i e", e=E),
                                         route_bias[:, :].unsqueeze(1).broadcast_to([P, NT, E]), ALU.add))
            dve.wait_ge(exped, 2)
            link(nc.vector.tensor_scalar(one_plus[:, :, :], size[:, :, :], 1.0, None, ALU.add))
            link(nc.vector.tensor_scalar(over[:, :, :], one_plus[:, :, :], 1.0, None, ALU.subtract))
            link(nc.vector.tensor_scalar(exact[:, :, :], over[:, :, :], 0.0, None, ALU.is_equal))
            link(nc.vector.tensor_tensor(over[:, :, :], over[:, :, :], exact[:, :, :], ALU.add))
            link(nc.vector.reciprocal(over[:, :, :], over[:, :, :]))
            dve.wait_ge(exped, 3)
            link(nc.vector.tensor_tensor(over[:, :, :], over[:, :, :], log_term[:, :, :], ALU.mult))
            link(nc.vector.tensor_tensor(over[:, :, :], over[:, :, :], exact[:, :, :], ALU.add))
            link(nc.vector.tensor_tensor(over[:, :, :], over[:, :, :], size[:, :, :], ALU.mult))
            link(nc.vector.scalar_tensor_tensor(out=log_term[:, :, :], in0=logits[:, :, :], scalar=0.0,
                                                in1=over[:, :, :], op0=ALU.max, op1=ALU.add))
            value = log_term
            mine = value[:, :, :].unsqueeze(3).broadcast_to([P, NT, E, E])
            other = value[:, :, :].unsqueeze(2).broadcast_to([P, NT, E, E])
            link(nc.vector.tensor_tensor(above[:, :, :, :], other, mine, ALU.is_gt))
            link(nc.vector.tensor_tensor(level[:, :, :, :], other, mine, ALU.is_equal))
            link(nc.vector.tensor_tensor(level[:, :, :, :], level[:, :, :, :],
                                         lower[:, :, :].unsqueeze(1).broadcast_to([P, NT, E, E]), ALU.mult))
            link(nc.vector.tensor_tensor(above[:, :, :, :], above[:, :, :, :], level[:, :, :, :], ALU.add))
            link(nc.vector.tensor_reduce(rank[:, :, :], above[:, :, :, :], AX.X, ALU.add))
            for n in range(TOP):
                link(nc.vector.tensor_scalar(is_best[:, n, :, :], rank[:, :, :], float(n), None, ALU.is_equal))
                link(nc.vector.tensor_tensor(others[:, :, :], is_best[:, n, :, :], value[:, :, :], ALU.mult))
                last = nc.vector.tensor_reduce(best[:, n, :], others[:, :, :], AX.X, ALU.add)
                if n < TOP - 1:
                    link(last)
            last.then_inc(found, 1)
            dve.wait_ge(rooted, 1)
            for n in range(TOP):
                link(nc.vector.tensor_tensor(is_best[:, n, :, :], is_best[:, n, :, :],
                                             best[:, n, :].unsqueeze(2).broadcast_to([P, NT, E]), ALU.mult))
            link(nc.vector.tensor_tensor(weight[:, :, :], is_best[:, 0, :, :], is_best[:, 1, :, :], ALU.add))
            part = [parts[:, :, 1 + n * E:1 + (n + 1) * E] for n in range(PARTS)]
            link(nc.vector.tensor_copy(part[0], weight[:, :, :]))
            link(nc.vector.tensor_tensor(rest[:, :, :], weight[:, :, :], part[0], ALU.subtract))
            link(nc.vector.tensor_copy(part[1], rest[:, :, :]))
            nc.vector.tensor_tensor(part[2], rest[:, :, :], part[1], ALU.subtract).then_inc(weighed, 1)

            def finish(c):
                t = slice(c * TPC, (c + 1) * TPC)
                dve.wait_ge(gated, c + 1)
                nc.vector.tensor_tensor(s[:, t, :], s[:, t, :], gate[:, c % 2, :].rearrange("p (i d) -> p i d", d=D),
                                        ALU.mult).then_inc(multiplied, 1)
                dve.wait_ge(multiplied, c + 1)
                nc.vector.tensor_tensor(x[:, t, :], x[:, t, :], s[:, t, :], ALU.add).then_inc(result, 1)

            for c in range(NC):
                for g in range(PAIRS):
                    n, p = c * GROUPS + g, c * PAIRS + g
                    dve.wait_ge(activated, n + 1)
                    dve.wait_ge(spread_made, p + 1)
                    nc.vector.tensor_tensor(hidden[:, c, g, :], hidden[:, c, g, :], ps_w[p % 2][:, :],
                                            ALU.mult).then_inc(hid_weighed, 1)
                if c >= 2:
                    finish(c - 2)
            finish(NC - 2)
            finish(NC - 1)


def constants():
    later = np.arange(P)[None, :] > np.arange(P)[:, None]
    spread = np.zeros((1 + PARTS * E, PAIRS, 2, EH), np.uint16)
    for n in range(PARTS):
        for e in range(E):
            spread[1 + n * E + e, e // 2, e % 2, :] = 0x3F80
    return {
        "ident": np.eye(P, dtype=np.float32),
        "masks": (np.stack([np.eye(P), np.where(later, NEG, 0.0), np.where(later.T, NEG, 0.0)])
                  .astype(np.float32).view(np.uint32) >> 16).astype(np.uint16),
        "rotary": rotary_tables(),
        "window_masks": window_masks(),
        "lower": np.tril(np.ones((E, E), np.float32), -1),
        "spread": spread.reshape(1 + PARTS * E, PAIRS, P),
        "fill": np.stack([np.full((MROW - ROWS, T), bits, np.uint16) for bits in (0, 0x3F80)]),
    }


def layout(inputs):
    g = lambda n: np.asarray(inputs[n])
    arrays = {
        "x": g("L0_attn_z").reshape(T, D),
        "ln_scale0": g("L0_attn_ln_scale"),
        "ln_bias0": g("L0_attn_ln_bias"),
        "w_qkv0": g("L0_attn_w_qkv").reshape(D, D, 3).transpose(2, 0, 1),
        "w_proj0": g("L0_attn_w_proj"),
        "b_proj0": g("L0_attn_b_proj"),
        "w_qkv1": g("L1_attn_w_qkv").reshape(3, D, D).transpose(0, 2, 1),
        "w_out1": g("L1_attn_w_out").T,
        "w_route": g("L1_ffn_routing_W").T,
        "expert_bias": g("L1_ffn_expert_bias"),
        "sW1": g("L1_ffn_sW1"), "sb1": g("L1_ffn_sb1"), "sW2": g("L1_ffn_sW2"), "sb2": g("L1_ffn_sb2"),
        "rW1": g("L1_ffn_rW1"),
        "rb1": g("L1_ffn_rb1").reshape(PAIRS, P).T,
        "rW2": g("L1_ffn_rW2").reshape(PAIRS, P, D).transpose(1, 0, 2),
        "rb2": g("L1_ffn_rb2"),
    }
    for n in ("wqkv", "q_scale", "k_scale", "w1", "b2"):
        arrays[n] = g("L0_ffn_" + n)
    fill = [(0, len(HCH) * P - HID)]
    arrays["wo"] = g("L0_ffn_wo").reshape(DEPTH, INNER // P, P, D).transpose(2, 0, 1, 3)
    arrays["w2"] = np.pad(g("L0_ffn_w2"), [(0, 0)] + fill + [(0, 0)]).reshape(DEPTH, -1, P, D).transpose(2, 0, 1, 3)
    arrays["b1"] = np.pad(g("L0_ffn_b1").reshape(DEPTH, 2, HID), [(0, 0)] * 2 + fill).reshape(
        DEPTH, 2, -1, P).transpose(3, 0, 1, 2)
    arrays["ln"] = np.stack([g("L0_ffn_ln_g"), g("L0_ffn_ln_b")], -1).transpose(1, 0, 2)
    arrays.update(constants())
    return {k: np.ascontiguousarray(v) for k, v in arrays.items()}


def load(nc, name, *pairs):
    with stage(nc, name) as (ctx, sem):
        loaded = sem("loaded")
        block = ctx.enter_context(nc.Block())

        @block.sync
        def _(sp):
            for dst, src in pairs:
                sp.dma_start(dst, src).then_inc(loaded, 16)
            sp.wait_ge(loaded, 16 * len(pairs))


def layer_buffers(a, mem, u):
    mem.h = u("h", [P, NT, D])
    mem.rot_cos = u("rot_cos", [P, NT, 2, FD])
    mem.rot_sin = u("rot_sin", [P, NT, 2, FD])
    mem.window_masks = u("window_masks_sb", [P, 2, 2 * WIN], BF16)
    mem.wqkv = u("wqkv", [P, DEPTH, 3 * INNER])
    mem.gains = u("gains", [P, DEPTH, 2, FD])
    mem.wo = u("wo", [P, DEPTH, INNER // P, D])
    mem.w1 = u("w1", [P, DEPTH, 2 * HID])
    mem.w2 = u("w2", [P, DEPTH, len(HCH), D])
    mem.b1 = u("b1", [P, DEPTH, 2, len(HCH)])
    mem.b2 = u("b2", [P, DEPTH, D])
    mem.ln = u("ln", [P, DEPTH, 2])
    return [
        (mem.gains[:, :, 0, :], a["q_scale"].partition_broadcast(P)),
        (mem.gains[:, :, 1, :], a["k_scale"].partition_broadcast(P)),
        (mem.window_masks[:, :, :], a["window_masks"].bitcast(BF16).rearrange("m p q -> p m q")),
        (mem.wqkv[:, :, :], a["wqkv"].rearrange("l p n -> p l n")),
        (mem.rot_cos[:, :, :, :], a["rotary"][0].rearrange("(i p) n d -> p i n d", p=P)),
        (mem.rot_sin[:, :, :, :], a["rotary"][1].rearrange("(i p) n d -> p i n d", p=P)),
        (mem.wo[:, :, :, :], a["wo"]),
        (mem.ln[:, :, :], a["ln"]),
        (mem.w1[:, :, :], a["w1"].rearrange("l p n -> p l n")),
        (mem.b1[:, :, :, :], a["b1"]),
        (mem.w2[:, :, :, :], a["w2"]),
        (mem.b2[:, :, :], a["b2"].partition_broadcast(P)),
    ]


def attend(nc, mem, name, causal):
    with ExitStack() as s1:
        mem.QS = s1.enter_context(nc.sbuf_tensor(f"{name}_QS", [P, H * T], BF16))
        mem.KS = s1.enter_context(nc.sbuf_tensor(f"{name}_KS", [P, H * T], BF16))
        attention(nc, mem, name, causal)


def build(nc, a, out):
    with ExitStack() as ctx:
        def buffers(stack):
            return lambda n, shape, dt=F32: stack.enter_context(nc.sbuf_tensor(n, shape, dt))

        mem = Memory()
        sb = buffers(ctx)
        mem.q_parts_dram = nc.dram_tensor("q_parts", (PARTS, D, T), BF16).ap()
        mem.k_parts_dram = nc.dram_tensor("k_parts", (PARTS, D, T), BF16).ap()
        xn_dram = nc.dram_tensor("xn_kept", (P, NT, D), F32).ap()
        wide_dram = nc.dram_tensor("wide_kept", (P, T), F32).ap()
        mem.fill = a["fill"].bitcast(BF16)
        x = sb("x", [P, NT, D])
        s = sb("s", [P, NT, D])
        mem.ident = sb("identity", [P, P])
        mem.ident_bf = sb("identity_bf", [P, P], BF16)
        mem.hide_later_keys = sb("hide_later_keys", [P, P], BF16)
        mem.hide_earlier_queries = sb("hide_earlier_queries", [P, P], BF16)
        mem.sums = sb("sums", [P, NT, 6])
        mem.moments = sb("moments", [P, NT, 2])
        mem.rstd = sb("rstd", [P, NT])
        mem.minus_half = sb("minus_half", [P, NT])

        with ExitStack() as s0:
            u = buffers(s0)
            xn, zn, wide = u("xn", [P, NT, D]), u("zn", [P, NT, D]), u("zn_wide", [P, T])
            w = [u(f"w0_{n}", [P, D]) for n in range(3)]
            ls = u("ls", [P, 2])
            load(nc, "x", (x[:, :, :], tiles_of(a["x"])), (mem.ident[:, :], a["ident"]),
                 (ls[:, 0:1], a["ln_scale0"].unsqueeze(1)), (ls[:, 1:2], a["ln_bias0"].unsqueeze(1)),
                 *[(w[n][:, :], a["w_qkv0"][n]) for n in range(3)],
                 *[(m[:, :], a["masks"][n].bitcast(BF16)) for n, m in enumerate(
                     (mem.ident_bf, mem.hide_later_keys, mem.hide_earlier_queries))])
            normalise(nc, mem, "ln_x0", x, xn)
            mem.v_tok = s
            project(nc, mem, "proj0", xn, zn, wide, *w, (xn_dram, xn), affine=(ls[:, 0:1], ls[:, 1:2]))
        w1 = [sb(f"w1_{n}", [P, D]) for n in range(3)]
        with ExitStack() as s0:
            u = buffers(s0)
            mem.heads_out = u("heads_out0", [P, H * CH])
            attend(nc, mem, "mix0", False)
            xn, o, f = u("xn_again", [P, NT, D]), u("xnb", [P, NT, D]), u("f", [P, NT, D])
            w_proj, b_proj = u("w_proj", [P, D]), u("b_proj", [P, D])
            later_loads = layer_buffers(a, mem, u) + [(w1[n][:, :], a["w_qkv1"][n]) for n in range(3)]
            later = nc.alloc_semaphore("layers_loaded")
            gather_heads(nc, mem, "gather0", s, [
                (xn[:, :, :], xn_dram), (w_proj[:, :], a["w_proj0"]),
                (b_proj[:, :], a["b_proj0"].partition_broadcast(P))], later_loads, later)
            linear_out(nc, mem, "out0", s, w_proj, o, xn, b_proj, (later, 16 * len(later_loads)))
            for layer in range(DEPTH):
                local_attention(nc, mem, f"local{layer}", layer, f if layer else xn, f)
                feed_forward(nc, mem, f"ff{layer}", layer, f)
            gate_residual(nc, mem, "gate0", f, o, x)

        with ExitStack() as s0:
            u = buffers(s0)
            xn, wide = u("xn1", [P, NT, D]), u("xn1_wide", [P, T])
            project(nc, mem, "proj1", x, xn, wide, *w1, (wide_dram, wide))
        with ExitStack() as s0:
            u = buffers(s0)
            mem.heads_out = u("heads_out1", [P, H * CH])
            attend(nc, mem, "mix1", True)
            w_out, wide = u("w_out1", [P, D]), u("wide_again", [P, T])
            gather_heads(nc, mem, "gather1", s, [(w_out[:, :], a["w_out1"]), (wide[:, :], wide_dram)]
                         + expert_buffers(a, mem, u))
            linear_out(nc, mem, "out1", s, w_out, s)
            experts(nc, mem, "moe", wide, s, x, out)


def kernel(**inputs):
    import concourse.bacc as bacc
    from concourse.bass_utils import run_bass_kernel_spmd

    arrays = {f"in_{n}": v for n, v in layout(inputs).items()}
    nc = bacc.Bacc("TRN2", target_bir_lowering=False, num_devices=1)
    a = {n[3:]: nc.dram_tensor(n, v.shape, mybir.dt.from_np(v.dtype), kind="ExternalInput").ap()
         for n, v in arrays.items()}
    out = nc.dram_tensor("out_0", (T, D), F32, kind="ExternalOutput").ap()
    build(nc, a, out)
    r = run_bass_kernel_spmd(nc, [arrays], core_ids=[0])
    return r.results[0]["out_0"].reshape(1, T, D)
```
